# Optimizing a Trainium2 kernel written in Bass

```python
import numpy as np
import jax
import jax.numpy as jnp

def _softmax(x, axis=-1):
    return jax.nn.softmax(x, axis=axis)

def _gelu(x):
    return jax.nn.gelu(x, approximate=True)

def _silu(x):
    return jax.nn.silu(x)

def _sigmoid(x):
    return jax.nn.sigmoid(x)

def _layernorm(x, axis=-1, eps=1e-05):
    m = jnp.mean(x, axis=axis, keepdims=True)
    v = jnp.var(x, axis=axis, keepdims=True)
    return (x - m) / jnp.sqrt(v + eps)

def _scatter_add(tgt, idx, src, axis=0):
    return tgt.at[idx].add(src)

def _segment_sum(src, seg, n):
    return jax.ops.segment_sum(src, seg, n)
kernel_name = 'mk_gnn_resnorm_d2_gnn_r32_748801'

def setup_inputs(seed: int=0):
    np.random.seed(seed)
    _w = jnp.asarray

    def _rec_inputs():
        import jax
        import jax.numpy as jnp
        _gk = jax.random.key(seed)
        x = -0.000202 + 1 * jax.random.normal(jax.random.fold_in(_gk, 1), (50000, 128), jnp.float32)
        src = jax.random.randint(jax.random.fold_in(_gk, 2), (25000,), 0, 50000, jnp.int32)
        dst = jax.random.randint(jax.random.fold_in(_gk, 3), (25000,), 0, 50000, jnp.int32)
        _o = jnp.argsort(dst, stable=True)
        src = src[_o]
        dst = dst[_o]
        edge_attr_128 = 2.93046e-05 + 1.00006 * jax.random.normal(jax.random.fold_in(_gk, 12), (25000, 128), jnp.float32)
        edge_attr_3 = -0.000451519 + 1.00018 * jax.random.normal(jax.random.fold_in(_gk, 13), (25000, 3), jnp.float32)
        edge_weight = jax.random.uniform(jax.random.fold_in(_gk, 15), (25000,), jnp.float32, 0.0, 0.999998)
        return (x, src, dst, edge_attr_128, edge_attr_3, edge_weight)
    x, src, dst, edge_attr_128, edge_attr_3, edge_weight = _rec_inputs()

    def _L0_gnn_setup():
        import jax, jax.numpy as jnp
        import numpy as np
        N = 50000
        E = 20000
        D = 128
        H = 2 * D
        BN_EPS = 1e-05

        def _batchnorm(x, gamma, beta):
            mean = jnp.mean(x, axis=0)
            var = jnp.var(x, axis=0)
            return (x - mean) * jax.lax.rsqrt(var + BN_EPS) * gamma + beta
        key = jax.random.key(seed)
        ks = jax.random.split(key, 8)
        h = jax.random.normal(ks[0], (N, D), dtype=jnp.float32)
        edge_index = jax.random.randint(ks[1], (2, E), 0, N, dtype=jnp.int64)
        edge_attr = jax.random.normal(ks[2], (E, D), dtype=jnp.float32)
        W1 = jax.random.normal(ks[3], (D, H), dtype=jnp.float32) * (1.0 / np.sqrt(D))
        g1 = jnp.ones((H,), dtype=jnp.float32)
        b1 = jnp.zeros((H,), dtype=jnp.float32)
        W2 = jax.random.normal(ks[4], (H, D), dtype=jnp.float32) * (1.0 / np.sqrt(H))
        g2 = jnp.ones((D,), dtype=jnp.float32)
        b2 = jnp.zeros((D,), dtype=jnp.float32)
        eps = jnp.zeros((), dtype=jnp.float32)
        return {'h': h, 'edge_index': edge_index, 'edge_attr': edge_attr, 'eps': eps, 'W1': W1, 'g1': g1, 'b1': b1, 'W2': W2, 'g2': g2, 'b2': b2}
    _L0_gnn_all = _L0_gnn_setup()
    _L0_gnn_in = {k: v for k, v in _L0_gnn_all.items() if k in ('eps', 'W1', 'g1', 'b1', 'W2', 'g2', 'b2')}
    del _L0_gnn_all

    def _L1_gnn_setup():
        import jax, jax.numpy as jnp
        import numpy as np
        N = 50000
        E = 25000
        MUL = 32
        NB = 8
        R_MAX = 1.0
        AVG = 16.0
        SQ3 = 3.0 ** 0.5

        def _radial_embedding(r):
            x = jnp.clip(r / R_MAX, 0.0, 1.0)
            centers = jnp.arange(NB, dtype=jnp.float32) / (NB - 1)
            sigma = 1.0 / (NB - 1)
            emb = jnp.exp(-0.5 * ((x[:, None] - centers[None, :]) / sigma) ** 2)
            emb = emb * NB ** 0.5 * (r <= R_MAX).astype(jnp.float32)[:, None]
            return emb
        key = jax.random.key(seed)
        k = jax.random.split(key, 12)
        inp = {'node_feats': jax.random.normal(k[0], (N, 4 * MUL), dtype=jnp.float32), 'edge_vec': jax.random.normal(k[1], (E, 3), dtype=jnp.float32), 'edge_length': jax.random.uniform(k[2], (E,), dtype=jnp.float32), 'senders': jax.random.randint(k[3], (E,), 0, N, dtype=jnp.int32), 'receivers': jax.random.randint(k[4], (E,), 0, N, dtype=jnp.int32), 'num_nodes': N, 'W_up0': jax.random.normal(k[5], (MUL, MUL), dtype=jnp.float32), 'W_up1': jax.random.normal(k[6], (MUL, MUL), dtype=jnp.float32), 'mlp_w0': jax.random.normal(k[7], (NB, 64), dtype=jnp.float32) / NB ** 0.5, 'mlp_b0': jnp.zeros((64,), dtype=jnp.float32), 'mlp_w1': jax.random.normal(k[8], (64, 64), dtype=jnp.float32) / 8.0, 'mlp_b1': jnp.zeros((64,), dtype=jnp.float32), 'mlp_w2': jax.random.normal(k[9], (64, 4 * MUL), dtype=jnp.float32) / 8.0, 'mlp_b2': jnp.zeros((4 * MUL,), dtype=jnp.float32), 'W_out0': jax.random.normal(k[10], (2 * MUL, MUL), dtype=jnp.float32), 'W_out1': jax.random.normal(k[11], (2 * MUL, MUL), dtype=jnp.float32)}
        return inp
    _L1_gnn_all = _L1_gnn_setup()
    _L1_gnn_in = {k: v for k, v in _L1_gnn_all.items() if k in ('W_up0', 'W_up1', 'mlp_w0', 'mlp_b0', 'mlp_w1', 'mlp_b1', 'mlp_w2', 'mlp_b2', 'W_out0', 'W_out1')}
    del _L1_gnn_all
    return {'x': x, 'src': src, 'dst': dst, 'edge_attr_128': edge_attr_128, 'edge_attr_3': edge_attr_3, 'edge_weight': edge_weight, 'L0_gnn_eps': _L0_gnn_in['eps'], 'L0_gnn_W1': _L0_gnn_in['W1'], 'L0_gnn_g1': _L0_gnn_in['g1'], 'L0_gnn_b1': _L0_gnn_in['b1'], 'L0_gnn_W2': _L0_gnn_in['W2'], 'L0_gnn_g2': _L0_gnn_in['g2'], 'L0_gnn_b2': _L0_gnn_in['b2'], 'L1_gnn_W_up0': _L1_gnn_in['W_up0'], 'L1_gnn_W_up1': _L1_gnn_in['W_up1'], 'L1_gnn_mlp_w0': _L1_gnn_in['mlp_w0'], 'L1_gnn_mlp_b0': _L1_gnn_in['mlp_b0'], 'L1_gnn_mlp_w1': _L1_gnn_in['mlp_w1'], 'L1_gnn_mlp_b1': _L1_gnn_in['mlp_b1'], 'L1_gnn_mlp_w2': _L1_gnn_in['mlp_w2'], 'L1_gnn_mlp_b2': _L1_gnn_in['mlp_b2'], 'L1_gnn_W_out0': _L1_gnn_in['W_out0'], 'L1_gnn_W_out1': _L1_gnn_in['W_out1']}

def reference(x, src, dst, edge_attr_128, edge_attr_3, edge_weight, L0_gnn_eps, L0_gnn_W1, L0_gnn_g1, L0_gnn_b1, L0_gnn_W2, L0_gnn_g2, L0_gnn_b2, L1_gnn_W_up0, L1_gnn_W_up1, L1_gnn_mlp_w0, L1_gnn_mlp_b0, L1_gnn_mlp_w1, L1_gnn_mlp_b1, L1_gnn_mlp_w2, L1_gnn_mlp_b2, L1_gnn_W_out0, L1_gnn_W_out1):
    import jax
    import jax.numpy as jnp

    def _L0_gnn_ref(h, edge_index, edge_attr, eps, W1, g1, b1, W2, g2, b2):
        import jax, jax.numpy as jnp
        import numpy as np
        N = 50000
        E = 20000
        D = 128
        H = 2 * D
        BN_EPS = 1e-05

        def _batchnorm(x, gamma, beta):
            mean = jnp.mean(x, axis=0)
            var = jnp.var(x, axis=0)
            return (x - mean) * jax.lax.rsqrt(var + BN_EPS) * gamma + beta
        n = h.shape[0]
        src = edge_index[0]
        dst = edge_index[1]
        msg = jax.nn.relu(h[src] + edge_attr)
        aggr = jax.ops.segment_sum(msg, dst, num_segments=n)
        z = (1.0 + eps) * h + aggr
        z = jax.nn.relu(_batchnorm(z @ W1, g1, b1))
        z = z @ W2
        z = jax.nn.relu(_batchnorm(z, g2, b2))
        return z + h

    def _L1_gnn_ref(node_feats, edge_vec, edge_length, senders, receivers, num_nodes, W_up0, W_up1, mlp_w0, mlp_b0, mlp_w1, mlp_b1, mlp_w2, mlp_b2, W_out0, W_out1):
        import jax, jax.numpy as jnp
        import numpy as np
        N = 50000
        E = 25000
        MUL = 32
        NB = 8
        R_MAX = 1.0
        AVG = 16.0
        SQ3 = 3.0 ** 0.5

        def _radial_embedding(r):
            x = jnp.clip(r / R_MAX, 0.0, 1.0)
            centers = jnp.arange(NB, dtype=jnp.float32) / (NB - 1)
            sigma = 1.0 / (NB - 1)
            emb = jnp.exp(-0.5 * ((x[:, None] - centers[None, :]) / sigma) ** 2)
            emb = emb * NB ** 0.5 * (r <= R_MAX).astype(jnp.float32)[:, None]
            return emb
        f32 = jnp.float32
        rhat = edge_vec / (jnp.linalg.norm(edge_vec, axis=-1, keepdims=True) + 1e-12)
        Y1 = SQ3 * rhat
        emb = _radial_embedding(edge_length)
        h = jax.nn.silu(emb @ mlp_w0 + mlp_b0)
        h = jax.nn.silu(h @ mlp_w1 + mlp_b1)
        w = (h @ mlp_w2 + mlp_b2).reshape(-1, 4, MUL)
        s = node_feats[:, :MUL]
        v = node_feats[:, MUL:].reshape(-1, MUL, 3)
        xs = s @ W_up0 / f32(MUL) ** 0.5
        xv = jnp.einsum('nmc,mk->nkc', v, W_up1) / f32(MUL) ** 0.5
        ss = xs[senders]
        vv = xv[senders]
        m0 = w[:, 0] * ss
        m1 = w[:, 1][:, :, None] * ss[:, :, None] * Y1[:, None, :]
        m2 = w[:, 2][:, :, None] * vv
        m3 = w[:, 3] * (jnp.einsum('emc,ec->em', vv, Y1) / SQ3)
        mid_s = jnp.concatenate([m0, m3], axis=1)
        mid_v = jnp.concatenate([m1, m2], axis=1)
        msg_s = jax.ops.segment_sum(mid_s, receivers, num_segments=num_nodes)
        msg_v = jax.ops.segment_sum(mid_v, receivers, num_segments=num_nodes)
        out_s = msg_s @ W_out0 / f32(2 * MUL) ** 0.5
        out_v = jnp.einsum('nmc,mk->nkc', msg_v, W_out1) / f32(2 * MUL) ** 0.5
        out = jnp.concatenate([out_s, out_v.reshape(-1, 3 * MUL)], axis=1)
        return out / max(AVG, 1e-08)
    edge_index = jnp.stack([src, dst])
    x = _layernorm(x + _L0_gnn_ref(x, edge_index, edge_attr_128, L0_gnn_eps, L0_gnn_W1, L0_gnn_g1, L0_gnn_b1, L0_gnn_W2, L0_gnn_g2, L0_gnn_b2), axis=-1)
    x = _layernorm(x + _L1_gnn_ref(x, edge_attr_3, edge_weight, src, dst, 50000, L1_gnn_W_up0, L1_gnn_W_up1, L1_gnn_mlp_w0, L1_gnn_mlp_b0, L1_gnn_mlp_w1, L1_gnn_mlp_b1, L1_gnn_mlp_w2, L1_gnn_mlp_b2, L1_gnn_W_out0, L1_gnn_W_out1), axis=-1)
    return x

_drawn_inputs = setup_inputs


def setup_inputs(seed=0):
    import zlib

    import numpy as np

    out = dict(_drawn_inputs(seed))
    spreads = {'L0_gnn_g1': (1.0, 0.2),
     'L0_gnn_b1': (0.0, 0.282),
     'L0_gnn_g2': (1.0, 0.2),
     'L0_gnn_b2': (0.0, 0.1),
     'L1_gnn_mlp_b0': (0.0, 0.8),
     'L1_gnn_mlp_b1': (0.0, 0.8),
     'L1_gnn_mlp_b2': (0.0, 0.8)}
    factors = {'edge_attr_3': 4.6,
     'edge_weight': 4.528,
     'L1_gnn_W_up0': 4.558,
     'L1_gnn_W_up1': 4.431,
     'L1_gnn_mlp_w0': 3.723,
     'L1_gnn_mlp_w1': 3.209,
     'L1_gnn_mlp_w2': 3.107,
     'L1_gnn_W_out0': 6.444,
     'L1_gnn_W_out1': 3.792}
    for name, (base, spread) in spreads.items():
        noise = np.random.default_rng([zlib.crc32(name.encode()), seed]).standard_normal(out[name].shape)
        drawn = base * np.exp(spread * noise) if base else spread * noise
        out[name] = jnp.asarray(drawn.astype(out[name].dtype))
    for name, factor in factors.items():
        out[name] = (out[name] * factor).astype(out[name].dtype)
    return out
```

```python
from contextlib import ExitStack

import concourse.bass as bass
from concourse import mybir

F32 = mybir.dt.float32
I32 = mybir.dt.int32
ALU = mybir.AluOpType
ACT = mybir.ActivationFunctionType
AX_X = mybir.AxisListType.X

P = 128
R = 125
TC = 4
CN = R * TC
WIN = 128
MW = 132
BN_EPS = 1e-5
LN_EPS = 1e-5
NO_ROW = 1 << 24


def split_rows(lo_hi=(0, 112, R)):
    return [(lo_hi[i], lo_hi[i + 1]) for i in range(2)]


def wait_reuse(eng, sem, value):
    if not (isinstance(value, int) and value == 0):
        eng.wait_ge(sem, value)


def wait_apart(eng, sem, value, passed):
    eng.wait_ge(sem, value)
    eng.sem_inc(passed, 1)


class Chain:

    def __init__(self, eng, sem):
        self.eng, self.sem, self.n = eng, sem, 0

    def step(self, ins):
        self.n += 1
        ins.then_inc(self.sem, 1)
        self.eng.wait_ge(self.sem, self.n)


def gnn_kernel(nc, x, src, dst, edge_attr_128, edge_attr_3, edge_weight, eps, W1, g1, b1, W2, g2, b2,
               W_up0, W_up1, mlp_w0, mlp_b0, mlp_w1, mlp_b1, mlp_w2, mlp_b2, W_out0, W_out1, out):
    N, D = x.shape
    E = src.shape[0]
    H = W1.shape[1]
    MUL = W_up0.shape[0]
    NB, HM = mlp_w0.shape
    NT, ET = N // R, E // R
    NC, EC = NT // TC, ET // TC
    THR = NT // (EC // 2)
    assert D == P and H == 2 * P and NT * R == N and ET * R == E and HM == 64 and NB == 8 and MUL == 32
    assert NC * TC == NT and EC * TC == ET and NC % 2 == 0 and EC % 2 == 0 and THR * (EC // 2) == NT and THR % 2 == 0

    msg = nc.dram_tensor("msg_rows", (E + WIN, MW), F32, kind="Internal").ap()
    zt_dram = nc.dram_tensor("z_transposed", (NC, P, CN), F32, kind="Internal").ap()
    x1_dram = nc.dram_tensor("x_after_layer0", (N, D), F32, kind="Internal").ap()
    h2_dram = nc.dram_tensor("radial_hidden", (EC // 2, P, CN), F32, kind="Internal").ap()

    agg = nc.dram_tensor("slow_path_sums", (N, D), F32, kind="Internal").ap()
    agg_tiles = agg.rearrange("(t p) d -> p t d", p=R)
    x_tiles = x.rearrange("(t p) d -> p t d", p=R)
    x1_tiles = x1_dram.rearrange("(t p) d -> p t d", p=R)
    out_tiles = out.rearrange("(t p) d -> p t d", p=R)
    ea_rows = edge_attr_128.rearrange("(p j) d -> p j d", j=ET)
    msg_rows = msg[0:E, :].rearrange("(p j) d -> p j d", j=ET)

    root = ExitStack()
    with root:
        def make(ctx):
            def sb(name, shape, dt=F32):
                return ctx.enter_context(nc.sbuf_tensor(name, shape, dt))

            def pb(name, shape=(P, 512)):
                return ctx.enter_context(nc.psum_tensor(name, list(shape), F32))

            def sem(name):
                return ctx.enter_context(nc.semaphore(name))
            return sb, pb, sem

        sb, pb, sem = make(root)

        ident = sb("ident", [P, P])
        ones = sb("ones", [P, P])
        node_iota = sb("node_iota", [P, R])
        tile_base = sb("tile_base", [P, NT])
        src_all = sb("src_all", [R, ET], I32)
        dst_f = sb("dst_f", [R, ET])
        rhat = sb("rhat", [R, ET, 3])
        emb = sb("emb", [R, ET, NB])
        eps1 = sb("eps1", [P, 1])
        w1 = sb("w1", [P, H])
        w2 = sb("w2", [P, 2, D])
        g1c, b1c = sb("g1c", [P, 2]), sb("b1c", [P, 2])
        g2c, b2c = sb("g2c", [P, 1]), sb("b2c", [P, 1])
        scale1, shift1 = sb("scale1", [P, 2]), sb("shift1", [P, 2])
        scale2, shift2 = sb("scale2", [P, 1]), sb("shift2", [P, 1])
        w_up = sb("w_up", [P, P])
        w_mlp0 = sb("w_mlp0", [64, 4, P])
        w_mlp1 = sb("w_mlp1", [P, P])
        w_mlp2 = sb("w_mlp2", [P, 2, 2, P])
        b_mlp0, b_mlp1, b_mlp2 = sb("b_mlp0", [P, 1]), sb("b_mlp1", [P, 1]), sb("b_mlp2", [P, 2])
        w_outA, w_outB = sb("w_outA", [P, P]), sb("w_outB", [P, P])
        starts = sb("starts", [1, NT], I32)
        slow_i = sb("slow_i", [1, 1], I32)
        unsorted = sb("unsorted", [R, 1])

        with ExitStack() as ctx:
            sb, pb, sem = make(ctx)
            dst_i = sb("dst_i", [R, ET], I32)
            next_i = sb("next_i", [R, ET], I32)
            next_f = sb("next_f", [R, ET])
            base_i = sb("base_i", [P, NT], I32)
            iota_i = sb("iota_i", [P, R], I32)
            k_i = sb("k_i", [R, NB], I32)
            k_f = sb("k_f", [R, NB])
            ew = sb("ew", [R, ET])
            xc = sb("xc", [R, ET])
            mask = sb("mask", [R, ET])
            ea3 = sb("ea3", [R, ET, 3])
            sq3 = sb("sq3", [R, ET, 3])
            nrm = sb("nrm", [R, ET])
            eps_in = sb("eps_in", [1, 1])
            tmpA, tmpB = sb("tmpA", [P, MUL]), sb("tmpB", [P, MUL])
            pad = sb("pad", [WIN, MW])
            p_eps = pb("p_eps")
            s_load = sem("inputs_loaded")
            s_blank = sem("tiles_blanked")
            s_wload = sem("weights_loaded")
            s_iota = sem("iotas_done")
            s_pool = sem("pool_step")
            s_ones = sem("ones_ready")
            s_pad = sem("pad_ready")
            s_padst = sem("pad_stored")
            s_epsmm = sem("eps_broadcast")
            s_dve = sem("dve_step")
            s_sqn = sem("norm_squared")
            s_nrm = sem("norm_ready")
            s_embx = sem("exponent_ready")
            s_embe = sem("exp_done")
            s_next = sem("next_blanked")
            with nc.Block() as block:
                n_loads = 14

                @block.sync
                def _(sp):
                    def load(dst_ap, src_ap, s):
                        sp.dma_start(dst_ap, src_ap, allow_slow_non_contiguous=True).then_inc(s, 16)

                    load(dst_i[:, :], dst.rearrange("(p j) -> p j", j=ET), s_load)
                    sp.wait_ge(s_next, 1)
                    load(next_i[0:R - 1, :], dst[1:1 + (R - 1) * ET].rearrange("(p j) -> p j", j=ET), s_load)
                    load(next_i[R - 1:R, 0:ET - 1], dst[1 + (R - 1) * ET:E].rearrange("(p j) -> p j", p=1), s_load)
                    load(src_all[:, :], src.rearrange("(p j) -> p j", j=ET), s_load)
                    load(ew[:, :], edge_weight.rearrange("(p j) -> p j", j=ET), s_load)
                    load(ea3[:, :, :], edge_attr_3.rearrange("(p j) c -> p j c", j=ET), s_load)
                    load(eps_in[:, :], eps.rearrange("(a b) -> a b", a=1), s_load)
                    load(w1[:, :], W1, s_load)
                    load(w2[:, :, :], W2.rearrange("(h p) d -> p h d", p=P), s_load)
                    load(g1c[:, :], g1.rearrange("(h p) -> p h", p=P), s_load)
                    load(b1c[:, :], b1.rearrange("(h p) -> p h", p=P), s_load)
                    load(g2c[:, :], g2.rearrange("(p a) -> p a", a=1), s_load)
                    load(b2c[:, :], b2.rearrange("(p a) -> p a", a=1), s_load)
                    load(b_mlp2[0:MUL, 0:1], mlp_b2[0:MUL].rearrange("(p a) -> p a", a=1), s_load)
                    sp.wait_ge(s_blank, 8)
                    n = 0
                    load(w_up[0:MUL, 0:MUL], W_up0, s_wload)
                    for c in range(3):
                        load(w_up[MUL + c:P:3, MUL * (c + 1):MUL * (c + 2)], W_up1, s_wload)
                    for v in range(4):
                        load(w_mlp0[NB * v:NB * v + NB, v, 0:HM], mlp_w0, s_wload)
                        load(w_mlp0[NB * (v + 4):NB * (v + 5), v, HM:P], mlp_w0, s_wload)
                    for h in range(2):
                        rows = slice(HM * h, HM * h + HM)
                        load(w_mlp1[rows, HM * h:HM * h + HM], mlp_w1, s_wload)
                        load(b_mlp0[rows, :], mlp_b0.rearrange("(p a) -> p a", a=1), s_wload)
                        load(b_mlp1[rows, :], mlp_b1.rearrange("(p a) -> p a", a=1), s_wload)
                        for q in range(2):
                            load(w_mlp2[rows, h, q, 0:MUL], mlp_w2[:, MUL * q:MUL * (q + 1)], s_wload)
                            for c in range(3):
                                load(w_mlp2[rows, h, q, MUL * (c + 1):MUL * (c + 2)],
                                     mlp_w2[:, MUL * (q + 2):MUL * (q + 3)], s_wload)
                    for q in range(2):
                        if q:
                            load(b_mlp2[0:MUL, 1:2], mlp_b2[MUL:2 * MUL].rearrange("(p a) -> p a", a=1), s_wload)
                        for c in range(3):
                            load(b_mlp2[MUL * (c + 1):MUL * (c + 2), q:q + 1],
                                 mlp_b2[MUL * (q + 2):MUL * (q + 3)].rearrange("(p a) -> p a", a=1), s_wload)
                    load(w_outA[0:MUL, 0:MUL], W_out0[0:MUL, :], s_wload)
                    load(w_outB[0:MUL, 0:MUL], W_out1[0:MUL, :], s_wload)
                    for c in range(3):
                        load(tmpA[MUL * (c + 1):MUL * (c + 2), :], W_out1[MUL:2 * MUL, :], s_wload)
                        load(tmpB[MUL * (c + 1):MUL * (c + 2), :], W_out0[MUL:2 * MUL, :], s_wload)
                    sp.wait_ge(s_pad, 2)
                    sp.dma_start(msg[E:E + WIN, :], pad[:, :]).then_inc(s_padst, 16)
                    sp.wait_ge(s_padst, 16)

                n_wload = 1 + 3 + 8 + 2 * (3 + 8) + 7 + 2 + 6

                @block.gpsimd
                def _(pool):
                    pool.memset(ident[:, :], 0.0).then_inc(s_pool, 1)
                    pool.wait_ge(s_pool, 1)
                    pool.affine_select(out=ident[:, :], in_=ident[:, :], compare_op=ALU.not_equal, fill=1.0,
                                       base=0, pattern=[[-1, P]], channel_multiplier=1)
                    pool.iota(iota_i[:, :], [[1, R]], base=0, channel_multiplier=0).then_inc(s_iota, 1)
                    pool.iota(base_i[:, :], [[R, NT]], base=0, channel_multiplier=0).then_inc(s_iota, 1)
                    pool.iota(k_i[:, :], [[1, NB]], base=0, channel_multiplier=0).then_inc(s_iota, 1)

                @block.tensor
                def _(pe):
                    pe.wait_ge(s_ones, 1)
                    pe.wait_ge(s_load, 16 * n_loads)
                    pe.matmul(p_eps[:, 0:1], ones[0:1, :], eps_in[:, :], start=True, stop=True).then_inc(s_epsmm, 1)

                @block.scalar
                def _(act):
                    act.wait_ge(s_sqn, 1)
                    act.activation(nrm[:, :], nrm[:, :], ACT.Sqrt).then_inc(s_nrm, 1)
                    act.wait_ge(s_embx, 1)
                    act.activation(emb[:, :, :], emb[:, :, :], ACT.Exp, scale=-0.5).then_inc(s_embe, 1)

                @block.vector
                def _(dve):
                    dve.memset(next_i[:, :], NO_ROW).then_inc(s_next, 1)
                    dve.memset(ones[:, :], 1.0).then_inc(s_ones, 1)
                    for t in (w_up, w_mlp1, w_outA, w_outB):
                        dve.memset(t[:, :], 0.0).then_inc(s_blank, 1)
                    dve.memset(w_mlp0[:, :, :], 0.0).then_inc(s_blank, 1)
                    dve.memset(w_mlp2[:, :, :, :], 0.0).then_inc(s_blank, 1)
                    dve.memset(tmpA[:, :], 0.0).then_inc(s_blank, 1)
                    dve.memset(tmpB[:, :], 0.0).then_inc(s_blank, 1)
                    dve.memset(pad[:, :], 0.0).then_inc(s_pad, 1)
                    dve.wait_ge(s_pad, 1)
                    dve.memset(pad[:, D:D + 1], -1.0).then_inc(s_pad, 1)
                    ch = Chain(dve, s_dve)
                    dve.wait_ge(s_iota, 3)
                    dve.tensor_copy(node_iota[:, :], iota_i[:, :])
                    dve.tensor_copy(tile_base[:, :], base_i[:, :])
                    ch.step(dve.tensor_copy(k_f[:, :], k_i[:, :]))
                    dve.wait_ge(s_load, 16 * n_loads)
                    ch.step(dve.tensor_copy(dst_f[:, :], dst_i[:, :]))
                    ch.step(dve.tensor_copy(next_f[:, :], next_i[:, :]))
                    ch.step(dve.tensor_tensor(next_f[:, :], next_f[:, :], dst_f[:, :], ALU.is_lt))
                    dve.tensor_reduce(unsorted[:, :], next_f[:, :], AX_X, ALU.add)
                    ch.step(dve.tensor_tensor(sq3[:, :, :], ea3[:, :, :], ea3[:, :, :], ALU.mult))
                    dve.tensor_reduce(nrm[:, :], sq3[:, :, :], AX_X, ALU.add).then_inc(s_sqn, 1)
                    ch.step(dve.tensor_scalar(xc[:, :], ew[:, :], 0.0, 1.0, ALU.max, ALU.min))
                    ch.step(dve.tensor_scalar(xc[:, :], xc[:, :], float(NB - 1), None, ALU.mult))
                    ch.step(dve.tensor_scalar(mask[:, :], ew[:, :], 1.0, float(NB) ** 0.5, ALU.is_le, ALU.mult))
                    ch.step(dve.tensor_tensor(emb[:, :, :], xc[:, :].unsqueeze(2).to_broadcast([R, ET, NB]),
                                              k_f[:, :].unsqueeze(1).to_broadcast([R, ET, NB]), ALU.subtract))
                    dve.tensor_tensor(emb[:, :, :], emb[:, :, :], emb[:, :, :], ALU.mult).then_inc(s_embx, 1)
                    dve.wait_ge(s_nrm, 1)
                    ch.step(dve.tensor_scalar(nrm[:, :], nrm[:, :], 1e-12, None, ALU.add))
                    ch.step(dve.reciprocal(nrm[:, :], nrm[:, :]))
                    dve.tensor_tensor(rhat[:, :, :], ea3[:, :, :], nrm[:, :].unsqueeze(2).to_broadcast([R, ET, 3]),
                                      ALU.mult)
                    dve.wait_ge(s_embe, 1)
                    dve.tensor_tensor(emb[:, :, :], emb[:, :, :], mask[:, :].unsqueeze(2).to_broadcast([R, ET, NB]),
                                      ALU.mult)
                    dve.wait_ge(s_epsmm, 1)
                    dve.tensor_scalar(eps1[:, :], p_eps[:, 0:1], 1.0, None, ALU.add)
                    dve.wait_ge(s_wload, 16 * n_wload)
                    dve.tensor_scalar(w_up[:, :], w_up[:, :], float(MUL) ** -0.5, None, ALU.mult)
                    c_out = float(2 * MUL) ** -0.5 / 16.0
                    for w, t, head in ((w_outA, tmpA, c_out), (w_outB, tmpB, c_out * 3.0 ** 0.5)):
                        dve.tensor_scalar(w[0:MUL, 0:MUL], w[0:MUL, 0:MUL], head, None, ALU.mult)
                        for c in range(3):
                            rows = slice(MUL * (c + 1), MUL * (c + 2))
                            dve.tensor_scalar(w[rows, MUL + c:P:3], t[rows, :], c_out, None, ALU.mult)

        with ExitStack() as ctx:
            sb, pb, sem = make(ctx)
            xg = [sb(f"xg{b}", [R, TC, D]) for b in range(2)]
            ea = [sb(f"ea{b}", [R, TC, D]) for b in range(2)]
            mo = [sb(f"mo{b}", [R, TC, MW]) for b in range(2)]
            idx = [sb(f"idx{b}", [R, TC], I32) for b in range(2)]
            less = [sb(f"less{b}", [R, THR // 2, ET]) for b in range(2)]
            counts = sb("counts", [R, NT])
            emb_in = sb("emb_in", [R, P])
            emb_t = sb("emb_t", [2 * TC * NB, R])
            h1 = sb("h1", [P, CN])
            h2 = sb("h2", [P, CN])
            p_t, p_h1, p_h2 = pb("p_t"), pb("p_h1"), pb("p_h2")
            g_done = [sem(f"rows_gathered{b}") for b in range(2)]
            i_ready = [sem(f"index_ready{b}") for b in range(2)]
            i_passed = sem("index_wait_passed")
            e_load = [sem(f"attr_loaded{b}") for b in range(2)]
            m_sum = sem("messages_summed")
            m_dst = sem("destination_written")
            m_relu = sem("messages_ready")
            m_store = [sem(f"messages_stored{b}") for b in range(2)]
            c_less = sem("compared")
            c_cnt = sem("counted")
            r_blank = sem("embedding_tile_blanked")
            r_in = sem("embedding_copied")
            r_t = sem("embedding_transposed")
            r_tc = sem("embedding_transpose_copied")
            r_m0, r_m1 = sem("mlp0_product"), sem("mlp1_product")
            r_h1, r_h2 = sem("hidden1_ready"), sem("hidden2_ready")
            r_store = sem("hidden2_stored")
            b_blank = sem("messages_blanked")
            with nc.Block() as block:

                @block.gpsimd
                def _(pool):
                    for b in range(2):
                        pool.memset(mo[b][:, :, :], 0.0).then_inc(b_blank, 1)
                    def rounds(k):
                        for b in range(2):
                            wait_reuse(pool, g_done[b], k * (16 * TC))
                            wait_reuse(pool, m_relu, k * 2)
                            pool.tensor_copy(idx[b][:, :], src_all[:, bass.ds(k * (2 * TC) + b * TC, TC)])\
                                .then_inc(i_ready[b], 1)
                            wait_apart(pool, i_ready[b], k + 1, i_passed)
                            for j in range(TC):
                                pool.indirect_dma_start(
                                    out=xg[b][:, j, :], out_offset=None, in_=x,
                                    in_offset=bass.IndirectOffsetOnAxis(ap=idx[b][:, j:j + 1], axis=0),
                                    bounds_check=N - 1, oob_is_err=False).then_inc(g_done[b], 16)

                    rounds(0)
                    with pool.Fori(1, EC // 2) as k:
                        rounds(k)

                @block.sync
                def _(sp):
                    def rounds(k):
                        for b in range(2):
                            wait_reuse(sp, m_sum, k * 2)
                            for lo, hi in split_rows():
                                sp.dma_start(ea[b][lo:hi, :, :], ea_rows[lo:hi, bass.ds(k * (2 * TC) + b * TC, TC), :])\
                                    .then_inc(e_load[b], 16)

                    rounds(0)
                    with sp.Fori(1, EC // 2) as k:
                        rounds(k)

                @block.scalar
                def _(act):
                    def rounds(k):
                        for b in range(2):
                            act.wait_ge(m_sum, k * 2 + b + 1)
                            act.wait_ge(b_blank, 2)
                            wait_reuse(act, m_store[b], k * 32)
                            act.activation(mo[b][:, :, 0:D], xg[b][:, :, :], ACT.Relu).then_inc(m_relu, 1)
                            act.wait_ge(m_relu, k * 2 + b + 1)
                            act.wait_ge(m_dst, k * 2 + b + 1)
                            for lo, hi in split_rows():
                                act.dma_start(msg_rows[lo:hi, bass.ds(k * (2 * TC) + b * TC, TC), :],
                                              mo[b][lo:hi, :, :]).then_inc(m_store[b], 16)
                        act.wait_ge(r_t, k + 1)
                        act.activation(emb_t[:, :], p_t[0:2 * TC * NB, 0:R], ACT.Copy).then_inc(r_tc, 1)
                        act.wait_ge(r_m0, k + 1)
                        act.activation(h1[:, :], p_h1[:, 0:CN], ACT.Silu, bias=b_mlp0[:, 0:1]).then_inc(r_h1, 1)
                        act.wait_ge(r_m1, k + 1)
                        wait_reuse(act, r_store, k * 16)
                        act.activation(h2[:, :], p_h2[:, 0:CN], ACT.Silu, bias=b_mlp1[:, 0:1]).then_inc(r_h2, 1)
                        act.wait_ge(r_h2, k + 1)
                        act.dma_start(h2_dram[bass.ds(k, 1), :, :].rearrange("a p n -> (a p) n"), h2[:, :])\
                            .then_inc(r_store, 16)

                    rounds(0)
                    with act.Fori(1, EC // 2) as k:
                        rounds(k)
                    for b in range(2):
                        act.wait_ge(m_store[b], 32 * (EC // 2))
                    act.wait_ge(r_store, 16 * (EC // 2))

                @block.vector
                def _(dve):
                    dve.memset(emb_in[:, :], 0.0).then_inc(r_blank, 1)
                    dve.wait_ge(r_blank, 1)
                    def rounds(k):
                        wait_reuse(dve, r_t, k)
                        dve.tensor_copy(emb_in[:, 0:2 * TC * NB].rearrange("p (j n) -> p j n", n=NB),
                                        emb[:, bass.ds(k * (2 * TC), 2 * TC), :]).then_inc(r_in, 1)
                        for b in range(2):
                            dve.wait_ge(g_done[b], (k + 1) * (16 * TC))
                            dve.wait_ge(e_load[b], (k + 1) * 32)
                            dve.tensor_tensor(xg[b][:, :, :], xg[b][:, :, :], ea[b][:, :, :], ALU.add)\
                                .then_inc(m_sum, 1)
                            dve.wait_ge(b_blank, 2)
                            wait_reuse(dve, m_store[b], k * 32)
                            dve.tensor_copy(mo[b][:, :, D:D + 1],
                                            dst_f[:, bass.ds(k * (2 * TC) + b * TC, TC)].unsqueeze(2))\
                                .then_inc(m_dst, 1)
                            half = THR // 2
                            wait_reuse(dve, c_cnt, k * 2)
                            dve.tensor_tensor(
                                less[b][:, :, :], dst_f[:, :].unsqueeze(1).to_broadcast([R, half, ET]),
                                tile_base[0:R, bass.ds(k * THR + b * half, half)].unsqueeze(2)
                                .to_broadcast([R, half, ET]), ALU.is_lt).then_inc(c_less, 1)
                            dve.wait_ge(c_less, k * 2 + b + 1)
                            dve.tensor_reduce(counts[:, bass.ds(k * THR + b * half, half)], less[b][:, :, :],
                                              AX_X, ALU.add).then_inc(c_cnt, 1)

                    rounds(0)
                    with dve.Fori(1, EC // 2) as k:
                        rounds(k)

                @block.tensor
                def _(pe):
                    def rounds(k):
                        pe.wait_ge(r_in, k + 1)
                        wait_reuse(pe, r_tc, k)
                        pe.transpose(p_t[:, 0:R], emb_in[:, :], ident[0:R, 0:R]).then_inc(r_t, 1)
                        pe.wait_ge(r_tc, k + 1)
                        wait_reuse(pe, r_h1, k)
                        for v in range(TC):
                            mm = pe.matmul(p_h1[:, v * R:(v + 1) * R], w_mlp0[:, v, :], emb_t[:, :],
                                           start=True, stop=True)
                        mm.then_inc(r_m0, 1)
                        pe.wait_ge(r_h1, k + 1)
                        wait_reuse(pe, r_h2, k)
                        pe.matmul(p_h2[:, 0:CN], w_mlp1[:, :], h1[:, :], start=True, stop=True).then_inc(r_m1, 1)

                    rounds(0)
                    with pe.Fori(1, EC // 2) as k:
                        rounds(k)


            p_cnt = pb("p_cnt")
            s_cnt = sem("counts_summed")
            s_step = sem("tables_step")
            first = sb("first", [1, NT + 1])
            size = sb("size", [1, NT])
            flags = sb("flags", [1, 2])
            with nc.Block() as block:
                @block.tensor
                def _(pe):
                    pe.matmul(p_cnt[0:1, 0:NT], ones[0:R, 0:1], counts[:, :], start=True, stop=True)
                    pe.matmul(p_cnt[0:1, NT:NT + 1], ones[0:R, 0:1], unsorted[:, :], start=True, stop=True)\
                        .then_inc(s_cnt, 1)

                @block.vector
                def _(dve):
                    ch = Chain(dve, s_step)
                    dve.wait_ge(s_cnt, 1)
                    ch.step(dve.tensor_copy(first[:, 0:NT], p_cnt[0:1, 0:NT]))
                    ch.step(dve.memset(first[:, NT:NT + 1], float(E)))
                    ch.step(dve.tensor_tensor(size[:, :], first[:, 1:NT + 1], first[:, 0:NT], ALU.subtract))
                    ch.step(dve.tensor_reduce(flags[:, 0:1], size[:, :], AX_X, ALU.max))
                    ch.step(dve.tensor_scalar(flags[:, 0:1], flags[:, 0:1], float(WIN), None, ALU.is_gt))
                    ch.step(dve.tensor_scalar(flags[:, 1:2], p_cnt[0:1, NT:NT + 1], 0.0, None, ALU.is_gt))
                    ch.step(dve.tensor_tensor(flags[:, 0:1], flags[:, 0:1], flags[:, 1:2], ALU.max))
                    ch.step(dve.tensor_copy(slow_i[:, :], flags[:, 0:1]))
                    ch.step(dve.tensor_scalar(size[:, :], first[:, 0:NT], -1.0, float(E), ALU.mult, ALU.add))
                    ch.step(dve.scalar_tensor_tensor(out=size[:, :], in0=size[:, :], scalar=flags[:, 0:1],
                                                     in1=first[:, 0:NT], op0=ALU.mult, op1=ALU.add))
                    ch.step(dve.tensor_copy(starts[:, :], size[:, :]))

        def slow_path(layer):
            with ExitStack() as ctx:
                sb, pb, _ = make(ctx)
                taken = []

                def sem(name):
                    taken.append(nc.alloc_semaphore(name))
                    return taken[-1]

                zero = sb(f"slow{layer}_zero", [R, TC, D])
                below = sb(f"slow{layer}_below", [R, R])
                rows = sb(f"slow{layer}_rows", [R, MW])
                dmat = sb(f"slow{layer}_dmat", [R, P])
                same = sb(f"slow{layer}_same", [R, R])
                earlier = sb(f"slow{layer}_earlier", [R, R])
                place = sb(f"slow{layer}_place", [R, 2])
                at = sb(f"slow{layer}_at", [R, 2], I32)
                held = sb(f"slow{layer}_held", [R, D])
                total = sb(f"slow{layer}_total", [R, D])
                p_d, p_s = pb(f"slow{layer}_p_d"), pb(f"slow{layer}_p_s")
                s_blank = sem(f"slow{layer}_blanked")
                s_zero = sem(f"slow{layer}_zeroed")
                s_below = sem(f"slow{layer}_below_ready")
                s_rows = sem(f"slow{layer}_rows_loaded")
                s_dmat, s_dt = sem(f"slow{layer}_dmat_ready"), sem(f"slow{layer}_dmat_transposed")
                s_same, s_sum = sem(f"slow{layer}_same_ready"), sem(f"slow{layer}_summed")
                s_step = sem(f"slow{layer}_dve_step")
                s_at, s_got = sem(f"slow{layer}_index_ready"), sem(f"slow{layer}_held_loaded")
                s_tot, s_put = sem(f"slow{layer}_total_ready"), sem(f"slow{layer}_total_stored")
                s_pass = sem(f"slow{layer}_wait_passed")
                steps = 6

                with nc.Block() as block:
                    @block.sync
                    def _(sp):
                        with sp.If(sp.value_load(slow_i[0:1, 0:1], min_val=0, max_val=1) > 0):
                            sp.wait_ge(s_blank, 1)

                            def blank(k):
                                for lo, hi in split_rows():
                                    sp.dma_start(agg_tiles[lo:hi, bass.ds(k * TC, TC), :], zero[lo:hi, :, :])\
                                        .then_inc(s_zero, 16)

                            with sp.Fori(0, NC) as k:
                                blank(k)

                            def load(t):
                                wait_reuse(sp, s_put, t * 16)
                                sp.dma_start(rows[:, :], msg[bass.ds(t * R, R), :]).then_inc(s_rows, 16)

                            load(0)
                            with sp.Fori(1, ET) as t:
                                load(t)

                    @block.gpsimd
                    def _(pool):
                        with pool.If(pool.value_load(slow_i[0:1, 0:1], min_val=0, max_val=1) > 0):
                            pool.memset(below[:, :], 1.0).then_inc(s_pass, 1)
                            pool.wait_ge(s_pass, 1)
                            pool.affine_select(out=below[:, :], in_=below[:, :], compare_op=ALU.is_gt, fill=0.0,
                                               base=0, pattern=[[-1, R]], channel_multiplier=1).then_inc(s_below, 1)
                            pool.wait_ge(s_zero, 32 * NC)

                            def update(t):
                                wait_apart(pool, s_at, t + 1, s_pass)
                                pool.indirect_dma_start(
                                    out=held[:, :], out_offset=None, in_=agg,
                                    in_offset=bass.IndirectOffsetOnAxis(ap=at[:, 0:1], axis=0),
                                    bounds_check=N - 1, oob_is_err=False).then_inc(s_got, 16)
                                wait_apart(pool, s_tot, t + 1, s_pass)
                                pool.indirect_dma_start(
                                    out=agg, out_offset=bass.IndirectOffsetOnAxis(ap=at[:, 1:2], axis=0),
                                    in_=held[:, :], in_offset=None,
                                    bounds_check=N - 1, oob_is_err=False).then_inc(s_put, 16)

                            update(0)
                            with pool.Fori(1, ET) as t:
                                update(t)
                            pool.wait_ge(s_put, 16 * ET)

                    @block.tensor
                    def _(pe):
                        with pe.If(pe.value_load(slow_i[0:1, 0:1], min_val=0, max_val=1) > 0):
                            def sums(t):
                                pe.wait_ge(s_dmat, t + 1)
                                pe.transpose(p_d[:, 0:R], dmat[:, :], ident[0:R, 0:R]).then_inc(s_dt, 1)
                                pe.wait_ge(s_same, t + 1)
                                pe.matmul(p_s[0:R, 0:D], same[:, :], rows[:, 0:D], start=True, stop=True)\
                                    .then_inc(s_sum, 1)

                            sums(0)
                            with pe.Fori(1, ET) as t:
                                sums(t)

                    @block.vector
                    def _(dve):
                        with dve.If(dve.value_load(slow_i[0:1, 0:1], min_val=0, max_val=1) > 0):
                            dve.memset(zero[:, :, :], 0.0).then_inc(s_blank, 1)

                            def combine(t):
                                def step(n, ins):
                                    ins.then_inc(s_step, 1)
                                    dve.wait_ge(s_step, t * steps + n)

                                dve.wait_ge(s_rows, (t + 1) * 16)
                                dve.tensor_copy(dmat[:, :], rows[:, D:D + 1].to_broadcast([R, P])).then_inc(s_dmat, 1)
                                dve.wait_ge(s_dt, t + 1)
                                dve.tensor_scalar(same[:, :], p_d[0:R, 0:R], rows[:, D:D + 1], None, ALU.is_equal)\
                                    .then_inc(s_same, 1)
                                dve.wait_ge(s_same, t + 1)
                                dve.wait_ge(s_below, 1)
                                step(1, dve.tensor_tensor(earlier[:, :], same[:, :], below[:, :], ALU.mult))
                                step(2, dve.tensor_reduce(place[:, 0:1], earlier[:, :], AX_X, ALU.add))
                                step(3, dve.tensor_scalar(place[:, 1:2], place[:, 0:1], float(NO_ROW), None, ALU.mult))
                                step(4, dve.tensor_tensor(place[:, 1:2], place[:, 1:2], rows[:, D:D + 1], ALU.add))
                                step(5, dve.tensor_copy(at[:, 1:2], place[:, 1:2]))
                                dve.tensor_copy(at[:, 0:1], rows[:, D:D + 1]).then_inc(s_at, 1)
                                dve.wait_ge(s_sum, t + 1)
                                step(6, dve.tensor_copy(total[:, :], p_s[0:R, 0:D]))
                                dve.wait_ge(s_got, (t + 1) * 16)
                                dve.tensor_tensor(held[:, :], held[:, :], total[:, :], ALU.add).then_inc(s_tot, 1)

                            combine(0)
                            with dve.Fori(1, ET) as t:
                                combine(t)

                nc.clear_and_free_semaphores(taken)
                nc.all_engine_barrier()

        def either(eng, program):
            with eng.If(eng.value_load(slow_i[0:1, 0:1], min_val=0, max_val=1) > 0):
                program(True)
            with eng.Else():
                program(False)

        def windows(sp, win, w_load, k, b):
            for j in range(TC):
                first = sp.value_load(starts[0:1, bass.ds((k * 2 + b) * TC + j, 1)], min_val=0, max_val=E)
                sp.dma_start(win[b][:, j, :], msg[bass.ds(first, WIN), :]).then_inc(w_load[b], 16)

        def one_hot(eng, hot, local, b):
            for j in range(TC):
                ins = eng.tensor_scalar(hot[b][:, j, :], node_iota[:, :], local[b][:, j:j + 1], None, ALU.is_equal)
            return ins

        slow_path(0)

        with ExitStack() as ctx:
            sb, pb, sem = make(ctx)
            xs = [sb(f"xs{b}", [R, TC, D]) for b in range(2)]
            ax = [sb(f"ax{b}", [R, TC, D]) for b in range(2)]
            win = [sb(f"win{b}", [P, TC, MW]) for b in range(2)]
            local = [sb(f"local{b}", [P, TC]) for b in range(2)]
            hot = [sb(f"hot{b}", [P, TC, R]) for b in range(2)]
            z = [sb(f"z{b}", [R, TC, D + 4]) for b in range(2)]
            zt = [sb(f"zt{b}", [P, CN]) for b in range(2)]
            zero = sb("zero", [R, D + 4])
            p_agg = [pb(f"p_agg{b}") for b in range(2)]
            p_zt = [pb(f"p_zt{b}") for b in range(2)]
            p_gram = pb("p_gram")
            x_load = [sem(f"nodes_loaded{b}") for b in range(2)]
            s_load = [sem(f"ax_loaded{b}") for b in range(2)]
            w_load = [sem(f"windows_loaded{b}") for b in range(2)]
            l_ready, l_passed = sem("local_ready"), sem("local_wait_passed")
            o_ready = sem("one_hot_ready")
            a_done = sem("messages_added")
            z_ready = sem("z_ready")
            z_used = sem("z_used")
            t_copied = sem("z_transpose_copied")
            t_store = [sem(f"z_stored{b}") for b in range(2)]
            z_blank = sem("z_blanked")
            with nc.Block() as block:
                @block.sync
                def _(sp):
                    def program(slow):
                        def rounds(k):
                            for b in range(2):
                                wait_reuse(sp, z_ready, k * 2)
                                for lo, hi in split_rows():
                                    sp.dma_start(xs[b][lo:hi, :, :], x_tiles[lo:hi, bass.ds((k * 2 + b) * TC, TC), :])\
                                        .then_inc(x_load[b], 16)
                                if slow:
                                    for lo, hi in split_rows():
                                        sp.dma_start(ax[b][lo:hi, :, :],
                                                     agg_tiles[lo:hi, bass.ds((k * 2 + b) * TC, TC), :])\
                                            .then_inc(s_load[b], 16)
                                windows(sp, win, w_load, k, b)

                        rounds(0)
                        with sp.Fori(1, NC // 2) as k:
                            rounds(k)

                    either(sp, program)

                @block.gpsimd
                def _(pool):
                    def rounds(k):
                        for b in range(2):
                            pool.wait_ge(w_load[b], (k + 1) * (16 * TC))
                            wait_reuse(pool, o_ready, k * 2)
                            pool.tensor_tensor(local[b][:, :].unsqueeze(2), win[b][:, :, D:D + 1],
                                               tile_base[:, bass.ds((k * 2 + b) * TC, TC)].unsqueeze(2),
                                               ALU.subtract).then_inc(l_ready, 1)
                            wait_reuse(pool, a_done, k * 2)
                            wait_apart(pool, l_ready, k * 2 + b + 1, l_passed)
                            one_hot(pool, hot, local, b).then_inc(o_ready, 1)

                    rounds(0)
                    with pool.Fori(1, NC // 2) as k:
                        rounds(k)

                @block.vector
                def _(dve):
                    dve.memset(zero[:, :], 0.0).then_inc(z_blank, 1)
                    for b in range(2):
                        dve.memset(z[b][:, :, D:D + 4], 1.0).then_inc(z_blank, 1)
                    def program(slow):
                        def rounds(k):
                            for b in range(2):
                                dve.wait_ge(x_load[b], (k + 1) * 32)
                                dve.wait_ge(a_done, k * 2 + b + 1)
                                if slow:
                                    dve.wait_ge(s_load[b], (k + 1) * 32)
                                wait_reuse(dve, z_used, k * 2)
                                dve.scalar_tensor_tensor(
                                    out=z[b][:, :, 0:D], in0=xs[b][:, :, :], scalar=eps1[0:R, 0:1],
                                    in1=ax[b][:, :, :] if slow else p_agg[b][0:R, :].rearrange("p (j d) -> p j d", d=D),
                                    op0=ALU.mult, op1=ALU.add).then_inc(z_ready, 1)

                        rounds(0)
                        with dve.Fori(1, NC // 2) as k:
                            rounds(k)

                    either(dve, program)

                @block.tensor
                def _(pe):
                    def aggregate(b, n):
                        pe.wait_ge(o_ready, n * 2 + b + 1)
                        wait_reuse(pe, z_ready, n * 2)
                        for j in range(TC):
                            mm = pe.matmul(p_agg[b][0:R, j * D:(j + 1) * D], hot[b][:, j, :], win[b][:, j, 0:D],
                                           start=True, stop=True)
                        mm.then_inc(a_done, 1)

                    def moments(b, n):
                        pe.wait_ge(z_ready, n * 2 + b + 1)
                        wait_reuse(pe, t_copied, n * 2)
                        for j in range(TC):
                            pe.matmul(p_gram[:, 0:D + 1], z[b][:, j, 0:D], z[b][:, j, 0:D + 1],
                                      start=False, stop=False, skip_group_check=True)
                        for j in range(TC):
                            mm = pe.transpose(p_zt[b][:, j * R:(j + 1) * R], z[b][:, j, 0:D], ident[0:R, 0:R])
                        mm.then_inc(z_used, 1)

                    pe.wait_ge(z_blank, 3)
                    pe.matmul(p_gram[:, 0:D + 1], zero[:, 0:D], zero[:, 0:D + 1], start=True, stop=False,
                              skip_group_check=True)
                    aggregate(0, 0)
                    def rounds(k):
                        aggregate(1, k)
                        moments(0, k)
                        aggregate(0, k + 1)
                        moments(1, k)

                    rounds(0)
                    with pe.Fori(1, NC // 2 - 1) as k:
                        rounds(k)
                    aggregate(1, NC // 2 - 1)
                    moments(0, NC // 2 - 1)
                    moments(1, NC // 2 - 1)

                @block.scalar
                def _(act):
                    def rounds(k):
                        for b in range(2):
                            act.wait_ge(z_used, k * 2 + b + 1)
                            wait_reuse(act, t_store[b], k * 16)
                            act.activation(zt[b][:, :], p_zt[b][:, 0:CN], ACT.Copy).then_inc(t_copied, 1)
                            act.wait_ge(t_copied, k * 2 + b + 1)
                            act.dma_start(zt_dram[bass.ds(k * 2 + b, 1), :, :].rearrange("a p n -> (a p) n"),
                                          zt[b][:, :]).then_inc(t_store[b], 16)

                    rounds(0)
                    with act.Fori(1, NC // 2) as k:
                        rounds(k)
                    for b in range(2):
                        act.wait_ge(t_store[b], 16 * (NC // 2))

            cov = sb("cov", [P, D])
            mean = sb("mean", [P, 1])
            mean_row = sb("mean_row", [1, P])
            neg_row = sb("neg_row", [1, P])
            wc = sb("wc", [P, H])
            var1, mean1 = sb("var1", [P, 2]), sb("mean1", [P, 2])
            p_s = pb("p_s")
            p_row = pb("p_row")
            s_step = sem("bn1_dve_step")
            s_mean, s_row, s_rowc = sem("mean_ready"), sem("mean_transposed"), sem("mean_row_ready")
            s_outer, s_cov, s_cw, s_wc = sem("outer_added"), sem("cov_ready"), sem("cov_w"), sem("w_cov_w")
            s_var, s_std, s_sq = sem("moments_ready"), sem("variance_ready"), sem("std_ready")
            with nc.Block() as block:
                @block.tensor
                def _(pe):
                    pe.wait_ge(s_mean, 1)
                    pe.transpose(p_row[0:1, 0:P], mean[:, :], ident[:, :]).then_inc(s_row, 1)
                    pe.wait_ge(s_rowc, 2)
                    pe.matmul(p_s[:, 0:D], neg_row[:, :], mean_row[:, :], start=True, stop=True)\
                        .then_inc(s_outer, 1)
                    pe.wait_ge(s_cov, 1)
                    pe.matmul(p_row[:, 0:H], cov[:, :], w1[:, :], start=True, stop=True).then_inc(s_cw, 1)
                    pe.wait_ge(s_wc, 1)
                    for h in range(2):
                        pe.matmul(p_s[:, h:h + 1], wc[:, h * P:(h + 1) * P], ones[:, 0:1], start=True, stop=True)
                        mm = pe.matmul(p_s[:, 2 + h:3 + h], w1[:, h * P:(h + 1) * P], mean[:, :],
                                       start=True, stop=True)
                    mm.then_inc(s_var, 1)

                @block.vector
                def _(dve):
                    ch = Chain(dve, s_step)
                    dve.tensor_scalar(mean[:, :], p_gram[:, D:D + 1], 1.0 / N, None, ALU.mult).then_inc(s_mean, 1)
                    dve.wait_ge(s_row, 1)
                    dve.tensor_copy(mean_row[:, :], p_row[0:1, 0:P]).then_inc(s_rowc, 1)
                    dve.tensor_scalar(neg_row[:, :], p_row[0:1, 0:P], -1.0, None, ALU.mult).then_inc(s_rowc, 1)
                    ch.step(dve.tensor_scalar(cov[:, :], p_gram[:, 0:D], 1.0 / N, None, ALU.mult))
                    dve.wait_ge(s_outer, 1)
                    dve.tensor_tensor(cov[:, :], cov[:, :], p_s[:, 0:D], ALU.add).then_inc(s_cov, 1)
                    dve.wait_ge(s_cw, 1)
                    dve.tensor_tensor(wc[:, :], w1[:, :], p_row[:, 0:H], ALU.mult).then_inc(s_wc, 1)
                    dve.wait_ge(s_var, 1)
                    ch.step(dve.tensor_copy(mean1[:, :], p_s[:, 2:4]))
                    dve.tensor_scalar(var1[:, :], p_s[:, 0:2], BN_EPS, None, ALU.add).then_inc(s_std, 1)
                    dve.wait_ge(s_sq, 1)
                    ch.step(dve.reciprocal(var1[:, :], var1[:, :]))
                    ch.step(dve.tensor_tensor(scale1[:, :], g1c[:, :], var1[:, :], ALU.mult))
                    ch.step(dve.tensor_tensor(mean1[:, :], mean1[:, :], scale1[:, :], ALU.mult))
                    ch.step(dve.tensor_tensor(shift1[:, :], b1c[:, :], mean1[:, :], ALU.subtract))

                @block.scalar
                def _(act):
                    act.wait_ge(s_std, 1)
                    act.activation(var1[:, :], var1[:, :], ACT.Sqrt).then_inc(s_sq, 1)

        with ExitStack() as ctx:
            sb, pb, sem = make(ctx)
            zt = [sb(f"zt_in{b}", [P, CN]) for b in range(2)]
            hid = [sb(f"hid{b}", [P, 2, CN]) for b in range(2)]
            y = [sb(f"y{b}", [P, CN]) for b in range(2)]
            stats = sb("stats", [P, NC, 6])
            p_h = [[pb(f"p_h{b}{h}") for h in range(2)] for b in range(2)]
            p_y = [pb(f"p_y{b}") for b in range(2)]
            t_load = [sem(f"zt_loaded{b}") for b in range(2)]
            h_prod = sem("hidden_product")
            h_ready = sem("hidden_ready")
            y_prod = sem("y_product")
            y_copied = sem("y_copied")
            y_store = [sem(f"y_stored{b}") for b in range(2)]
            with nc.Block() as block:
                @block.sync
                def _(sp):
                    def rounds(k):
                        for b in range(2):
                            wait_reuse(sp, h_prod, k * 2)
                            sp.dma_start(zt[b][:, :],
                                         zt_dram[bass.ds(k * 2 + b, 1), :, :].rearrange("a p n -> (a p) n"))\
                                .then_inc(t_load[b], 16)

                    rounds(0)
                    with sp.Fori(1, NC // 2) as k:
                        rounds(k)

                @block.gpsimd
                def _(pool):
                    def rounds(k):
                        for b in range(2):
                            pool.wait_ge(y_copied, k * 2 + b + 1)
                            pool.dma_start(zt_dram[bass.ds(k * 2 + b, 1), :, :].rearrange("a p n -> (a p) n"),
                                           y[b][:, :]).then_inc(y_store[b], 16)

                    rounds(0)
                    with pool.Fori(1, NC // 2) as k:
                        rounds(k)
                    for b in range(2):
                        pool.wait_ge(y_store[b], 16 * (NC // 2))

                @block.tensor
                def _(pe):
                    def up(b, n):
                        pe.wait_ge(t_load[b], (n + 1) * 16)
                        wait_reuse(pe, h_ready, n * 2)
                        for h in range(2):
                            mm = pe.matmul(p_h[b][h][:, 0:CN], w1[:, h * P:(h + 1) * P], zt[b][:, :],
                                           start=True, stop=True)
                        mm.then_inc(h_prod, 1)

                    def down(b, n):
                        pe.wait_ge(h_ready, n * 2 + b + 1)
                        wait_reuse(pe, y_copied, n * 2)
                        for h in range(2):
                            mm = pe.matmul(p_y[b][:, 0:CN], w2[:, h, :], hid[b][:, h, :],
                                           start=(h == 0), stop=(h == 1))
                        mm.then_inc(y_prod, 1)

                    up(0, 0)
                    def rounds(k):
                        up(1, k)
                        down(0, k)
                        up(0, k + 1)
                        down(1, k)

                    rounds(0)
                    with pe.Fori(1, NC // 2 - 1) as k:
                        rounds(k)
                    up(1, NC // 2 - 1)
                    down(0, NC // 2 - 1)
                    down(1, NC // 2 - 1)

                @block.scalar
                def _(act):
                    def rounds(k):
                        for b in range(2):
                            act.wait_ge(h_prod, k * 2 + b + 1)
                            wait_reuse(act, y_prod, k * 2)
                            for h in range(2):
                                ins = act.activation(hid[b][:, h, :], p_h[b][h][:, 0:CN], ACT.Relu,
                                                     bias=shift1[:, h:h + 1], scale=scale1[:, h:h + 1])
                            ins.then_inc(h_ready, 1)

                    rounds(0)
                    with act.Fori(1, NC // 2) as k:
                        rounds(k)

                @block.vector
                def _(dve):
                    def rounds(k):
                        for b in range(2):
                            dve.wait_ge(y_prod, k * 2 + b + 1)
                            dve.bn_stats(stats[:, bass.ds(k * 2 + b, 1), :].rearrange("p a n -> p (a n)"),
                                         p_y[b][:, 0:CN])
                            wait_reuse(dve, y_store[b], k * 16)
                            dve.tensor_copy(y[b][:, :], p_y[b][:, 0:CN]).then_inc(y_copied, 1)

                    rounds(0)
                    with dve.Fori(1, NC // 2) as k:
                        rounds(k)

            mv = sb("mv", [P, 2])
            s_agg, s_std, s_sq = sem("moments2"), sem("variance2"), sem("std2")
            s_step = sem("bn2_dve_step")
            with nc.Block() as block:
                @block.vector
                def _(dve):
                    ch = Chain(dve, s_step)
                    ch.step(dve.bn_aggr(mv[:, :], stats[:, :, :].rearrange("p a n -> p (a n)")))
                    dve.tensor_scalar(mv[:, 1:2], mv[:, 1:2], BN_EPS, None, ALU.add).then_inc(s_std, 1)
                    dve.wait_ge(s_sq, 1)
                    ch.step(dve.reciprocal(mv[:, 1:2], mv[:, 1:2]))
                    ch.step(dve.tensor_tensor(scale2[:, :], g2c[:, :], mv[:, 1:2], ALU.mult))
                    ch.step(dve.tensor_tensor(mv[:, 0:1], mv[:, 0:1], scale2[:, :], ALU.mult))
                    ch.step(dve.tensor_tensor(shift2[:, :], b2c[:, :], mv[:, 0:1], ALU.subtract))

                @block.scalar
                def _(act):
                    act.wait_ge(s_std, 1)
                    act.activation(mv[:, 1:2], mv[:, 1:2], ACT.Sqrt).then_inc(s_sq, 1)

        class Norm:

            def __init__(self, tag, sb, sem, out_tiles):
                self.u = [sb(f"{tag}_u{b}", [R, TC, D]) for b in range(2)]
                self.o = [sb(f"{tag}_o{b}", [R, TC, D]) for b in range(2)]
                self.st = [sb(f"{tag}_st{b}", [R, TC, 6]) for b in range(2)]
                self.mv = [sb(f"{tag}_mv{b}", [R, TC, 2]) for b in range(2)]
                self.nb = [sb(f"{tag}_nb{b}", [R, TC]) for b in range(2)]
                self.out_tiles = out_tiles
                self.passed = sem(f"{tag}_wait_passed")
                self.u_ready, self.s_ready = sem(f"{tag}_sum_ready"), sem(f"{tag}_stats_ready")
                self.v_ready, self.q_ready = sem(f"{tag}_variance_ready"), sem(f"{tag}_sqrt_ready")
                self.r_ready, self.f_ready = sem(f"{tag}_rstd_ready"), sem(f"{tag}_factors_ready")
                self.o_ready, self.a_ready = sem(f"{tag}_norm_ready"), sem(f"{tag}_aggregated")
                self.o_store = [sem(f"{tag}_norm_stored{b}") for b in range(2)]

            def moments(self, dve, b, k):
                dve.wait_ge(self.u_ready, k * 2 + b + 1)
                for j in range(TC):
                    ins = dve.bn_stats(self.st[b][:, j, :], self.u[b][:, j, :])
                ins.then_inc(self.s_ready, 1)
                wait_apart(dve, self.s_ready, k * 2 + b + 1, self.passed)
                for j in range(TC):
                    ins = dve.bn_aggr(self.mv[b][:, j, :], self.st[b][:, j, :])
                ins.then_inc(self.a_ready, 1)
                dve.wait_ge(self.a_ready, k * 2 + b + 1)
                dve.tensor_scalar(self.mv[b][:, :, 1:2], self.mv[b][:, :, 1:2], LN_EPS, None, ALU.add)\
                    .then_inc(self.v_ready, 1)

            def factors(self, dve, b, n):
                dve.wait_ge(self.q_ready, n * 2 + b + 1)
                dve.reciprocal(self.mv[b][:, :, 1:2], self.mv[b][:, :, 1:2]).then_inc(self.r_ready, 1)
                dve.wait_ge(self.r_ready, n * 2 + b + 1)
                dve.scalar_tensor_tensor(out=self.nb[b][:, :].unsqueeze(2), in0=self.mv[b][:, :, 0:1], scalar=-1.0,
                                         in1=self.mv[b][:, :, 1:2], op0=ALU.mult, op1=ALU.mult)\
                    .then_inc(self.f_ready, 1)

            def root(self, act, b, n):
                act.wait_ge(self.v_ready, n * 2 + b + 1)
                act.activation(self.mv[b][:, :, 1:2], self.mv[b][:, :, 1:2], ACT.Sqrt).then_inc(self.q_ready, 1)

            def scale(self, act, b, n):
                act.wait_ge(self.f_ready, n * 2 + b + 1)
                wait_reuse(act, self.o_store[b], n * 32)
                for j in range(TC):
                    ins = act.activation(self.o[b][:, j, :], self.u[b][:, j, :], ACT.Identity,
                                         bias=self.nb[b][:, j:j + 1], scale=self.mv[b][:, j, 1:2])
                ins.then_inc(self.o_ready, 1)
                act.wait_ge(self.o_ready, n * 2 + b + 1)
                for lo, hi in split_rows():
                    act.dma_start(self.out_tiles[lo:hi, bass.ds((n * 2 + b) * TC, TC), :], self.o[b][lo:hi, :, :])\
                        .then_inc(self.o_store[b], 16)

            def stored(self, act):
                for b in range(2):
                    act.wait_ge(self.o_store[b], 32 * (NC // 2))

        with ExitStack() as ctx:
            sb, pb, sem = make(ctx)
            yt = [sb(f"yt{b}", [P, CN]) for b in range(2)]
            xs = [sb(f"x2s{b}", [R, TC, D]) for b in range(2)]
            r = [sb(f"r{b}", [P, CN]) for b in range(2)]
            p_r = [pb(f"p_r{b}") for b in range(2)]
            y_load = [sem(f"y_loaded{b}") for b in range(2)]
            x_load = [sem(f"x_loaded{b}") for b in range(2)]
            r_ready, t_done = sem("relu_ready"), sem("relu_transposed")
            norm = Norm("norm0", sb, sem, x1_tiles)
            with nc.Block() as block:
                @block.sync
                def _(sp):
                    def rounds(k):
                        for b in range(2):
                            wait_reuse(sp, r_ready, k * 2)
                            sp.dma_start(yt[b][:, :],
                                         zt_dram[bass.ds(k * 2 + b, 1), :, :].rearrange("a p n -> (a p) n"))\
                                .then_inc(y_load[b], 16)
                            wait_reuse(sp, norm.u_ready, k * 2)
                            for lo, hi in split_rows():
                                sp.dma_start(xs[b][lo:hi, :, :], x_tiles[lo:hi, bass.ds((k * 2 + b) * TC, TC), :])\
                                    .then_inc(x_load[b], 16)

                    rounds(0)
                    with sp.Fori(1, NC // 2) as k:
                        rounds(k)

                @block.scalar
                def _(act):
                    def relu(b, n):
                        act.wait_ge(y_load[b], (n + 1) * 16)
                        wait_reuse(act, t_done, n * 2)
                        act.activation(r[b][:, :], yt[b][:, :], ACT.Relu, bias=shift2[:, 0:1],
                                       scale=scale2[:, 0:1]).then_inc(r_ready, 1)

                    relu(0, 0)
                    def rounds(k):
                        relu(1, k)
                        norm.root(act, 0, k)
                        norm.scale(act, 0, k)
                        relu(0, k + 1)
                        norm.root(act, 1, k)
                        norm.scale(act, 1, k)

                    rounds(0)
                    with act.Fori(1, NC // 2 - 1) as k:
                        rounds(k)
                    last = NC // 2 - 1
                    relu(1, last)
                    for b in range(2):
                        norm.root(act, b, last)
                        norm.scale(act, b, last)
                    norm.stored(act)

                @block.tensor
                def _(pe):
                    def rounds(k):
                        for b in range(2):
                            pe.wait_ge(r_ready, k * 2 + b + 1)
                            wait_reuse(pe, norm.u_ready, k * 2)
                            for j in range(TC):
                                mm = pe.transpose(p_r[b][0:R, j * D:(j + 1) * D], r[b][:, j * R:(j + 1) * R],
                                                  ident[:, :])
                            mm.then_inc(t_done, 1)

                    rounds(0)
                    with pe.Fori(1, NC // 2) as k:
                        rounds(k)

                @block.vector
                def _(dve):
                    def rounds(k):
                        for b in range(2):
                            dve.wait_ge(x_load[b], (k + 1) * 32)
                            dve.wait_ge(t_done, k * 2 + b + 1)
                            wait_reuse(dve, norm.o_ready, k * 2)
                            dve.scalar_tensor_tensor(
                                out=norm.u[b][:, :, :], in0=xs[b][:, :, :], scalar=2.0,
                                in1=p_r[b][0:R, :].rearrange("p (j d) -> p j d", d=D),
                                op0=ALU.mult, op1=ALU.add).then_inc(norm.u_ready, 1)
                            norm.moments(dve, b, k)
                            norm.factors(dve, b, k)

                    rounds(0)
                    with dve.Fori(1, NC // 2) as k:
                        rounds(k)

        with ExitStack() as ctx:
            sb, pb, sem = make(ctx)
            xg = [sb(f"x1g{b}", [R, TC, D]) for b in range(2)]
            idx = [sb(f"idx1{b}", [R, TC], I32) for b in range(2)]
            h2 = sb("h2_in", [P, CN])
            xt = [sb(f"xt{b}", [P, CN]) for b in range(2)]
            wq = [[sb(f"wq{b}{q}", [P, CN]) for q in range(2)] for b in range(2)]
            m = [[sb(f"m{b}{q}", [P, CN]) for q in range(2)] for b in range(2)]
            rv = [sb(f"rv{b}", [R, TC, MUL, 3]) for b in range(2)]
            gs = [sb(f"gs{b}", [R, TC, MUL, 3]) for b in range(2)]
            gr = [sb(f"gr{b}", [R, TC, MUL]) for b in range(2)]
            mo = [sb(f"mo1{b}", [R, TC, MW]) for b in range(2)]
            p_xt, p_up = pb("p_xt"), pb("p_up")
            p_w = [pb(f"p_w{q}") for q in range(2)]
            p_o = [[pb(f"p_o{b}{q}") for q in range(2)] for b in range(2)]
            g_done = [sem(f"x1_gathered{b}") for b in range(2)]
            i_ready = [sem(f"index1_ready{b}") for b in range(2)]
            i_passed = sem("index1_wait_passed")
            h_load = sem("h2_loaded")
            t_done, t_copied = sem("x1_transposed"), sem("x1_transpose_copied")
            u_done, w_done = sem("up_product"), sem("path_weights_product")
            w_copied = sem("path_weights_ready")
            m_ready = sem("paths_ready")
            o_done = sem("out_product")
            c1, c2, c3 = sem("direction_products"), sem("direction_sums"), sem("messages1_ready")
            b_blank = sem("messages1_blanked")
            m_dst = sem("destination1_written")
            m_store = [sem(f"messages1_stored{b}") for b in range(2)]
            with nc.Block() as block:
                @block.gpsimd
                def _(pool):
                    for b in range(2):
                        pool.memset(mo[b][:, :, :], 0.0).then_inc(b_blank, 1)
                    def rounds(k):
                        for b in range(2):
                            wait_reuse(pool, g_done[b], k * (16 * TC))
                            wait_reuse(pool, t_done, k * 2)
                            pool.tensor_copy(idx[b][:, :], src_all[:, bass.ds(k * (2 * TC) + b * TC, TC)])\
                                .then_inc(i_ready[b], 1)
                            wait_apart(pool, i_ready[b], k + 1, i_passed)
                            for j in range(TC):
                                pool.indirect_dma_start(
                                    out=xg[b][:, j, :], out_offset=None, in_=x1_dram,
                                    in_offset=bass.IndirectOffsetOnAxis(ap=idx[b][:, j:j + 1], axis=0),
                                    bounds_check=N - 1, oob_is_err=False).then_inc(g_done[b], 16)

                    rounds(0)
                    with pool.Fori(1, EC // 2) as k:
                        rounds(k)

                @block.sync
                def _(sp):
                    sp.dma_start(h2[:, :], h2_dram[0, :, :]).then_inc(h_load, 16)
                    def store(b, n):
                        sp.wait_ge(c3, n * 2 + b + 1)
                        sp.wait_ge(m_dst, n * 2 + b + 1)
                        for lo, hi in split_rows():
                            sp.dma_start(msg_rows[lo:hi, bass.ds(n * (2 * TC) + b * TC, TC), :], mo[b][lo:hi, :, :])\
                                .then_inc(m_store[b], 16)
                    def rounds(k):
                        sp.wait_ge(w_done, k * 2 + 2)
                        sp.dma_start(h2[:, :], h2_dram[bass.ds(k + 1, 1), :, :].rearrange("a p n -> (a p) n"))\
                            .then_inc(h_load, 16)
                        store(0, k)
                        store(1, k)

                    rounds(0)
                    with sp.Fori(1, EC // 2 - 1) as k:
                        rounds(k)
                    store(0, EC // 2 - 1)
                    store(1, EC // 2 - 1)
                    for b in range(2):
                        sp.wait_ge(m_store[b], 32 * (EC // 2))

                @block.tensor
                def _(pe):
                    def paths(b, n):
                        pe.wait_ge(g_done[b], (n + 1) * (16 * TC))
                        wait_reuse(pe, t_copied, n * 2 + b)
                        for j in range(TC):
                            mm = pe.transpose(p_xt[:, j * R:(j + 1) * R], xg[b][:, j, :], ident[0:R, 0:R])
                        mm.then_inc(t_done, 1)
                        pe.wait_ge(h_load, (n + 1) * 16)
                        wait_reuse(pe, w_copied, n * 2 + b)
                        for q in range(2):
                            mm = pe.matmul(p_w[q][:, 0:CN], w_mlp2[:, b, q, :], h2[:, :], start=True, stop=True)
                        mm.then_inc(w_done, 1)
                        pe.wait_ge(t_copied, n * 2 + b + 1)
                        wait_reuse(pe, m_ready, n * 2 + b)
                        pe.matmul(p_up[:, 0:CN], w_up[:, :], xt[b][:, :], start=True, stop=True).then_inc(u_done, 1)

                    def outputs(b, n):
                        pe.wait_ge(m_ready, n * 2 + b + 1)
                        wait_reuse(pe, c3, n * 2)
                        for q, w in ((0, w_outA), (1, w_outB)):
                            for j in range(TC):
                                mm = pe.matmul(p_o[b][q][0:R, j * D:(j + 1) * D], m[b][q][:, j * R:(j + 1) * R],
                                               w[:, :], start=True, stop=True)
                        mm.then_inc(o_done, 1)

                    paths(0, 0)
                    def rounds(k):
                        paths(1, k)
                        outputs(0, k)
                        paths(0, k + 1)
                        outputs(1, k)

                    rounds(0)
                    with pe.Fori(1, EC // 2 - 1) as k:
                        rounds(k)
                    paths(1, EC // 2 - 1)
                    outputs(0, EC // 2 - 1)
                    outputs(1, EC // 2 - 1)

                @block.scalar
                def _(act):
                    def rounds(k):
                        for b in range(2):
                            act.wait_ge(t_done, k * 2 + b + 1)
                            wait_reuse(act, u_done, k * 2)
                            act.activation(xt[b][:, :], p_xt[:, 0:CN], ACT.Copy).then_inc(t_copied, 1)
                            act.wait_ge(w_done, k * 2 + b + 1)
                            wait_reuse(act, m_ready, k * 2)
                            for q in range(2):
                                ins = act.activation(wq[b][q][:, :], p_w[q][:, 0:CN], ACT.Identity,
                                                     bias=b_mlp2[:, q:q + 1])
                            ins.then_inc(w_copied, 1)

                    rounds(0)
                    with act.Fori(1, EC // 2) as k:
                        rounds(k)

                @block.vector
                def _(dve):
                    def products(b, n):
                        dve.wait_ge(u_done, n * 2 + b + 1)
                        dve.wait_ge(w_copied, n * 2 + b + 1)
                        wait_reuse(dve, o_done, n * 2)
                        for q in range(2):
                            ins = dve.tensor_tensor(m[b][q][:, :], p_up[:, 0:CN], wq[b][q][:, :], ALU.mult)
                        ins.then_inc(m_ready, 1)

                    def combine(b, n):
                        full = [R, TC, MUL, 3]
                        rh = rhat[:, bass.ds(n * (2 * TC) + b * TC, TC), :].unsqueeze(2).to_broadcast(full)
                        oA = p_o[b][0][0:R, :].rearrange("p (j d) -> p j d", d=D)
                        oB = p_o[b][1][0:R, :].rearrange("p (j d) -> p j d", d=D)
                        dve.wait_ge(o_done, n * 2 + b + 1)
                        wait_reuse(dve, c3, n * 2 + b)
                        dve.tensor_tensor(rv[b][:, :, :, :], oB[:, :, 0:MUL].unsqueeze(3).to_broadcast(full), rh,
                                          ALU.mult)
                        dve.tensor_tensor(gs[b][:, :, :, :],
                                          oB[:, :, MUL:D].rearrange("p j (k c) -> p j k c", c=3), rh,
                                          ALU.mult).then_inc(c1, 1)
                        dve.wait_ge(c1, n * 2 + b + 1)
                        dve.tensor_reduce(gr[b][:, :, :], gs[b][:, :, :, :], AX_X, ALU.add).then_inc(c2, 1)
                        wait_reuse(dve, m_store[b], n * 32)
                        dve.wait_ge(b_blank, 2)
                        dve.tensor_tensor(mo[b][:, :, MUL:D].rearrange("p j (k c) -> p j k c", c=3),
                                          oA[:, :, MUL:D].rearrange("p j (k c) -> p j k c", c=3),
                                          rv[b][:, :, :, :], ALU.add)
                        dve.tensor_copy(mo[b][:, :, D:D + 1],
                                        dst_f[:, bass.ds(n * (2 * TC) + b * TC, TC)].unsqueeze(2)).then_inc(m_dst, 1)
                        dve.wait_ge(c2, n * 2 + b + 1)
                        dve.tensor_tensor(mo[b][:, :, 0:MUL], oA[:, :, 0:MUL], gr[b][:, :, :], ALU.add)\
                            .then_inc(c3, 1)

                    products(0, 0)
                    def rounds(k):
                        products(1, k)
                        combine(0, k)
                        products(0, k + 1)
                        combine(1, k)

                    rounds(0)
                    with dve.Fori(1, EC // 2 - 1) as k:
                        rounds(k)
                    products(1, EC // 2 - 1)
                    combine(0, EC // 2 - 1)
                    combine(1, EC // 2 - 1)

        slow_path(1)

        with ExitStack() as ctx:
            sb, pb, sem = make(ctx)
            xs = [sb(f"x3s{b}", [R, TC, D]) for b in range(2)]
            ax = [sb(f"ax1{b}", [R, TC, D]) for b in range(2)]
            win = [sb(f"win1{b}", [P, TC, MW]) for b in range(2)]
            local = [sb(f"local1{b}", [P, TC]) for b in range(2)]
            hot = [sb(f"hot1{b}", [P, TC, R]) for b in range(2)]
            p_agg = [pb(f"p_agg1{b}") for b in range(2)]
            x_load = [sem(f"x1_loaded{b}") for b in range(2)]
            s_load = [sem(f"ax1_loaded{b}") for b in range(2)]
            w_load = [sem(f"windows1_loaded{b}") for b in range(2)]
            l_ready, l_passed = sem("local1_ready"), sem("local1_wait_passed")
            o_ready, a_done = sem("one_hot1_ready"), sem("messages1_added")
            norm = Norm("norm1", sb, sem, out_tiles)
            with nc.Block() as block:
                @block.sync
                def _(sp):
                    def program(slow):
                        def rounds(k):
                            for b in range(2):
                                wait_reuse(sp, norm.u_ready, k * 2)
                                for lo, hi in split_rows():
                                    sp.dma_start(xs[b][lo:hi, :, :], x1_tiles[lo:hi, bass.ds((k * 2 + b) * TC, TC), :])\
                                        .then_inc(x_load[b], 16)
                                if slow:
                                    for lo, hi in split_rows():
                                        sp.dma_start(ax[b][lo:hi, :, :],
                                                     agg_tiles[lo:hi, bass.ds((k * 2 + b) * TC, TC), :])\
                                            .then_inc(s_load[b], 16)
                                windows(sp, win, w_load, k, b)

                        rounds(0)
                        with sp.Fori(1, NC // 2) as k:
                            rounds(k)

                    either(sp, program)

                @block.gpsimd
                def _(pool):
                    def rounds(k):
                        for b in range(2):
                            pool.wait_ge(w_load[b], (k + 1) * (16 * TC))
                            wait_reuse(pool, o_ready, k * 2)
                            pool.tensor_tensor(local[b][:, :].unsqueeze(2), win[b][:, :, D:D + 1],
                                               tile_base[:, bass.ds((k * 2 + b) * TC, TC)].unsqueeze(2),
                                               ALU.subtract).then_inc(l_ready, 1)
                            wait_reuse(pool, a_done, k * 2)
                            wait_apart(pool, l_ready, k * 2 + b + 1, l_passed)
                            one_hot(pool, hot, local, b).then_inc(o_ready, 1)

                    rounds(0)
                    with pool.Fori(1, NC // 2) as k:
                        rounds(k)

                @block.tensor
                def _(pe):
                    def rounds(k):
                        for b in range(2):
                            pe.wait_ge(o_ready, k * 2 + b + 1)
                            wait_reuse(pe, norm.u_ready, k * 2)
                            for j in range(TC):
                                mm = pe.matmul(p_agg[b][0:R, j * D:(j + 1) * D], hot[b][:, j, :],
                                               win[b][:, j, 0:D], start=True, stop=True)
                            mm.then_inc(a_done, 1)

                    rounds(0)
                    with pe.Fori(1, NC // 2) as k:
                        rounds(k)

                @block.vector
                def _(dve):
                    def program(slow):
                        def rounds(k):
                            for b in range(2):
                                dve.wait_ge(x_load[b], (k + 1) * 32)
                                dve.wait_ge(a_done, k * 2 + b + 1)
                                if slow:
                                    dve.wait_ge(s_load[b], (k + 1) * 32)
                                wait_reuse(dve, norm.o_ready, k * 2)
                                dve.tensor_tensor(norm.u[b][:, :, :], xs[b][:, :, :],
                                                  ax[b][:, :, :] if slow else p_agg[b][0:R, :].rearrange("p (j d) -> p j d", d=D), ALU.add)\
                                    .then_inc(norm.u_ready, 1)
                                norm.moments(dve, b, k)
                                norm.factors(dve, b, k)

                        rounds(0)
                        with dve.Fori(1, NC // 2) as k:
                            rounds(k)

                    either(dve, program)

                @block.scalar
                def _(act):
                    def rounds(k):
                        for b in range(2):
                            norm.root(act, b, k)
                            norm.scale(act, b, k)

                    rounds(0)
                    with act.Fori(1, NC // 2) as k:
                        rounds(k)
                    norm.stored(act)


_INS = ["x", "src", "dst", "edge_attr_128", "edge_attr_3", "edge_weight", "L0_gnn_eps", "L0_gnn_W1", "L0_gnn_g1",
        "L0_gnn_b1", "L0_gnn_W2", "L0_gnn_g2", "L0_gnn_b2", "L1_gnn_W_up0", "L1_gnn_W_up1", "L1_gnn_mlp_w0",
        "L1_gnn_mlp_b0", "L1_gnn_mlp_w1", "L1_gnn_mlp_b1", "L1_gnn_mlp_w2", "L1_gnn_mlp_b2", "L1_gnn_W_out0",
        "L1_gnn_W_out1"]


def kernel(**inputs):
    import numpy as _np
    import concourse.bacc as _bacc
    from concourse import mybir as _mybir
    from concourse.bass_utils import run_bass_kernel_spmd as _run

    nc = _bacc.Bacc("TRN2", target_bir_lowering=False, num_devices=1)
    arrays, args = {}, []
    for name in _INS:
        a = _np.ascontiguousarray(inputs[name])
        if a.ndim == 0:
            a = a.reshape(1)
        arrays[f"in_{name}_dram"] = a
        args.append(nc.dram_tensor(f"in_{name}_dram", a.shape, _mybir.dt.from_np(a.dtype), kind="ExternalInput").ap())
    shape = tuple(inputs["x"].shape)
    args.append(nc.dram_tensor("out_0_dram", shape, _mybir.dt.float32, kind="ExternalOutput").ap())
    gnn_kernel(nc, *args)
    r = _run(nc, [arrays], core_ids=[0])
    return r.results[0]["out_0_dram"]
```

```python
from contextlib import ExitStack

import concourse.bass as bass
from concourse import mybir

F32 = mybir.dt.float32
I32 = mybir.dt.int32
ALU = mybir.AluOpType
ACT = mybir.ActivationFunctionType
AX_X = mybir.AxisListType.X

P = 128
R = 125
TC = 4
CN = R * TC
WIN = 128
S = 4
MW = 132
BN_EPS = 1e-5
LN_EPS = 1e-5
NO_ROW = 1 << 24


def split_rows(lo_hi=(0, 112, R)):
    return [(lo_hi[i], lo_hi[i + 1]) for i in range(2)]


def wait_reuse(eng, sem, value):
    if not (isinstance(value, int) and value <= 0):
        eng.wait_ge(sem, value)


def run(eng, total, *stages):
    rounds = total // S

    def step(n, b, at):
        for lag, f in stages:
            m, c = (n, b - lag) if b >= lag else (n - 1, b - lag + S)
            if at is None or 0 <= at - lag < total:
                f(m, c)

    for at in range(S):
        step(0, at, at)
    if rounds > 1:
        with eng.Fori(1, rounds) as n:
            for b in range(S):
                step(n, b, None)
    for at in range(rounds * S, total + max(lag for lag, _ in stages)):
        step(at // S, at % S, at)


def wait_apart(eng, sem, value, passed):
    eng.wait_ge(sem, value)
    eng.sem_inc(passed, 1)


class Chain:

    def __init__(self, eng, sem):
        self.eng, self.sem, self.n = eng, sem, 0

    def step(self, ins):
        self.n += 1
        ins.then_inc(self.sem, 1)
        self.eng.wait_ge(self.sem, self.n)


def gnn_kernel(nc, x, src, dst, edge_attr_128, edge_attr_3, edge_weight, eps, W1, g1, b1, W2, g2, b2,
               W_up0, W_up1, mlp_w0, mlp_b0, mlp_w1, mlp_b1, mlp_w2, mlp_b2, W_out0, W_out1, out):
    N, D = x.shape
    E = src.shape[0]
    H = W1.shape[1]
    MUL = W_up0.shape[0]
    NB, HM = mlp_w0.shape
    NT, ET = N // R, E // R
    NC, EC = NT // TC, ET // TC
    FINE = next(f for f in range(int(NT ** 0.5), 0, -1) if NT % f == 0)
    COARSE = NT // FINE
    assert D == P and H == 2 * P and NT * R == N and ET * R == E and HM == 64 and NB == 8 and MUL == 32
    assert NC * TC == NT and EC * TC == ET and NC % S == 0 and EC % 2 == 0 and COARSE <= 64

    msg = nc.dram_tensor("msg_rows", (E + WIN, MW), F32, kind="Internal").ap()
    zt_dram = nc.dram_tensor("z_transposed", (NC, P, CN), F32, kind="Internal").ap()
    x1_dram = nc.dram_tensor("x_after_layer0", (N, D), F32, kind="Internal").ap()
    h2_dram = nc.dram_tensor("radial_hidden", (EC // 2, P, CN), F32, kind="Internal").ap()

    first_dram = nc.dram_tensor("first_edges", (COARSE, FINE), F32, kind="Internal").ap()
    agg = nc.dram_tensor("slow_path_sums", (N, D), F32, kind="Internal").ap()
    agg_tiles = agg.rearrange("(t p) d -> p t d", p=R)
    x_tiles = x.rearrange("(t p) d -> p t d", p=R)
    x1_tiles = x1_dram.rearrange("(t p) d -> p t d", p=R)
    out_tiles = out.rearrange("(t p) d -> p t d", p=R)
    ea_rows = edge_attr_128.rearrange("(p j) d -> p j d", j=ET)
    msg_rows = msg[0:E, :].rearrange("(p j) d -> p j d", j=ET)

    root = ExitStack()
    with root:
        def make(ctx):
            def sb(name, shape, dt=F32):
                return ctx.enter_context(nc.sbuf_tensor(name, shape, dt))

            def pb(name, shape=(P, 512)):
                return ctx.enter_context(nc.psum_tensor(name, list(shape), F32))

            def sem(name):
                return ctx.enter_context(nc.semaphore(name))
            return sb, pb, sem

        def phase(ctx):
            sb, pb, _ = make(ctx)
            taken = []

            def sem(name):
                taken.append(nc.alloc_semaphore(name))
                return taken[-1]

            def clear():
                nc.clear_and_free_semaphores(taken)
                nc.all_engine_barrier()

            ctx.callback(clear)
            return sb, pb, sem

        sb, pb, sem = make(root)

        ident = sb("ident", [P, P])
        ones = sb("ones", [P, P])
        node_iota = sb("node_iota", [P, R])
        tile_base = sb("tile_base", [P, NT])
        src_all = sb("src_all", [R, ET], I32)
        dst_f = sb("dst_f", [R, ET])
        rhat = sb("rhat", [R, ET, 3])
        emb = sb("emb", [R, ET, NB])
        eps1 = sb("eps1", [P, 1])
        w1 = sb("w1", [P, H])
        w2 = sb("w2", [P, 2, D])
        g1c, b1c = sb("g1c", [P, 2]), sb("b1c", [P, 2])
        g2c, b2c = sb("g2c", [P, 1]), sb("b2c", [P, 1])
        scale1, shift1 = sb("scale1", [P, 2]), sb("shift1", [P, 2])
        scale2, shift2 = sb("scale2", [P, 1]), sb("shift2", [P, 1])
        w_up = sb("w_up", [P, P])
        w_mlp0 = sb("w_mlp0", [64, 4, P])
        w_mlp1 = sb("w_mlp1", [P, P])
        w_mlp2 = sb("w_mlp2", [P, 2, 2, P])
        b_mlp0, b_mlp1, b_mlp2 = sb("b_mlp0", [P, 1]), sb("b_mlp1", [P, 1]), sb("b_mlp2", [P, 2])
        w_outA, w_outB = sb("w_outA", [P, P]), sb("w_outB", [P, P])
        starts = sb("starts", [1, NT], I32)
        slow_i = sb("slow_i", [1, 1], I32)
        unsorted = sb("unsorted", [R, 1])

        with ExitStack() as ctx:
            sb, pb, sem = phase(ctx)
            dst_i = sb("dst_i", [R, ET], I32)
            next_i = sb("next_i", [R, ET], I32)
            next_f = sb("next_f", [R, ET])
            base_i = sb("base_i", [P, NT], I32)
            iota_i = sb("iota_i", [P, R], I32)
            k_i = sb("k_i", [R, NB], I32)
            k_f = sb("k_f", [R, NB])
            ew = sb("ew", [R, ET])
            xc = sb("xc", [R, ET])
            mask = sb("mask", [R, ET])
            ea3 = sb("ea3", [R, ET, 3])
            sq3 = sb("sq3", [R, ET, 3])
            nrm = sb("nrm", [R, ET])
            eps_in = sb("eps_in", [1, 1])
            tmpA, tmpB = sb("tmpA", [P, MUL]), sb("tmpB", [P, MUL])
            pad = sb("pad", [WIN, MW])
            p_eps = pb("p_eps")
            s_load = sem("inputs_loaded")
            s_blank = sem("tiles_blanked")
            s_wload = sem("weights_loaded")
            s_iota = sem("iotas_done")
            s_pool = sem("pool_step")
            s_ones = sem("ones_ready")
            s_pad = sem("pad_ready")
            s_padst = sem("pad_stored")
            s_epsmm = sem("eps_broadcast")
            s_dve = sem("dve_step")
            s_sqn = sem("norm_squared")
            s_nrm = sem("norm_ready")
            s_embx = sem("exponent_ready")
            s_embe = sem("exp_done")
            s_next = sem("next_blanked")
            with nc.Block() as block:
                n_loads = 14

                @block.sync
                def _(sp):
                    def load(dst_ap, src_ap, s):
                        sp.dma_start(dst_ap, src_ap, allow_slow_non_contiguous=True).then_inc(s, 16)

                    load(dst_i[:, :], dst.rearrange("(p j) -> p j", j=ET), s_load)
                    sp.wait_ge(s_next, 1)
                    load(next_i[0:R - 1, :], dst[1:1 + (R - 1) * ET].rearrange("(p j) -> p j", j=ET), s_load)
                    load(next_i[R - 1:R, 0:ET - 1], dst[1 + (R - 1) * ET:E].rearrange("(p j) -> p j", p=1), s_load)
                    load(src_all[:, :], src.rearrange("(p j) -> p j", j=ET), s_load)
                    load(ew[:, :], edge_weight.rearrange("(p j) -> p j", j=ET), s_load)
                    load(ea3[:, :, :], edge_attr_3.rearrange("(p j) c -> p j c", j=ET), s_load)
                    load(eps_in[:, :], eps.rearrange("(a b) -> a b", a=1), s_load)
                    load(w1[:, :], W1, s_load)
                    load(w2[:, :, :], W2.rearrange("(h p) d -> p h d", p=P), s_load)
                    load(g1c[:, :], g1.rearrange("(h p) -> p h", p=P), s_load)
                    load(b1c[:, :], b1.rearrange("(h p) -> p h", p=P), s_load)
                    load(g2c[:, :], g2.rearrange("(p a) -> p a", a=1), s_load)
                    load(b2c[:, :], b2.rearrange("(p a) -> p a", a=1), s_load)
                    load(b_mlp2[0:MUL, 0:1], mlp_b2[0:MUL].rearrange("(p a) -> p a", a=1), s_load)
                    sp.wait_ge(s_blank, 8)
                    n = 0
                    load(w_up[0:MUL, 0:MUL], W_up0, s_wload)
                    for c in range(3):
                        load(w_up[MUL + c:P:3, MUL * (c + 1):MUL * (c + 2)], W_up1, s_wload)
                    for v in range(4):
                        load(w_mlp0[NB * v:NB * v + NB, v, 0:HM], mlp_w0, s_wload)
                        load(w_mlp0[NB * (v + 4):NB * (v + 5), v, HM:P], mlp_w0, s_wload)
                    for h in range(2):
                        rows = slice(HM * h, HM * h + HM)
                        load(w_mlp1[rows, HM * h:HM * h + HM], mlp_w1, s_wload)
                        load(b_mlp0[rows, :], mlp_b0.rearrange("(p a) -> p a", a=1), s_wload)
                        load(b_mlp1[rows, :], mlp_b1.rearrange("(p a) -> p a", a=1), s_wload)
                        for q in range(2):
                            load(w_mlp2[rows, h, q, 0:MUL], mlp_w2[:, MUL * q:MUL * (q + 1)], s_wload)
                            for c in range(3):
                                load(w_mlp2[rows, h, q, MUL * (c + 1):MUL * (c + 2)],
                                     mlp_w2[:, MUL * (q + 2):MUL * (q + 3)], s_wload)
                    for q in range(2):
                        if q:
                            load(b_mlp2[0:MUL, 1:2], mlp_b2[MUL:2 * MUL].rearrange("(p a) -> p a", a=1), s_wload)
                        for c in range(3):
                            load(b_mlp2[MUL * (c + 1):MUL * (c + 2), q:q + 1],
                                 mlp_b2[MUL * (q + 2):MUL * (q + 3)].rearrange("(p a) -> p a", a=1), s_wload)
                    load(w_outA[0:MUL, 0:MUL], W_out0[0:MUL, :], s_wload)
                    load(w_outB[0:MUL, 0:MUL], W_out1[0:MUL, :], s_wload)
                    for c in range(3):
                        load(tmpA[MUL * (c + 1):MUL * (c + 2), :], W_out1[MUL:2 * MUL, :], s_wload)
                        load(tmpB[MUL * (c + 1):MUL * (c + 2), :], W_out0[MUL:2 * MUL, :], s_wload)
                    sp.wait_ge(s_pad, 2)
                    sp.dma_start(msg[E:E + WIN, :], pad[:, :]).then_inc(s_padst, 16)
                    sp.wait_ge(s_padst, 16)

                n_wload = 1 + 3 + 8 + 2 * (3 + 8) + 7 + 2 + 6

                @block.gpsimd
                def _(pool):
                    pool.memset(ident[:, :], 0.0).then_inc(s_pool, 1)
                    pool.wait_ge(s_pool, 1)
                    pool.affine_select(out=ident[:, :], in_=ident[:, :], compare_op=ALU.not_equal, fill=1.0,
                                       base=0, pattern=[[-1, P]], channel_multiplier=1)
                    pool.iota(iota_i[:, :], [[1, R]], base=0, channel_multiplier=0).then_inc(s_iota, 1)
                    pool.iota(base_i[:, :], [[R, NT]], base=0, channel_multiplier=0).then_inc(s_iota, 1)
                    pool.iota(k_i[:, :], [[1, NB]], base=0, channel_multiplier=0).then_inc(s_iota, 1)

                @block.tensor
                def _(pe):
                    pe.wait_ge(s_ones, 1)
                    pe.wait_ge(s_load, 16 * n_loads)
                    pe.matmul(p_eps[:, 0:1], ones[0:1, :], eps_in[:, :], start=True, stop=True).then_inc(s_epsmm, 1)

                @block.scalar
                def _(act):
                    act.wait_ge(s_sqn, 1)
                    act.activation(nrm[:, :], nrm[:, :], ACT.Sqrt).then_inc(s_nrm, 1)
                    act.wait_ge(s_embx, 1)
                    act.activation(emb[:, :, :], emb[:, :, :], ACT.Exp, scale=-0.5).then_inc(s_embe, 1)

                @block.vector
                def _(dve):
                    dve.memset(next_i[:, :], NO_ROW).then_inc(s_next, 1)
                    dve.memset(ones[:, :], 1.0).then_inc(s_ones, 1)
                    for t in (w_up, w_mlp1, w_outA, w_outB):
                        dve.memset(t[:, :], 0.0).then_inc(s_blank, 1)
                    dve.memset(w_mlp0[:, :, :], 0.0).then_inc(s_blank, 1)
                    dve.memset(w_mlp2[:, :, :, :], 0.0).then_inc(s_blank, 1)
                    dve.memset(tmpA[:, :], 0.0).then_inc(s_blank, 1)
                    dve.memset(tmpB[:, :], 0.0).then_inc(s_blank, 1)
                    dve.memset(pad[:, :], 0.0).then_inc(s_pad, 1)
                    dve.wait_ge(s_pad, 1)
                    dve.memset(pad[:, D:D + 1], -1.0).then_inc(s_pad, 1)
                    ch = Chain(dve, s_dve)
                    dve.wait_ge(s_iota, 3)
                    dve.tensor_copy(node_iota[:, :], iota_i[:, :])
                    dve.tensor_copy(tile_base[:, :], base_i[:, :])
                    ch.step(dve.tensor_copy(k_f[:, :], k_i[:, :]))
                    dve.wait_ge(s_load, 16 * n_loads)
                    ch.step(dve.tensor_copy(dst_f[:, :], dst_i[:, :]))
                    ch.step(dve.tensor_copy(next_f[:, :], next_i[:, :]))
                    ch.step(dve.tensor_tensor(next_f[:, :], next_f[:, :], dst_f[:, :], ALU.is_lt))
                    dve.tensor_reduce(unsorted[:, :], next_f[:, :], AX_X, ALU.add)
                    ch.step(dve.tensor_tensor(sq3[:, :, :], ea3[:, :, :], ea3[:, :, :], ALU.mult))
                    dve.tensor_reduce(nrm[:, :], sq3[:, :, :], AX_X, ALU.add).then_inc(s_sqn, 1)
                    ch.step(dve.tensor_scalar(xc[:, :], ew[:, :], 0.0, 1.0, ALU.max, ALU.min))
                    ch.step(dve.tensor_scalar(xc[:, :], xc[:, :], float(NB - 1), None, ALU.mult))
                    ch.step(dve.tensor_scalar(mask[:, :], ew[:, :], 1.0, float(NB) ** 0.5, ALU.is_le, ALU.mult))
                    ch.step(dve.tensor_tensor(emb[:, :, :], xc[:, :].unsqueeze(2).to_broadcast([R, ET, NB]),
                                              k_f[:, :].unsqueeze(1).to_broadcast([R, ET, NB]), ALU.subtract))
                    dve.tensor_tensor(emb[:, :, :], emb[:, :, :], emb[:, :, :], ALU.mult).then_inc(s_embx, 1)
                    dve.wait_ge(s_nrm, 1)
                    ch.step(dve.tensor_scalar(nrm[:, :], nrm[:, :], 1e-12, None, ALU.add))
                    ch.step(dve.reciprocal(nrm[:, :], nrm[:, :]))
                    dve.tensor_tensor(rhat[:, :, :], ea3[:, :, :], nrm[:, :].unsqueeze(2).to_broadcast([R, ET, 3]),
                                      ALU.mult)
                    dve.wait_ge(s_embe, 1)
                    dve.tensor_tensor(emb[:, :, :], emb[:, :, :], mask[:, :].unsqueeze(2).to_broadcast([R, ET, NB]),
                                      ALU.mult)
                    dve.wait_ge(s_epsmm, 1)
                    dve.tensor_scalar(eps1[:, :], p_eps[:, 0:1], 1.0, None, ALU.add)
                    dve.wait_ge(s_wload, 16 * n_wload)
                    dve.tensor_scalar(w_up[:, :], w_up[:, :], float(MUL) ** -0.5, None, ALU.mult)
                    c_out = float(2 * MUL) ** -0.5 / 16.0
                    for w, t, head in ((w_outA, tmpA, c_out), (w_outB, tmpB, c_out * 3.0 ** 0.5)):
                        dve.tensor_scalar(w[0:MUL, 0:MUL], w[0:MUL, 0:MUL], head, None, ALU.mult)
                        for c in range(3):
                            rows = slice(MUL * (c + 1), MUL * (c + 2))
                            dve.tensor_scalar(w[rows, MUL + c:P:3], t[rows, :], c_out, None, ALU.mult)

        with ExitStack() as ctx:
            sb, pb, sem = phase(ctx)
            xg = [sb(f"xg{b}", [R, TC, D]) for b in range(S)]
            ea = [sb(f"ea{h}", [R, 2, TC, D]) for h in range(S // 2)]
            mo = [sb(f"mo{h}", [R, 2, TC, MW]) for h in range(S // 2)]
            idx = [sb(f"idx{b}", [R, TC], I32) for b in range(S)]
            G = 2 * TC
            low = [sb(f"low{h}", [R, G, COARSE + 1]) for h in range(2)]
            inside = [sb(f"inside{h}", [R, G, COARSE]) for h in range(2)]
            over = [sb(f"over{h}", [R, G]) for h in range(2)]
            rest = [sb(f"rest{h}", [R, G]) for h in range(2)]
            fine = [sb(f"fine{h}", [R, G, FINE]) for h in range(2)]
            coarse_at = sb("coarse_at", [P, COARSE + 1])
            first_cf = sb("first_cf", [COARSE, FINE])
            emb_in = [sb(f"emb_in{h}", [R, P]) for h in range(2)]
            emb_t = [sb(f"emb_t{h}", [G * NB, R]) for h in range(2)]
            h1 = [sb(f"h1{h}", [P, CN]) for h in range(2)]
            h2 = [sb(f"h2{h}", [P, CN]) for h in range(2)]
            p_t, p_h1, p_h2, p_cnt = pb("p_t"), pb("p_h1"), pb("p_h2"), pb("p_cnt")
            g_done = [sem(f"rows_gathered{b}") for b in range(S)]
            i_ready, i_passed = sem("index_ready"), sem("index_wait_passed")
            e_load = [sem(f"attr_loaded{h}") for h in range(2)]
            m_sum, m_dst, m_relu = sem("messages_summed"), sem("destination_written"), sem("messages_ready")
            m_store = [sem(f"messages_stored{h}") for h in range(2)]
            k_ready = sem("coarse_bounds_ready")
            c_low, c_in, c_over, c_rest, c_fine = (sem("low_ready"), sem("inside_ready"), sem("over_ready"),
                                                   sem("rest_ready"), sem("fine_ready"))
            c_cnt = sem("counted")
            r_blank, r_in = sem("embedding_tile_blanked"), sem("embedding_copied")
            r_t, r_tc = sem("embedding_transposed"), sem("embedding_transpose_copied")
            r_m0, r_m1 = sem("mlp0_product"), sem("mlp1_product")
            r_h1, r_h2 = sem("hidden1_ready"), sem("hidden2_ready")
            r_store = [sem(f"hidden2_stored{h}") for h in range(2)]
            b_blank = sem("messages_blanked")

            def tiles(n, b):
                return bass.ds((n * S + b) * TC, TC)

            def pair_tiles(n, b):
                return bass.ds((n * S + b) * TC, G)

            with nc.Block() as block:
                @block.gpsimd
                def _(pool):
                    for h in range(2):
                        pool.memset(mo[h][:, :, :, :], 0.0).then_inc(b_blank, 1)

                    def gather(n, b):
                        wait_reuse(pool, m_relu, (n - 1) * S + b + 1)
                        pool.tensor_copy(idx[b][:, :], src_all[:, tiles(n, b)]).then_inc(i_ready, 1)
                        wait_apart(pool, i_ready, n * S + b + 1, i_passed)
                        for j in range(TC):
                            pool.indirect_dma_start(
                                out=xg[b][:, j, :], out_offset=None, in_=x,
                                in_offset=bass.IndirectOffsetOnAxis(ap=idx[b][:, j:j + 1], axis=0),
                                bounds_check=N - 1, oob_is_err=False).then_inc(g_done[b], 16)

                    run(pool, EC, (0, gather))

                @block.sync
                def _(sp):
                    def load(n, b):
                        if b % 2 == 0:
                            wait_reuse(sp, m_sum, (n - 1) * S + b + 2)
                            for lo, hi in split_rows():
                                sp.dma_start(ea[b // 2][lo:hi, :, :, :].rearrange("p a j d -> p (a j) d"),
                                             ea_rows[lo:hi, pair_tiles(n, b), :]).then_inc(e_load[b // 2], 16)

                    run(sp, EC, (0, load))

                @block.scalar
                def _(act):
                    def messages(n, b):
                        act.wait_ge(m_sum, n * S + b + 1)
                        if isinstance(n, int) and n == 0:
                            act.wait_ge(b_blank, 2)
                        wait_reuse(act, m_store[b // 2], n * 32)
                        act.activation(mo[b // 2][:, b % 2, :, 0:D], xg[b][:, :, :], ACT.Relu).then_inc(m_relu, 1)
                        if b % 2:
                            act.wait_ge(m_relu, n * S + b + 1)
                            act.wait_ge(m_dst, n * S + b + 1)
                            for lo, hi in split_rows():
                                act.dma_start(msg_rows[lo:hi, pair_tiles(n, b - 1), :],
                                              mo[b // 2][lo:hi, :, :, :].rearrange("p a j d -> p (a j) d"))\
                                    .then_inc(m_store[b // 2], 16)

                    def embedding(n, b):
                        if b % 2 == 0:
                            act.wait_ge(r_t, n * 2 + b // 2 + 1)
                            wait_reuse(act, r_m0, n * 2 + b // 2 - 1)
                            act.activation(emb_t[b // 2][:, :], p_t[0:G * NB, 0:R], ACT.Copy).then_inc(r_tc, 1)

                    def hidden1(n, b):
                        if b % 2 == 0:
                            act.wait_ge(r_m0, n * 2 + b // 2 + 1)
                            wait_reuse(act, r_m1, n * 2 + b // 2 - 1)
                            act.activation(h1[b // 2][:, :], p_h1[:, 0:CN], ACT.Silu, bias=b_mlp0[:, 0:1])\
                                .then_inc(r_h1, 1)

                    def hidden2(n, b):
                        if b % 2 == 0:
                            act.wait_ge(r_m1, n * 2 + b // 2 + 1)
                            wait_reuse(act, r_store[b // 2], n * 16)
                            act.activation(h2[b // 2][:, :], p_h2[:, 0:CN], ACT.Silu, bias=b_mlp1[:, 0:1])\
                                .then_inc(r_h2, 1)
                            act.wait_ge(r_h2, n * 2 + b // 2 + 1)
                            act.dma_start(h2_dram[bass.ds(n * 2 + b // 2, 1), :, :].rearrange("a p n -> (a p) n"),
                                          h2[b // 2][:, :]).then_inc(r_store[b // 2], 16)

                    run(act, EC, (0, embedding), (1, hidden1), (2, hidden2), (0, messages))
                    for h in range(2):
                        pairs = (EC // 2 - h + 1) // 2
                        act.wait_ge(m_store[h], 32 * pairs)
                        act.wait_ge(r_store[h], 16 * pairs)

                @block.vector
                def _(dve):
                    for h in range(2):
                        dve.memset(emb_in[h][:, :], 0.0).then_inc(r_blank, 1)
                    dve.tensor_copy(coarse_at[:, 0:COARSE], tile_base[:, 0:NT:FINE]).then_inc(k_ready, 1)
                    dve.memset(coarse_at[:, COARSE:COARSE + 1], float(N)).then_inc(k_ready, 1)
                    dve.wait_ge(r_blank, 2)
                    dve.wait_ge(k_ready, 2)

                    def embedding(n, b):
                        if b % 2 == 0:
                            wait_reuse(dve, r_t, n * 2 + b // 2 - 1)
                            dve.tensor_copy(emb_in[b // 2][:, 0:G * NB].rearrange("p (j n) -> p j n", n=NB),
                                            emb[:, pair_tiles(n, b), :]).then_inc(r_in, 1)

                    def count(n, b):
                        if b % 2 == 0:
                            h, i = b // 2, n * 2 + b // 2
                            dst_p = dst_f[:, pair_tiles(n, b)]
                            wait_reuse(dve, c_cnt, i - 1)
                            dve.tensor_tensor(low[h][:, :, :], dst_p.unsqueeze(2).to_broadcast([R, G, COARSE + 1]),
                                              coarse_at[0:R, :].unsqueeze(1).to_broadcast([R, G, COARSE + 1]),
                                              ALU.is_lt).then_inc(c_low, 1)
                            dve.wait_ge(c_low, i + 1)
                            dve.tensor_tensor(inside[h][:, :, :], low[h][:, :, 1:COARSE + 1],
                                              low[h][:, :, 0:COARSE], ALU.subtract).then_inc(c_in, 1)
                            dve.tensor_reduce(over[h][:, :], low[h][:, :, 1:COARSE + 1], AX_X, ALU.add)\
                                .then_inc(c_over, 1)
                            dve.wait_ge(c_over, i + 1)
                            dve.tensor_scalar(over[h][:, :], over[h][:, :], float(R * FINE), float(-R * NT),
                                              ALU.mult, ALU.add).then_inc(c_rest, 1)
                            dve.wait_ge(c_rest, 2 * i + 1)
                            dve.tensor_tensor(rest[h][:, :], dst_p, over[h][:, :], ALU.add).then_inc(c_rest, 1)
                            dve.wait_ge(c_rest, 2 * i + 2)
                            dve.tensor_tensor(fine[h][:, :, :], rest[h][:, :].unsqueeze(2).to_broadcast([R, G, FINE]),
                                              tile_base[0:R, 0:FINE].unsqueeze(1).to_broadcast([R, G, FINE]),
                                              ALU.is_lt).then_inc(c_fine, 1)

                    def messages(n, b):
                        dve.wait_ge(g_done[b], (n + 1) * (16 * TC))
                        dve.wait_ge(e_load[b // 2], (n + 1) * 32)
                        dve.tensor_tensor(xg[b][:, :, :], xg[b][:, :, :], ea[b // 2][:, b % 2, :, :], ALU.add)\
                            .then_inc(m_sum, 1)
                        if isinstance(n, int) and n == 0:
                            dve.wait_ge(b_blank, 2)
                        wait_reuse(dve, m_store[b // 2], n * 32)
                        dve.tensor_copy(mo[b // 2][:, b % 2, :, D:D + 1], dst_f[:, tiles(n, b)].unsqueeze(2))\
                            .then_inc(m_dst, 1)

                    run(dve, EC, (0, embedding), (0, messages), (0, count))

                @block.tensor
                def _(pe):
                    def hidden0(n, b):
                        if b % 2 == 0:
                            h, i = b // 2, n * 2 + b // 2
                            pe.wait_ge(r_in, i + 1)
                            wait_reuse(pe, r_tc, i)
                            pe.transpose(p_t[:, 0:R], emb_in[h][:, :], ident[0:R, 0:R]).then_inc(r_t, 1)
                            pe.wait_ge(r_tc, i + 1)
                            wait_reuse(pe, r_h1, i)
                            for v in range(TC):
                                mm = pe.matmul(p_h1[:, v * R:(v + 1) * R], w_mlp0[:, v, :], emb_t[h][:, :],
                                               start=True, stop=True)
                            mm.then_inc(r_m0, 1)

                    def hidden1(n, b):
                        if b % 2 == 0:
                            h, i = b // 2, n * 2 + b // 2
                            pe.wait_ge(r_h1, i + 1)
                            wait_reuse(pe, r_h2, i)
                            pe.matmul(p_h2[:, 0:CN], w_mlp1[:, :], h1[h][:, :], start=True, stop=True)\
                                .then_inc(r_m1, 1)

                    def count(n, b):
                        if b % 2 == 0:
                            h, i = b // 2, n * 2 + b // 2
                            pe.wait_ge(c_in, i + 1)
                            pe.wait_ge(c_fine, i + 1)
                            for j in range(G):
                                pe.matmul(p_cnt[0:COARSE, 0:FINE], low[h][:, j, 0:COARSE], ones[0:R, 0:FINE],
                                          start=False, stop=False, skip_group_check=True)
                                mm = pe.matmul(p_cnt[0:COARSE, 0:FINE], inside[h][:, j, :], fine[h][:, j, :],
                                               start=False, stop=False, skip_group_check=True)
                            mm.then_inc(c_cnt, 1)

                    pe.wait_ge(r_blank, 1)
                    pe.matmul(p_cnt[0:COARSE, 0:FINE], emb_in[0][:, P - COARSE:P], ones[0:R, 0:FINE], start=True,
                              stop=False, skip_group_check=True)
                    run(pe, EC, (0, hidden0), (1, hidden1), (1, count))

            s_cnt, s_cf, s_out, s_in = sem("unsorted_summed"), sem("counts_copied"), sem("counts_out"), sem("counts_in")
            s_step = sem("tables_step")
            first = sb("first", [1, NT + 1])
            size = sb("size", [1, NT])
            flags = sb("flags", [1, 2])
            with nc.Block() as block:
                @block.tensor
                def _(pe):
                    pe.matmul(p_t[0:1, 0:1], ones[0:R, 0:1], unsorted[:, :], start=True, stop=True)\
                        .then_inc(s_cnt, 1)

                @block.sync
                def _(sp):
                    sp.wait_ge(s_cf, 1)
                    sp.dma_start(first_dram[:, :], first_cf[:, :]).then_inc(s_out, 16)
                    sp.wait_ge(s_out, 16)
                    sp.dma_start(first[:, 0:NT], first_dram.rearrange("(o c) f -> o (c f)", o=1)).then_inc(s_in, 16)

                @block.vector
                def _(dve):
                    ch = Chain(dve, s_step)
                    dve.tensor_copy(first_cf[:, :], p_cnt[0:COARSE, 0:FINE]).then_inc(s_cf, 1)
                    dve.wait_ge(s_cnt, 1)
                    ch.step(dve.memset(first[:, NT:NT + 1], float(E)))
                    ch.step(dve.tensor_scalar(flags[:, 1:2], p_t[0:1, 0:1], 0.0, None, ALU.is_gt))
                    dve.wait_ge(s_in, 16)
                    ch.step(dve.tensor_tensor(size[:, :], first[:, 1:NT + 1], first[:, 0:NT], ALU.subtract))
                    ch.step(dve.tensor_reduce(flags[:, 0:1], size[:, :], AX_X, ALU.max))
                    ch.step(dve.tensor_scalar(flags[:, 0:1], flags[:, 0:1], float(WIN), None, ALU.is_gt))
                    ch.step(dve.tensor_tensor(flags[:, 0:1], flags[:, 0:1], flags[:, 1:2], ALU.max))
                    ch.step(dve.tensor_copy(slow_i[:, :], flags[:, 0:1]))
                    ch.step(dve.tensor_scalar(size[:, :], first[:, 0:NT], -1.0, float(E), ALU.mult, ALU.add))
                    ch.step(dve.scalar_tensor_tensor(out=size[:, :], in0=size[:, :], scalar=flags[:, 0:1],
                                                     in1=first[:, 0:NT], op0=ALU.mult, op1=ALU.add))
                    ch.step(dve.tensor_copy(starts[:, :], size[:, :]))

        def slow_path(layer):
            with ExitStack() as ctx:
                sb, pb, sem = phase(ctx)
                zero = sb(f"slow{layer}_zero", [R, TC, D])
                below = sb(f"slow{layer}_below", [R, R])
                rows = sb(f"slow{layer}_rows", [R, MW])
                dmat = sb(f"slow{layer}_dmat", [R, P])
                same = sb(f"slow{layer}_same", [R, R])
                earlier = sb(f"slow{layer}_earlier", [R, R])
                place = sb(f"slow{layer}_place", [R, 2])
                at = sb(f"slow{layer}_at", [R, 2], I32)
                held = sb(f"slow{layer}_held", [R, D])
                total = sb(f"slow{layer}_total", [R, D])
                p_d, p_s = pb(f"slow{layer}_p_d"), pb(f"slow{layer}_p_s")
                s_blank = sem(f"slow{layer}_blanked")
                s_zero = sem(f"slow{layer}_zeroed")
                s_below = sem(f"slow{layer}_below_ready")
                s_rows = sem(f"slow{layer}_rows_loaded")
                s_dmat, s_dt = sem(f"slow{layer}_dmat_ready"), sem(f"slow{layer}_dmat_transposed")
                s_same, s_sum = sem(f"slow{layer}_same_ready"), sem(f"slow{layer}_summed")
                s_step = sem(f"slow{layer}_dve_step")
                s_at, s_got = sem(f"slow{layer}_index_ready"), sem(f"slow{layer}_held_loaded")
                s_tot, s_put = sem(f"slow{layer}_total_ready"), sem(f"slow{layer}_total_stored")
                s_pass = sem(f"slow{layer}_wait_passed")
                steps = 6

                with nc.Block() as block:
                    @block.sync
                    def _(sp):
                        with sp.If(sp.value_load(slow_i[0:1, 0:1], min_val=0, max_val=1) > 0):
                            sp.wait_ge(s_blank, 1)

                            def blank(k):
                                for lo, hi in split_rows():
                                    sp.dma_start(agg_tiles[lo:hi, bass.ds(k * TC, TC), :], zero[lo:hi, :, :])\
                                        .then_inc(s_zero, 16)

                            with sp.Fori(0, NC) as k:
                                blank(k)

                            def load(t):
                                wait_reuse(sp, s_put, t * 16)
                                sp.dma_start(rows[:, :], msg[bass.ds(t * R, R), :]).then_inc(s_rows, 16)

                            load(0)
                            with sp.Fori(1, ET) as t:
                                load(t)

                    @block.gpsimd
                    def _(pool):
                        with pool.If(pool.value_load(slow_i[0:1, 0:1], min_val=0, max_val=1) > 0):
                            pool.memset(below[:, :], 1.0).then_inc(s_pass, 1)
                            pool.wait_ge(s_pass, 1)
                            pool.affine_select(out=below[:, :], in_=below[:, :], compare_op=ALU.is_gt, fill=0.0,
                                               base=0, pattern=[[-1, R]], channel_multiplier=1).then_inc(s_below, 1)
                            pool.wait_ge(s_zero, 32 * NC)

                            def update(t):
                                wait_apart(pool, s_at, t + 1, s_pass)
                                pool.indirect_dma_start(
                                    out=held[:, :], out_offset=None, in_=agg,
                                    in_offset=bass.IndirectOffsetOnAxis(ap=at[:, 0:1], axis=0),
                                    bounds_check=N - 1, oob_is_err=False).then_inc(s_got, 16)
                                wait_apart(pool, s_tot, t + 1, s_pass)
                                pool.indirect_dma_start(
                                    out=agg, out_offset=bass.IndirectOffsetOnAxis(ap=at[:, 1:2], axis=0),
                                    in_=held[:, :], in_offset=None,
                                    bounds_check=N - 1, oob_is_err=False).then_inc(s_put, 16)

                            update(0)
                            with pool.Fori(1, ET) as t:
                                update(t)
                            pool.wait_ge(s_put, 16 * ET)

                    @block.tensor
                    def _(pe):
                        with pe.If(pe.value_load(slow_i[0:1, 0:1], min_val=0, max_val=1) > 0):
                            def sums(t):
                                pe.wait_ge(s_dmat, t + 1)
                                pe.transpose(p_d[:, 0:R], dmat[:, :], ident[0:R, 0:R]).then_inc(s_dt, 1)
                                pe.wait_ge(s_same, t + 1)
                                pe.matmul(p_s[0:R, 0:D], same[:, :], rows[:, 0:D], start=True, stop=True)\
                                    .then_inc(s_sum, 1)

                            sums(0)
                            with pe.Fori(1, ET) as t:
                                sums(t)

                    @block.vector
                    def _(dve):
                        with dve.If(dve.value_load(slow_i[0:1, 0:1], min_val=0, max_val=1) > 0):
                            dve.memset(zero[:, :, :], 0.0).then_inc(s_blank, 1)

                            def combine(t):
                                def step(n, ins):
                                    ins.then_inc(s_step, 1)
                                    dve.wait_ge(s_step, t * steps + n)

                                dve.wait_ge(s_rows, (t + 1) * 16)
                                dve.tensor_copy(dmat[:, :], rows[:, D:D + 1].to_broadcast([R, P])).then_inc(s_dmat, 1)
                                dve.wait_ge(s_dt, t + 1)
                                dve.tensor_scalar(same[:, :], p_d[0:R, 0:R], rows[:, D:D + 1], None, ALU.is_equal)\
                                    .then_inc(s_same, 1)
                                dve.wait_ge(s_same, t + 1)
                                dve.wait_ge(s_below, 1)
                                step(1, dve.tensor_tensor(earlier[:, :], same[:, :], below[:, :], ALU.mult))
                                step(2, dve.tensor_reduce(place[:, 0:1], earlier[:, :], AX_X, ALU.add))
                                step(3, dve.tensor_scalar(place[:, 1:2], place[:, 0:1], float(NO_ROW), None, ALU.mult))
                                step(4, dve.tensor_tensor(place[:, 1:2], place[:, 1:2], rows[:, D:D + 1], ALU.add))
                                step(5, dve.tensor_copy(at[:, 1:2], place[:, 1:2]))
                                dve.tensor_copy(at[:, 0:1], rows[:, D:D + 1]).then_inc(s_at, 1)
                                dve.wait_ge(s_sum, t + 1)
                                step(6, dve.tensor_copy(total[:, :], p_s[0:R, 0:D]))
                                dve.wait_ge(s_got, (t + 1) * 16)
                                dve.tensor_tensor(held[:, :], held[:, :], total[:, :], ALU.add).then_inc(s_tot, 1)

                            combine(0)
                            with dve.Fori(1, ET) as t:
                                combine(t)

        def either(eng, program):
            with eng.If(eng.value_load(slow_i[0:1, 0:1], min_val=0, max_val=1) > 0):
                program(True)
            with eng.Else():
                program(False)

        def load_windows(sp, win, w_load, a_done, n, b):
            wait_reuse(sp, a_done, (n - 1) * S + b + 1)
            _, rows = nc.values_load_multi_w_load_instructions(
                starts[0:1, bass.ds((n * S + b) * TC, TC)], engines=(mybir.EngineType.SP,), min_val=0, max_val=E)
            for j, row in enumerate(rows):
                sp.dma_start(win[b][:, j, :], msg[bass.ds(row, WIN), :]).then_inc(w_load[b], 16)

        def load_pair(sp, into, tiled, loaded, used, n, b):
            if b % 2 == 0:
                wait_reuse(sp, used, (n - 1) * S + b + 2)
                for lo, hi in split_rows():
                    sp.dma_start(into[b // 2][lo:hi, :, :, :].rearrange("p a j d -> p (a j) d"),
                                 tiled[lo:hi, bass.ds((n * S + b) * TC, 2 * TC), :]).then_inc(loaded[b // 2], 16)

        slow_path(0)

        with ExitStack() as ctx:
            sb, pb, sem = phase(ctx)
            xs = [sb(f"xs{h}", [R, 2, TC, D]) for h in range(2)]
            ax = [sb(f"ax{h}", [R, 2, TC, D]) for h in range(2)]
            win = [sb(f"win{b}", [P, TC, MW]) for b in range(S)]
            local = [sb(f"local{b}", [P, TC]) for b in range(S)]
            hot = [sb(f"hot{b}", [P, TC, R]) for b in range(S)]
            z = [sb(f"z{b}", [R, TC, D + 4]) for b in range(S)]
            zt = [sb(f"zt{b}", [P, CN]) for b in range(S)]
            zero = sb("zero", [R, D + 4])
            p_agg = [pb(f"p_agg{b}") for b in range(2)]
            p_zt = [pb(f"p_zt{b}") for b in range(2)]
            p_gram = pb("p_gram")
            x_load = [sem(f"nodes_loaded{h}") for h in range(2)]
            s_load = [sem(f"slow_sums_loaded{h}") for h in range(2)]
            w_load = [sem(f"windows_loaded{b}") for b in range(S)]
            l_ready, o_ready, a_done = sem("local_ready"), sem("one_hot_ready"), sem("messages_added")
            z_ready, z_used, t_copied = sem("z_ready"), sem("z_used"), sem("z_transpose_copied")
            t_store = [sem(f"z_stored{b}") for b in range(S)]
            z_blank = sem("z_blanked")
            with nc.Block() as block:
                @block.sync
                def _(sp):
                    def program(slow):
                        def load(n, b):
                            load_pair(sp, xs, x_tiles, x_load, z_ready, n, b)
                            if slow:
                                load_pair(sp, ax, agg_tiles, s_load, z_ready, n, b)
                            load_windows(sp, win, w_load, a_done, n, b)

                        run(sp, NC, (0, load))

                    either(sp, program)

                @block.gpsimd
                def _(pool):
                    def store(n, b):
                        pool.wait_ge(t_copied, n * S + b + 1)
                        pool.dma_start(zt_dram[bass.ds(n * S + b, 1), :, :].rearrange("a p n -> (a p) n"),
                                       zt[b][:, :]).then_inc(t_store[b], 16)

                    run(pool, NC, (0, store))
                    for b in range(S):
                        pool.wait_ge(t_store[b], 16 * (NC // S))

                @block.vector
                def _(dve):
                    dve.memset(zero[:, :], 0.0).then_inc(z_blank, 1)
                    for b in range(S):
                        dve.memset(z[b][:, :, D:D + 4], 1.0).then_inc(z_blank, 1)

                    def program(slow):
                        def one_hot(n, b):
                            dve.wait_ge(w_load[b], (n + 1) * (16 * TC))
                            wait_reuse(dve, o_ready, (n - 1) * S + b + 1)
                            dve.tensor_tensor(local[b][:, :].unsqueeze(2), win[b][:, :, D:D + 1],
                                              tile_base[:, bass.ds((n * S + b) * TC, TC)].unsqueeze(2),
                                              ALU.subtract).then_inc(l_ready, 1)
                            wait_reuse(dve, a_done, (n - 1) * S + b + 1)
                            dve.wait_ge(l_ready, n * S + b + 1)
                            dve.tensor_tensor(hot[b][:, :, :], node_iota[:, :].unsqueeze(1).to_broadcast([P, TC, R]),
                                              local[b][:, :].unsqueeze(2).to_broadcast([P, TC, R]), ALU.is_equal)\
                                .then_inc(o_ready, 1)

                        def z_sum(n, b):
                            h = b // 2
                            dve.wait_ge(x_load[h], (n + 1) * 32)
                            dve.wait_ge(a_done, n * S + b + 1)
                            if slow:
                                dve.wait_ge(s_load[h], (n + 1) * 32)
                            wait_reuse(dve, z_used, (n - 1) * S + b + 1)
                            dve.scalar_tensor_tensor(
                                out=z[b][:, :, 0:D], in0=xs[h][:, b % 2, :, :], scalar=eps1[0:R, 0:1],
                                in1=ax[h][:, b % 2, :, :] if slow
                                else p_agg[b % 2][0:R, :].rearrange("p (j d) -> p j d", d=D),
                                op0=ALU.mult, op1=ALU.add).then_inc(z_ready, 1)

                        run(dve, NC, (0, one_hot), (1, z_sum))

                    either(dve, program)

                @block.tensor
                def _(pe):
                    def aggregate(n, b):
                        pe.wait_ge(o_ready, n * S + b + 1)
                        wait_reuse(pe, z_ready, n * S + b - 1)
                        for j in range(TC):
                            mm = pe.matmul(p_agg[b % 2][0:R, j * D:(j + 1) * D], hot[b][:, j, :],
                                           win[b][:, j, 0:D], start=True, stop=True)
                        mm.then_inc(a_done, 1)

                    def moments(n, b):
                        pe.wait_ge(z_ready, n * S + b + 1)
                        for j in range(TC):
                            pe.matmul(p_gram[:, 0:D + 1], z[b][:, j, 0:D], z[b][:, j, 0:D + 1],
                                      start=False, stop=False, skip_group_check=True)
                        wait_reuse(pe, t_copied, n * S + b - 1)
                        for j in range(TC):
                            mm = pe.transpose(p_zt[b % 2][:, j * R:(j + 1) * R], z[b][:, j, 0:D], ident[0:R, 0:R])
                        mm.then_inc(z_used, 1)

                    pe.wait_ge(z_blank, 1 + S)
                    pe.matmul(p_gram[:, 0:D + 1], zero[:, 0:D], zero[:, 0:D + 1], start=True, stop=False,
                              skip_group_check=True)
                    run(pe, NC, (0, aggregate), (1, moments))

                @block.scalar
                def _(act):
                    def copy(n, b):
                        act.wait_ge(z_used, n * S + b + 1)
                        wait_reuse(act, t_store[b], n * 16)
                        act.activation(zt[b][:, :], p_zt[b % 2][:, 0:CN], ACT.Copy).then_inc(t_copied, 1)

                    run(act, NC, (0, copy))

            cov = sb("cov", [P, D])
            mean = sb("mean", [P, 1])
            mean_row = sb("mean_row", [1, P])
            neg_row = sb("neg_row", [1, P])
            wc = sb("wc", [P, H])
            var1, mean1 = sb("var1", [P, 2]), sb("mean1", [P, 2])
            p_s = pb("p_s")
            p_row = pb("p_row")
            s_step = sem("bn1_dve_step")
            s_mean, s_row, s_rowc = sem("mean_ready"), sem("mean_transposed"), sem("mean_row_ready")
            s_outer, s_cov, s_cw, s_wc = sem("outer_added"), sem("cov_ready"), sem("cov_w"), sem("w_cov_w")
            s_var, s_std, s_sq = sem("moments_ready"), sem("variance_ready"), sem("std_ready")
            with nc.Block() as block:
                @block.tensor
                def _(pe):
                    pe.wait_ge(s_mean, 1)
                    pe.transpose(p_row[0:1, 0:P], mean[:, :], ident[:, :]).then_inc(s_row, 1)
                    pe.wait_ge(s_rowc, 2)
                    pe.matmul(p_s[:, 0:D], neg_row[:, :], mean_row[:, :], start=True, stop=True)\
                        .then_inc(s_outer, 1)
                    pe.wait_ge(s_cov, 1)
                    pe.matmul(p_row[:, 0:H], cov[:, :], w1[:, :], start=True, stop=True).then_inc(s_cw, 1)
                    pe.wait_ge(s_wc, 1)
                    for h in range(2):
                        pe.matmul(p_s[:, h:h + 1], wc[:, h * P:(h + 1) * P], ones[:, 0:1], start=True, stop=True)
                        mm = pe.matmul(p_s[:, 2 + h:3 + h], w1[:, h * P:(h + 1) * P], mean[:, :],
                                       start=True, stop=True)
                    mm.then_inc(s_var, 1)

                @block.vector
                def _(dve):
                    ch = Chain(dve, s_step)
                    dve.tensor_scalar(mean[:, :], p_gram[:, D:D + 1], 1.0 / N, None, ALU.mult).then_inc(s_mean, 1)
                    dve.wait_ge(s_row, 1)
                    dve.tensor_copy(mean_row[:, :], p_row[0:1, 0:P]).then_inc(s_rowc, 1)
                    dve.tensor_scalar(neg_row[:, :], p_row[0:1, 0:P], -1.0, None, ALU.mult).then_inc(s_rowc, 1)
                    ch.step(dve.tensor_scalar(cov[:, :], p_gram[:, 0:D], 1.0 / N, None, ALU.mult))
                    dve.wait_ge(s_outer, 1)
                    dve.tensor_tensor(cov[:, :], cov[:, :], p_s[:, 0:D], ALU.add).then_inc(s_cov, 1)
                    dve.wait_ge(s_cw, 1)
                    dve.tensor_tensor(wc[:, :], w1[:, :], p_row[:, 0:H], ALU.mult).then_inc(s_wc, 1)
                    dve.wait_ge(s_var, 1)
                    ch.step(dve.tensor_copy(mean1[:, :], p_s[:, 2:4]))
                    dve.tensor_scalar(var1[:, :], p_s[:, 0:2], BN_EPS, None, ALU.add).then_inc(s_std, 1)
                    dve.wait_ge(s_sq, 1)
                    ch.step(dve.reciprocal(var1[:, :], var1[:, :]))
                    ch.step(dve.tensor_tensor(scale1[:, :], g1c[:, :], var1[:, :], ALU.mult))
                    ch.step(dve.tensor_tensor(mean1[:, :], mean1[:, :], scale1[:, :], ALU.mult))
                    ch.step(dve.tensor_tensor(shift1[:, :], b1c[:, :], mean1[:, :], ALU.subtract))

                @block.scalar
                def _(act):
                    act.wait_ge(s_std, 1)
                    act.activation(var1[:, :], var1[:, :], ACT.Sqrt).then_inc(s_sq, 1)

        with ExitStack() as ctx:
            sb, pb, sem = phase(ctx)
            zt = [sb(f"zt_in{b}", [P, CN]) for b in range(S)]
            hid = [sb(f"hid{b}", [P, 2, CN]) for b in range(S)]
            y = [sb(f"y{b}", [P, CN]) for b in range(S)]
            stats = sb("stats", [P, NC, 6])
            p_h = [[pb(f"p_h{b}{h}") for h in range(2)] for b in range(2)]
            p_y = [pb(f"p_y{b}") for b in range(2)]
            t_load = [sem(f"zt_loaded{b}") for b in range(S)]
            h_prod, h_ready = sem("hidden_product"), sem("hidden_ready")
            y_prod, y_copied = sem("y_product"), sem("y_copied")
            y_store = [sem(f"y_stored{b}") for b in range(S)]
            with nc.Block() as block:
                @block.sync
                def _(sp):
                    def load(n, b):
                        wait_reuse(sp, h_prod, (n - 1) * S + b + 1)
                        sp.dma_start(zt[b][:, :],
                                     zt_dram[bass.ds(n * S + b, 1), :, :].rearrange("a p n -> (a p) n"))\
                            .then_inc(t_load[b], 16)

                    run(sp, NC, (0, load))

                @block.gpsimd
                def _(pool):
                    def store(n, b):
                        pool.wait_ge(y_copied, n * S + b + 1)
                        pool.dma_start(zt_dram[bass.ds(n * S + b, 1), :, :].rearrange("a p n -> (a p) n"),
                                       y[b][:, :]).then_inc(y_store[b], 16)

                    run(pool, NC, (0, store))
                    for b in range(S):
                        pool.wait_ge(y_store[b], 16 * (NC // S))

                @block.tensor
                def _(pe):
                    def up(n, b):
                        pe.wait_ge(t_load[b], (n + 1) * 16)
                        wait_reuse(pe, h_ready, n * S + b - 1)
                        for h in range(2):
                            mm = pe.matmul(p_h[b % 2][h][:, 0:CN], w1[:, h * P:(h + 1) * P], zt[b][:, :],
                                           start=True, stop=True)
                        mm.then_inc(h_prod, 1)

                    def down(n, b):
                        pe.wait_ge(h_ready, n * S + b + 1)
                        wait_reuse(pe, y_copied, n * S + b - 1)
                        for h in range(2):
                            mm = pe.matmul(p_y[b % 2][:, 0:CN], w2[:, h, :], hid[b][:, h, :],
                                           start=(h == 0), stop=(h == 1))
                        mm.then_inc(y_prod, 1)

                    run(pe, NC, (0, up), (1, down))

                @block.scalar
                def _(act):
                    def relu(n, b):
                        act.wait_ge(h_prod, n * S + b + 1)
                        wait_reuse(act, y_prod, (n - 1) * S + b + 1)
                        for h in range(2):
                            ins = act.activation(hid[b][:, h, :], p_h[b % 2][h][:, 0:CN], ACT.Relu,
                                                 bias=shift1[:, h:h + 1], scale=scale1[:, h:h + 1])
                        ins.then_inc(h_ready, 1)

                    run(act, NC, (0, relu))

                @block.vector
                def _(dve):
                    def moments(n, b):
                        dve.wait_ge(y_prod, n * S + b + 1)
                        dve.bn_stats(stats[:, bass.ds(n * S + b, 1), :].rearrange("p a n -> p (a n)"),
                                     p_y[b % 2][:, 0:CN])
                        wait_reuse(dve, y_store[b], n * 16)
                        dve.tensor_copy(y[b][:, :], p_y[b % 2][:, 0:CN]).then_inc(y_copied, 1)

                    run(dve, NC, (0, moments))

            mv = sb("mv", [P, 2])
            s_agg, s_std, s_sq = sem("moments2"), sem("variance2"), sem("std2")
            s_step = sem("bn2_dve_step")
            with nc.Block() as block:
                @block.vector
                def _(dve):
                    ch = Chain(dve, s_step)
                    ch.step(dve.bn_aggr(mv[:, :], stats[:, :, :].rearrange("p a n -> p (a n)")))
                    dve.tensor_scalar(mv[:, 1:2], mv[:, 1:2], BN_EPS, None, ALU.add).then_inc(s_std, 1)
                    dve.wait_ge(s_sq, 1)
                    ch.step(dve.reciprocal(mv[:, 1:2], mv[:, 1:2]))
                    ch.step(dve.tensor_tensor(scale2[:, :], g2c[:, :], mv[:, 1:2], ALU.mult))
                    ch.step(dve.tensor_tensor(mv[:, 0:1], mv[:, 0:1], scale2[:, :], ALU.mult))
                    ch.step(dve.tensor_tensor(shift2[:, :], b2c[:, :], mv[:, 0:1], ALU.subtract))

                @block.scalar
                def _(act):
                    act.wait_ge(s_std, 1)
                    act.activation(mv[:, 1:2], mv[:, 1:2], ACT.Sqrt).then_inc(s_sq, 1)

        class Norm:

            def __init__(self, tag, sb, sem, out_tiles):
                self.u = [sb(f"{tag}_u{b}", [R, TC, D]) for b in range(S)]
                self.o = [sb(f"{tag}_o{h}", [R, 2, TC, D]) for h in range(2)]
                self.st = [sb(f"{tag}_st{b}", [R, TC, 6]) for b in range(S)]
                self.mv = [sb(f"{tag}_mv{b}", [R, TC, 2]) for b in range(S)]
                self.nb = [sb(f"{tag}_nb{b}", [R, TC]) for b in range(S)]
                self.out_tiles = out_tiles
                self.passed = sem(f"{tag}_wait_passed")
                self.u_ready, self.s_ready = sem(f"{tag}_sum_ready"), sem(f"{tag}_stats_ready")
                self.v_ready, self.q_ready = sem(f"{tag}_variance_ready"), sem(f"{tag}_sqrt_ready")
                self.r_ready, self.f_ready = sem(f"{tag}_rstd_ready"), sem(f"{tag}_factors_ready")
                self.o_ready, self.a_ready = sem(f"{tag}_norm_ready"), sem(f"{tag}_aggregated")
                self.o_store = [sem(f"{tag}_stored{h}") for h in range(2)]

            def moments(self, dve, n, b):
                dve.wait_ge(self.u_ready, n * S + b + 1)
                for j in range(TC):
                    ins = dve.bn_stats(self.st[b][:, j, :], self.u[b][:, j, :])
                ins.then_inc(self.s_ready, 1)
                wait_apart(dve, self.s_ready, n * S + b + 1, self.passed)
                for j in range(TC):
                    ins = dve.bn_aggr(self.mv[b][:, j, :], self.st[b][:, j, :])
                ins.then_inc(self.a_ready, 1)
                dve.wait_ge(self.a_ready, n * S + b + 1)
                dve.tensor_scalar(self.mv[b][:, :, 1:2], self.mv[b][:, :, 1:2], LN_EPS, None, ALU.add)\
                    .then_inc(self.v_ready, 1)

            def root(self, act, n, b):
                act.wait_ge(self.v_ready, n * S + b + 1)
                act.activation(self.mv[b][:, :, 1:2], self.mv[b][:, :, 1:2], ACT.Sqrt).then_inc(self.q_ready, 1)

            def factors(self, dve, n, b):
                dve.wait_ge(self.q_ready, n * S + b + 1)
                dve.reciprocal(self.mv[b][:, :, 1:2], self.mv[b][:, :, 1:2]).then_inc(self.r_ready, 1)
                dve.wait_ge(self.r_ready, n * S + b + 1)
                dve.scalar_tensor_tensor(out=self.nb[b][:, :].unsqueeze(2), in0=self.mv[b][:, :, 0:1], scalar=-1.0,
                                         in1=self.mv[b][:, :, 1:2], op0=ALU.mult, op1=ALU.mult)\
                    .then_inc(self.f_ready, 1)

            def scale(self, act, n, b):
                act.wait_ge(self.f_ready, n * S + b + 1)
                wait_reuse(act, self.o_store[b // 2], n * 32)
                for j in range(TC):
                    ins = act.activation(self.o[b // 2][:, b % 2, j, :], self.u[b][:, j, :], ACT.Identity,
                                         bias=self.nb[b][:, j:j + 1], scale=self.mv[b][:, j, 1:2])
                ins.then_inc(self.o_ready, 1)

            def store(self, eng, n, b):
                if b % 2:
                    eng.wait_ge(self.o_ready, n * S + b + 1)
                    for lo, hi in split_rows():
                        eng.dma_start(self.out_tiles[lo:hi, bass.ds((n * S + b - 1) * TC, 2 * TC), :],
                                      self.o[b // 2][lo:hi, :, :, :].rearrange("p a j d -> p (a j) d"))\
                            .then_inc(self.o_store[b // 2], 16)

            def stored(self, eng):
                for h in range(2):
                    eng.wait_ge(self.o_store[h], 32 * (NC // S))

        with ExitStack() as ctx:
            sb, pb, sem = phase(ctx)
            yt = [sb(f"yt{b}", [P, CN]) for b in range(S)]
            xs = [sb(f"x2s{h}", [R, 2, TC, D]) for h in range(2)]
            r = [sb(f"r{b}", [P, CN]) for b in range(S)]
            p_r = [pb(f"p_r{b}") for b in range(S)]
            y_load = [sem(f"y_loaded{b}") for b in range(S)]
            x_load = [sem(f"x_loaded{h}") for h in range(2)]
            r_ready, t_done = sem("relu_ready"), sem("relu_transposed")
            norm = Norm("norm0", sb, sem, x1_tiles)
            with nc.Block() as block:
                @block.sync
                def _(sp):
                    def load(n, b):
                        wait_reuse(sp, r_ready, (n - 1) * S + b + 1)
                        sp.dma_start(yt[b][:, :],
                                     zt_dram[bass.ds(n * S + b, 1), :, :].rearrange("a p n -> (a p) n"))\
                            .then_inc(y_load[b], 16)
                        load_pair(sp, xs, x_tiles, x_load, norm.u_ready, n, b)

                    run(sp, NC, (0, load))

                @block.gpsimd
                def _(pool):
                    run(pool, NC, (0, lambda n, b: norm.store(pool, n, b)))
                    norm.stored(pool)

                @block.scalar
                def _(act):
                    def relu(n, b):
                        act.wait_ge(y_load[b], (n + 1) * 16)
                        wait_reuse(act, t_done, (n - 1) * S + b + 1)
                        act.activation(r[b][:, :], yt[b][:, :], ACT.Relu, bias=shift2[:, 0:1],
                                       scale=scale2[:, 0:1]).then_inc(r_ready, 1)

                    run(act, NC, (0, relu), (1, lambda n, b: norm.root(act, n, b)),
                        (2, lambda n, b: norm.scale(act, n, b)))

                @block.tensor
                def _(pe):
                    def turn(n, b):
                        pe.wait_ge(r_ready, n * S + b + 1)
                        wait_reuse(pe, norm.u_ready, (n - 1) * S + b + 1)
                        for j in range(TC):
                            mm = pe.transpose(p_r[b][0:R, j * D:(j + 1) * D], r[b][:, j * R:(j + 1) * R],
                                              ident[:, :])
                        mm.then_inc(t_done, 1)

                    run(pe, NC, (0, turn))

                @block.vector
                def _(dve):
                    def total(n, b):
                        dve.wait_ge(x_load[b // 2], (n + 1) * 32)
                        dve.wait_ge(t_done, n * S + b + 1)
                        wait_reuse(dve, norm.o_ready, (n - 1) * S + b + 1)
                        dve.scalar_tensor_tensor(
                            out=norm.u[b][:, :, :], in0=xs[b // 2][:, b % 2, :, :], scalar=2.0,
                            in1=p_r[b][0:R, :].rearrange("p (j d) -> p j d", d=D),
                            op0=ALU.mult, op1=ALU.add).then_inc(norm.u_ready, 1)
                        norm.moments(dve, n, b)

                    run(dve, NC, (0, total), (1, lambda n, b: norm.factors(dve, n, b)))

        with ExitStack() as ctx:
            sb, pb, sem = phase(ctx)
            xg = [sb(f"x1g{b}", [R, TC, D]) for b in range(S)]
            idx = [sb(f"idx1{b}", [R, TC], I32) for b in range(S)]
            h2 = [sb(f"h2_in{h}", [P, CN]) for h in range(2)]
            xt = [sb(f"xt{b}", [P, CN]) for b in range(2)]
            wq = [[sb(f"wq{b}{q}", [P, CN]) for q in range(2)] for b in range(2)]
            m = [[sb(f"m{b}{q}", [P, CN]) for q in range(2)] for b in range(2)]
            rv = [sb(f"rv{b}", [R, TC, MUL, 3]) for b in range(2)]
            gs = [sb(f"gs{b}", [R, TC, MUL, 3]) for b in range(2)]
            gr = [sb(f"gr{b}", [R, TC, MUL]) for b in range(2)]
            mo = [sb(f"mo1{h}", [R, 2, TC, MW]) for h in range(2)]
            p_xt, p_up = pb("p_xt"), pb("p_up")
            p_w = [pb(f"p_w{q}") for q in range(2)]
            p_o = [[pb(f"p_o{b}{q}") for q in range(2)] for b in range(2)]
            g_done = [sem(f"x1_gathered{b}") for b in range(S)]
            i_ready, i_passed = sem("index1_ready"), sem("index1_wait_passed")
            h_load = [sem(f"h2_loaded{h}") for h in range(2)]
            t_done, t_copied = sem("x1_transposed"), sem("x1_transpose_copied")
            u_done, w_done = sem("up_product"), sem("path_weights_product")
            w_copied, m_ready, o_done = sem("path_weights_ready"), sem("paths_ready"), sem("out_product")
            c1, c2, c3 = sem("direction_products"), sem("direction_sums"), sem("messages1_ready")
            b_blank, m_dst = sem("messages1_blanked"), sem("destination1_written")
            m_store = [sem(f"messages1_stored{h}") for h in range(2)]
            with nc.Block() as block:
                @block.gpsimd
                def _(pool):
                    for h in range(2):
                        pool.memset(mo[h][:, :, :, :], 0.0).then_inc(b_blank, 1)

                    def gather(n, b):
                        wait_reuse(pool, t_done, (n - 1) * S + b + 1)
                        pool.tensor_copy(idx[b][:, :], src_all[:, bass.ds((n * S + b) * TC, TC)])\
                            .then_inc(i_ready, 1)
                        wait_apart(pool, i_ready, n * S + b + 1, i_passed)
                        for j in range(TC):
                            pool.indirect_dma_start(
                                out=xg[b][:, j, :], out_offset=None, in_=x1_dram,
                                in_offset=bass.IndirectOffsetOnAxis(ap=idx[b][:, j:j + 1], axis=0),
                                bounds_check=N - 1, oob_is_err=False).then_inc(g_done[b], 16)

                    run(pool, EC, (0, gather))

                @block.sync
                def _(sp):
                    def load(n, b):
                        if b % 2 == 0:
                            wait_reuse(sp, w_done, (n - 1) * S + b + 2)
                            sp.dma_start(h2[b // 2][:, :],
                                         h2_dram[bass.ds(n * 2 + b // 2, 1), :, :].rearrange("a p n -> (a p) n"))\
                                .then_inc(h_load[b // 2], 16)

                    def store(n, b):
                        if b % 2:
                            sp.wait_ge(c3, n * S + b + 1)
                            sp.wait_ge(m_dst, n * S + b + 1)
                            for lo, hi in split_rows():
                                sp.dma_start(msg_rows[lo:hi, bass.ds((n * S + b - 1) * TC, 2 * TC), :],
                                             mo[b // 2][lo:hi, :, :, :].rearrange("p a j d -> p (a j) d"))\
                                    .then_inc(m_store[b // 2], 16)

                    run(sp, EC, (0, load), (2, store))
                    for h in range(2):
                        sp.wait_ge(m_store[h], 32 * ((EC // 2 - h + 1) // 2))

                @block.tensor
                def _(pe):
                    def inputs(n, b):
                        pe.wait_ge(g_done[b], (n + 1) * (16 * TC))
                        wait_reuse(pe, t_copied, n * S + b)
                        for j in range(TC):
                            mm = pe.transpose(p_xt[:, j * R:(j + 1) * R], xg[b][:, j, :], ident[0:R, 0:R])
                        mm.then_inc(t_done, 1)
                        pe.wait_ge(h_load[b // 2], (n + 1) * 16)
                        wait_reuse(pe, w_copied, n * S + b)
                        for q in range(2):
                            mm = pe.matmul(p_w[q][:, 0:CN], w_mlp2[:, b % 2, q, :], h2[b // 2][:, :],
                                           start=True, stop=True)
                        mm.then_inc(w_done, 1)

                    def outputs(n, b):
                        pe.wait_ge(m_ready, n * S + b + 1)
                        wait_reuse(pe, c3, n * S + b - 1)
                        for q, w in ((0, w_outA), (1, w_outB)):
                            for j in range(TC):
                                mm = pe.matmul(p_o[b % 2][q][0:R, j * D:(j + 1) * D],
                                               m[b % 2][q][:, j * R:(j + 1) * R], w[:, :], start=True, stop=True)
                        mm.then_inc(o_done, 1)

                    def up(n, b):
                        pe.wait_ge(t_copied, n * S + b + 1)
                        wait_reuse(pe, m_ready, n * S + b)
                        pe.matmul(p_up[:, 0:CN], w_up[:, :], xt[b % 2][:, :], start=True, stop=True)\
                            .then_inc(u_done, 1)

                    run(pe, EC, (0, inputs), (1, outputs), (0, up))

                @block.scalar
                def _(act):
                    def copies(n, b):
                        act.wait_ge(t_done, n * S + b + 1)
                        wait_reuse(act, u_done, n * S + b - 1)
                        act.activation(xt[b % 2][:, :], p_xt[:, 0:CN], ACT.Copy).then_inc(t_copied, 1)
                        act.wait_ge(w_done, n * S + b + 1)
                        wait_reuse(act, m_ready, n * S + b - 1)
                        for q in range(2):
                            ins = act.activation(wq[b % 2][q][:, :], p_w[q][:, 0:CN], ACT.Identity,
                                                 bias=b_mlp2[:, q:q + 1])
                        ins.then_inc(w_copied, 1)

                    run(act, EC, (0, copies))

                @block.vector
                def _(dve):
                    def combine(n, b):
                        full = [R, TC, MUL, 3]
                        c = b % 2
                        rh = rhat[:, bass.ds((n * S + b) * TC, TC), :].unsqueeze(2).to_broadcast(full)
                        oA = p_o[c][0][0:R, :].rearrange("p (j d) -> p j d", d=D)
                        oB = p_o[c][1][0:R, :].rearrange("p (j d) -> p j d", d=D)
                        out_m = mo[b // 2][:, c, :, :]
                        dve.wait_ge(o_done, n * S + b + 1)
                        wait_reuse(dve, c3, n * S + b)
                        dve.tensor_tensor(rv[c][:, :, :, :], oB[:, :, 0:MUL].unsqueeze(3).to_broadcast(full), rh,
                                          ALU.mult)
                        dve.tensor_tensor(gs[c][:, :, :, :],
                                          oB[:, :, MUL:D].rearrange("p j (k c) -> p j k c", c=3), rh,
                                          ALU.mult).then_inc(c1, 1)
                        dve.wait_ge(c1, n * S + b + 1)
                        dve.tensor_reduce(gr[c][:, :, :], gs[c][:, :, :, :], AX_X, ALU.add).then_inc(c2, 1)
                        wait_reuse(dve, m_store[b // 2], n * 32)
                        if isinstance(n, int) and n == 0:
                            dve.wait_ge(b_blank, 2)
                        dve.tensor_tensor(out_m[:, :, MUL:D].rearrange("p j (k c) -> p j k c", c=3),
                                          oA[:, :, MUL:D].rearrange("p j (k c) -> p j k c", c=3),
                                          rv[c][:, :, :, :], ALU.add)
                        dve.tensor_copy(out_m[:, :, D:D + 1],
                                        dst_f[:, bass.ds((n * S + b) * TC, TC)].unsqueeze(2)).then_inc(m_dst, 1)
                        dve.wait_ge(c2, n * S + b + 1)
                        dve.tensor_tensor(out_m[:, :, 0:MUL], oA[:, :, 0:MUL], gr[c][:, :, :], ALU.add)\
                            .then_inc(c3, 1)

                    def products(n, b):
                        c = b % 2
                        dve.wait_ge(u_done, n * S + b + 1)
                        dve.wait_ge(w_copied, n * S + b + 1)
                        wait_reuse(dve, o_done, n * S + b - 1)
                        for q in range(2):
                            ins = dve.tensor_tensor(m[c][q][:, :], p_up[:, 0:CN], wq[c][q][:, :], ALU.mult)
                        ins.then_inc(m_ready, 1)

                    run(dve, EC, (1, combine), (0, products))

        slow_path(1)

        with ExitStack() as ctx:
            sb, pb, sem = phase(ctx)
            xs = [sb(f"x3s{h}", [R, 2, TC, D]) for h in range(2)]
            ax = [sb(f"ax1{h}", [R, 2, TC, D]) for h in range(2)]
            win = [sb(f"win1{b}", [P, TC, MW]) for b in range(S)]
            local = [sb(f"local1{b}", [P, TC]) for b in range(S)]
            hot = [sb(f"hot1{b}", [P, TC, R]) for b in range(S)]
            p_agg = [pb(f"p_agg1{b}") for b in range(S)]
            x_load = [sem(f"x1_loaded{h}") for h in range(2)]
            s_load = [sem(f"slow_sums1_loaded{h}") for h in range(2)]
            w_load = [sem(f"windows1_loaded{b}") for b in range(S)]
            l_ready, l_passed = sem("local1_ready"), sem("local1_wait_passed")
            o_ready, a_done = sem("one_hot1_ready"), sem("messages1_added")
            norm = Norm("norm1", sb, sem, out_tiles)
            with nc.Block() as block:
                @block.sync
                def _(sp):
                    def program(slow):
                        def load(n, b):
                            load_pair(sp, xs, x1_tiles, x_load, norm.u_ready, n, b)
                            if slow:
                                load_pair(sp, ax, agg_tiles, s_load, norm.u_ready, n, b)
                            load_windows(sp, win, w_load, a_done, n, b)

                        run(sp, NC, (0, load))

                    either(sp, program)

                @block.gpsimd
                def _(pool):
                    def one_hot(n, b):
                        pool.wait_ge(w_load[b], (n + 1) * (16 * TC))
                        wait_reuse(pool, o_ready, (n - 1) * S + b + 1)
                        pool.tensor_tensor(local[b][:, :].unsqueeze(2), win[b][:, :, D:D + 1],
                                           tile_base[:, bass.ds((n * S + b) * TC, TC)].unsqueeze(2),
                                           ALU.subtract).then_inc(l_ready, 1)
                        wait_reuse(pool, a_done, (n - 1) * S + b + 1)
                        wait_apart(pool, l_ready, n * S + b + 1, l_passed)
                        for j in range(TC):
                            ins = pool.tensor_scalar(hot[b][:, j, :], node_iota[:, :], local[b][:, j:j + 1], None,
                                                     ALU.is_equal)
                        ins.then_inc(o_ready, 1)

                    run(pool, NC, (0, one_hot))

                @block.tensor
                def _(pe):
                    def aggregate(n, b):
                        pe.wait_ge(o_ready, n * S + b + 1)
                        wait_reuse(pe, norm.u_ready, (n - 1) * S + b + 1)
                        for j in range(TC):
                            mm = pe.matmul(p_agg[b][0:R, j * D:(j + 1) * D], hot[b][:, j, :],
                                           win[b][:, j, 0:D], start=True, stop=True)
                        mm.then_inc(a_done, 1)

                    run(pe, NC, (0, aggregate))

                @block.vector
                def _(dve):
                    def program(slow):
                        def total(n, b):
                            h = b // 2
                            dve.wait_ge(x_load[h], (n + 1) * 32)
                            dve.wait_ge(a_done, n * S + b + 1)
                            if slow:
                                dve.wait_ge(s_load[h], (n + 1) * 32)
                            wait_reuse(dve, norm.o_ready, (n - 1) * S + b + 1)
                            dve.tensor_tensor(norm.u[b][:, :, :], xs[h][:, b % 2, :, :],
                                              ax[h][:, b % 2, :, :] if slow
                                              else p_agg[b][0:R, :].rearrange("p (j d) -> p j d", d=D), ALU.add)\
                                .then_inc(norm.u_ready, 1)
                            norm.moments(dve, n, b)

                        run(dve, NC, (0, total), (1, lambda n, b: norm.factors(dve, n, b)))

                    either(dve, program)

                @block.scalar
                def _(act):
                    run(act, NC, (0, lambda n, b: norm.root(act, n, b)), (1, lambda n, b: norm.scale(act, n, b)),
                        (1, lambda n, b: norm.store(act, n, b)))
                    norm.stored(act)


_INS = ["x", "src", "dst", "edge_attr_128", "edge_attr_3", "edge_weight", "L0_gnn_eps", "L0_gnn_W1", "L0_gnn_g1",
        "L0_gnn_b1", "L0_gnn_W2", "L0_gnn_g2", "L0_gnn_b2", "L1_gnn_W_up0", "L1_gnn_W_up1", "L1_gnn_mlp_w0",
        "L1_gnn_mlp_b0", "L1_gnn_mlp_w1", "L1_gnn_mlp_b1", "L1_gnn_mlp_w2", "L1_gnn_mlp_b2", "L1_gnn_W_out0",
        "L1_gnn_W_out1"]


def kernel(**inputs):
    import numpy as _np
    import concourse.bacc as _bacc
    from concourse import mybir as _mybir
    from concourse.bass_utils import run_bass_kernel_spmd as _run

    nc = _bacc.Bacc("TRN2", target_bir_lowering=False, num_devices=1)
    arrays, args = {}, []
    for name in _INS:
        a = _np.ascontiguousarray(inputs[name])
        if a.ndim == 0:
            a = a.reshape(1)
        arrays[f"in_{name}_dram"] = a
        args.append(nc.dram_tensor(f"in_{name}_dram", a.shape, _mybir.dt.from_np(a.dtype), kind="ExternalInput").ap())
    shape = tuple(inputs["x"].shape)
    args.append(nc.dram_tensor("out_0_dram", shape, _mybir.dt.float32, kind="ExternalOutput").ap())
    gnn_kernel(nc, *args)
    r = _run(nc, [arrays], core_ids=[0])
    return r.results[0]["out_0_dram"]
```

```python
from contextlib import ExitStack

import concourse.bass as bass
from concourse import mybir

F32 = mybir.dt.float32
F32R = mybir.dt.float32r
I32 = mybir.dt.int32
ALU = mybir.AluOpType
ACT = mybir.ActivationFunctionType
AX_X = mybir.AxisListType.X

P = 128
R = 125
TC = 4
CN = R * TC
WIN = 96
S = 12
ES = 6
EP = ES // 2
QD = 4
QS = S // QD
KEEP = 4
POOL_HOT = 2
LAG_DOWN = 2
AHEAD = 4
MW = 132
BN_EPS = 1e-5
LN_EPS = 1e-5
NO_ROW = 1 << 24


def split_rows(lo_hi=(0, 112, R)):
    return [(lo_hi[i], lo_hi[i + 1]) for i in range(2)]


def wait_reuse(eng, sem, value):
    if not (isinstance(value, int) and value <= 0):
        eng.wait_ge(sem, value)


def uses(total, slot, slots):
    return (total - slot + slots - 1) // slots


def run(eng, total, *stages, ring=S, peeled=1):
    rounds = total // ring

    def step(n, b, at):
        for lag, f in stages:
            m, c = (n, b - lag) if b >= lag else (n - 1, b - lag + ring)
            if at is None or 0 <= at - lag < total:
                f(m, c)

    for at in range(peeled * ring):
        step(at // ring, at % ring, at)
    if rounds > peeled:
        with eng.Fori(peeled, rounds) as n:
            for b in range(ring):
                step(n, b, None)
    for at in range(max(rounds, peeled) * ring, total + max(lag for lag, _ in stages)):
        step(at // ring, at % ring, at)


def wait_apart(eng, sem, value, passed):
    eng.wait_ge(sem, value)
    eng.sem_inc(passed, 1)


def wait_reuse_apart(eng, sem, value, passed):
    if not (isinstance(value, int) and value <= 0):
        wait_apart(eng, sem, value, passed)


class Chain:

    def __init__(self, eng, sem):
        self.eng, self.sem, self.n = eng, sem, 0

    def step(self, ins):
        self.n += 1
        ins.then_inc(self.sem, 1)
        self.eng.wait_ge(self.sem, self.n)


def gnn_kernel(nc, x, src, dst, edge_attr_128, edge_attr_3, edge_weight, eps, W1, g1, b1, W2, g2, b2,
               W_up0, W_up1, mlp_w0, mlp_b0, mlp_w1, mlp_b1, mlp_w2, mlp_b2, W_out0, W_out1, out):
    N, D = x.shape
    E = src.shape[0]
    H = W1.shape[1]
    MUL = W_up0.shape[0]
    NB, HM = mlp_w0.shape
    NT, ET = N // R, E // R
    NC, EC = NT // TC, ET // TC
    FINE = next(f for f in range(int(NT ** 0.5), 0, -1) if NT % f == 0)
    COARSE = NT // FINE
    assert D == P and H == 2 * P and NT * R == N and ET * R == E and HM == 64 and NB == 8 and MUL == 32
    assert NC * TC == NT and EC * TC == ET and NC % QD == 0 and EC % 2 == 0 and COARSE <= 64

    msg = nc.dram_tensor("msg_rows", (E + WIN, MW), F32, kind="Internal").ap()
    zt_dram = nc.dram_tensor("z_transposed", (NC, P, CN), F32, kind="Internal").ap()
    x1_dram = nc.dram_tensor("x_after_layer0", (N, D), F32, kind="Internal").ap()
    h2_dram = nc.dram_tensor("radial_hidden", (EC // 2, P, CN), F32, kind="Internal").ap()

    first_dram = nc.dram_tensor("first_edges", (COARSE, FINE), F32, kind="Internal").ap()
    agg = nc.dram_tensor("slow_path_sums", (N, D), F32, kind="Internal").ap()
    agg_tiles = agg.rearrange("(t p) d -> p t d", p=R)
    x_tiles = x.rearrange("(t p) d -> p t d", p=R)
    x1_tiles = x1_dram.rearrange("(t p) d -> p t d", p=R)
    out_tiles = out.rearrange("(t p) d -> p t d", p=R)
    ea_rows = edge_attr_128.rearrange("(p j) d -> p j d", j=ET)
    msg_rows = msg[0:E, :].rearrange("(p j) d -> p j d", j=ET)

    root = ExitStack()
    with root:
        def make(ctx):
            def sb(name, shape, dt=F32):
                return ctx.enter_context(nc.sbuf_tensor(name, shape, dt))

            def pb(name, shape=(P, 512)):
                return ctx.enter_context(nc.psum_tensor(name, list(shape), F32))

            def sem(name):
                return ctx.enter_context(nc.semaphore(name))
            return sb, pb, sem

        def phase(ctx):
            sb, pb, _ = make(ctx)
            taken = []

            def sem(name):
                taken.append(nc.alloc_semaphore(name))
                return taken[-1]

            def clear():
                nc.clear_and_free_semaphores(taken)
                nc.all_engine_barrier()

            ctx.callback(clear)
            return sb, pb, sem

        sb, pb, sem = make(root)

        ident = sb("ident", [P, P])
        ones = sb("ones", [P, P])
        node_iota = sb("node_iota", [P, R])
        tile_base = sb("tile_base", [P, NT])
        src_all = sb("src_all", [R, ET], I32)
        dst_f = sb("dst_f", [R, ET])
        rhat = sb("rhat", [R, ET, 3])
        emb = sb("emb", [R, ET, NB])
        eps1 = sb("eps1", [P, 1])
        w1 = sb("w1", [P, H])
        w2 = sb("w2", [P, 2, D])
        g1c, b1c = sb("g1c", [P, 2]), sb("b1c", [P, 2])
        g2c, b2c = sb("g2c", [P, 1]), sb("b2c", [P, 1])
        scale1, shift1 = sb("scale1", [P, 2]), sb("shift1", [P, 2])
        scale2, shift2 = sb("scale2", [P, 1]), sb("shift2", [P, 1])
        w_up = sb("w_up", [P, P])
        w_mlp0 = sb("w_mlp0", [64, 4, P])
        w_mlp1 = sb("w_mlp1", [P, P])
        w_mlp2 = sb("w_mlp2", [P, 2, 2, P])
        b_mlp0, b_mlp1, b_mlp2 = sb("b_mlp0", [P, 1]), sb("b_mlp1", [P, 1]), sb("b_mlp2", [P, 2])
        w_outA, w_outB = sb("w_outA", [P, P]), sb("w_outB", [P, P])
        starts = sb("starts", [1, NT], I32)
        slow_i = sb("slow_i", [1, 1], I32)
        unsorted = sb("unsorted", [R, 1])

        with ExitStack() as ctx:
            sb, pb, sem = phase(ctx)
            dst_i = sb("dst_i", [R, ET], I32)
            next_i = sb("next_i", [R, ET], I32)
            next_f = sb("next_f", [R, ET])
            base_i = sb("base_i", [P, NT], I32)
            iota_i = sb("iota_i", [P, R], I32)
            k_i = sb("k_i", [R, NB], I32)
            k_f = sb("k_f", [R, NB])
            ew = sb("ew", [R, ET])
            xc = sb("xc", [R, ET])
            mask = sb("mask", [R, ET])
            ea3 = sb("ea3", [R, ET, 3])
            sq3 = sb("sq3", [R, ET, 3])
            nrm = sb("nrm", [R, ET])
            eps_in = sb("eps_in", [1, 1])
            tmpA, tmpB = sb("tmpA", [P, MUL]), sb("tmpB", [P, MUL])
            mlp2_in = sb("mlp2_in", [P, 4 * MUL])
            pad = sb("pad", [WIN, MW])
            p_eps = pb("p_eps")
            s_load = sem("inputs_loaded")
            s_blank = sem("tiles_blanked")
            s_wload = sem("weights_loaded")
            s_iota = sem("iotas_done")
            s_pool = sem("pool_step")
            s_ones = sem("ones_ready")
            s_pad = sem("pad_ready")
            s_padst = sem("pad_stored")
            s_epsmm = sem("eps_broadcast")
            s_dve = sem("dve_step")
            s_sqn = sem("norm_squared")
            s_nrm = sem("norm_ready")
            s_embx = sem("exponent_ready")
            s_embe = sem("exp_done")
            s_next = sem("next_blanked")
            with nc.Block() as block:
                n_loads = 14

                @block.sync
                def _(sp):
                    def load(dst_ap, src_ap, s):
                        sp.dma_start(dst_ap, src_ap, allow_slow_non_contiguous=True).then_inc(s, 16)

                    load(dst_i[:, :], dst.rearrange("(p j) -> p j", j=ET), s_load)
                    sp.wait_ge(s_next, 1)
                    load(next_i[0:R - 1, :], dst[1:1 + (R - 1) * ET].rearrange("(p j) -> p j", j=ET), s_load)
                    load(next_i[R - 1:R, 0:ET - 1], dst[1 + (R - 1) * ET:E].rearrange("(p j) -> p j", p=1), s_load)
                    load(src_all[:, :], src.rearrange("(p j) -> p j", j=ET), s_load)
                    load(ew[:, :], edge_weight.rearrange("(p j) -> p j", j=ET), s_load)
                    load(ea3[:, :, :], edge_attr_3.rearrange("(p j) c -> p j c", j=ET), s_load)
                    load(eps_in[:, :], eps.rearrange("(a b) -> a b", a=1), s_load)
                    load(w1[:, :], W1, s_load)
                    load(w2[:, :, :], W2.rearrange("(h p) d -> p h d", p=P), s_load)
                    load(g1c[:, :], g1.rearrange("(h p) -> p h", p=P), s_load)
                    load(b1c[:, :], b1.rearrange("(h p) -> p h", p=P), s_load)
                    load(g2c[:, :], g2.rearrange("(p a) -> p a", a=1), s_load)
                    load(b2c[:, :], b2.rearrange("(p a) -> p a", a=1), s_load)
                    load(b_mlp2[0:MUL, 0:1], mlp_b2[0:MUL].rearrange("(p a) -> p a", a=1), s_load)
                    sp.wait_ge(s_blank, 8)
                    load(w_up[0:MUL, 0:MUL], W_up0, s_wload)
                    for c in range(3):
                        load(w_up[MUL + c:P:3, MUL * (c + 1):MUL * (c + 2)], W_up1, s_wload)
                    for v in range(4):
                        load(w_mlp0[NB * v:NB * v + NB, v, 0:HM], mlp_w0, s_wload)
                        load(w_mlp0[NB * (v + 4):NB * (v + 5), v, HM:P], mlp_w0, s_wload)
                    for h in range(2):
                        rows = slice(HM * h, HM * h + HM)
                        load(w_mlp1[rows, HM * h:HM * h + HM], mlp_w1, s_wload)
                        load(b_mlp0[rows, :], mlp_b0.rearrange("(p a) -> p a", a=1), s_wload)
                        load(b_mlp1[rows, :], mlp_b1.rearrange("(p a) -> p a", a=1), s_wload)
                        load(mlp2_in[rows, :], mlp_w2, s_wload)
                    sp.wait_ge(s_pad, 2)
                    sp.dma_start(msg[E:E + WIN, :], pad[:, :]).then_inc(s_padst, 16)
                    sp.wait_ge(s_padst, 16)

                n_wload = 1 + 3 + 8 + 2 * (3 + 1) + 7 + 2 + 6

                @block.gpsimd
                def _(pool):
                    pool.memset(ident[:, :], 0.0).then_inc(s_pool, 1)
                    pool.wait_ge(s_pool, 1)
                    pool.affine_select(out=ident[:, :], in_=ident[:, :], compare_op=ALU.not_equal, fill=1.0,
                                       base=0, pattern=[[-1, P]], channel_multiplier=1)
                    pool.iota(iota_i[:, :], [[1, R]], base=0, channel_multiplier=0).then_inc(s_iota, 1)
                    pool.iota(base_i[:, :], [[R, NT]], base=0, channel_multiplier=0).then_inc(s_iota, 1)
                    pool.iota(k_i[:, :], [[1, NB]], base=0, channel_multiplier=0).then_inc(s_iota, 1)

                @block.tensor
                def _(pe):
                    pe.wait_ge(s_ones, 1)
                    pe.wait_ge(s_load, 16 * n_loads)
                    pe.matmul(p_eps[:, 0:1], ones[0:1, :], eps_in[:, :], start=True, stop=True).then_inc(s_epsmm, 1)

                @block.scalar
                def _(act):
                    def load_w(dst_ap, src_ap, s):
                        act.dma_start(dst_ap, src_ap, allow_slow_non_contiguous=True).then_inc(s, 16)

                    act.wait_ge(s_blank, 8)
                    for q in range(2):
                        if q:
                            load_w(b_mlp2[0:MUL, 1:2], mlp_b2[MUL:2 * MUL].rearrange("(p a) -> p a", a=1), s_wload)
                        for c in range(3):
                            load_w(b_mlp2[MUL * (c + 1):MUL * (c + 2), q:q + 1],
                                   mlp_b2[MUL * (q + 2):MUL * (q + 3)].rearrange("(p a) -> p a", a=1), s_wload)
                    load_w(w_outA[0:MUL, 0:MUL], W_out0[0:MUL, :], s_wload)
                    load_w(w_outB[0:MUL, 0:MUL], W_out1[0:MUL, :], s_wload)
                    for c in range(3):
                        load_w(tmpA[MUL * (c + 1):MUL * (c + 2), :], W_out1[MUL:2 * MUL, :], s_wload)
                        load_w(tmpB[MUL * (c + 1):MUL * (c + 2), :], W_out0[MUL:2 * MUL, :], s_wload)
                    act.wait_ge(s_sqn, 1)
                    act.activation(nrm[:, :], nrm[:, :], ACT.Sqrt).then_inc(s_nrm, 1)
                    act.wait_ge(s_embx, 1)
                    act.activation(emb[:, :, :], emb[:, :, :], ACT.Exp, scale=-0.5).then_inc(s_embe, 1)

                @block.vector
                def _(dve):
                    dve.memset(next_i[:, :], NO_ROW).then_inc(s_next, 1)
                    dve.memset(ones[:, :], 1.0).then_inc(s_ones, 1)
                    for t in (w_up, w_mlp1, w_outA, w_outB):
                        dve.memset(t[:, :], 0.0).then_inc(s_blank, 1)
                    dve.memset(w_mlp0[:, :, :], 0.0).then_inc(s_blank, 1)
                    dve.memset(w_mlp2[:, :, :, :], 0.0).then_inc(s_blank, 1)
                    dve.memset(tmpA[:, :], 0.0).then_inc(s_blank, 1)
                    dve.memset(tmpB[:, :], 0.0).then_inc(s_blank, 1)
                    dve.memset(pad[:, :], 0.0).then_inc(s_pad, 1)
                    dve.wait_ge(s_pad, 1)
                    dve.memset(pad[:, D:D + 1], -1.0).then_inc(s_pad, 1)
                    ch = Chain(dve, s_dve)
                    dve.wait_ge(s_iota, 3)
                    dve.tensor_copy(node_iota[:, :], iota_i[:, :])
                    dve.tensor_copy(tile_base[:, :], base_i[:, :])
                    ch.step(dve.tensor_copy(k_f[:, :], k_i[:, :]))
                    dve.wait_ge(s_load, 16 * n_loads)
                    ch.step(dve.tensor_copy(dst_f[:, :], dst_i[:, :]))
                    ch.step(dve.tensor_copy(next_f[:, :], next_i[:, :]))
                    ch.step(dve.tensor_tensor(next_f[:, :], next_f[:, :], dst_f[:, :], ALU.is_lt))
                    dve.tensor_reduce(unsorted[:, :], next_f[:, :], AX_X, ALU.add)
                    ch.step(dve.tensor_tensor(sq3[:, :, :], ea3[:, :, :], ea3[:, :, :], ALU.mult))
                    dve.tensor_reduce(nrm[:, :], sq3[:, :, :], AX_X, ALU.add).then_inc(s_sqn, 1)
                    ch.step(dve.tensor_scalar(xc[:, :], ew[:, :], 0.0, 1.0, ALU.max, ALU.min))
                    ch.step(dve.tensor_scalar(xc[:, :], xc[:, :], float(NB - 1), None, ALU.mult))
                    ch.step(dve.tensor_scalar(mask[:, :], ew[:, :], 1.0, float(NB) ** 0.5, ALU.is_le, ALU.mult))
                    ch.step(dve.tensor_tensor(emb[:, :, :], xc[:, :].unsqueeze(2).to_broadcast([R, ET, NB]),
                                              k_f[:, :].unsqueeze(1).to_broadcast([R, ET, NB]), ALU.subtract))
                    dve.tensor_tensor(emb[:, :, :], emb[:, :, :], emb[:, :, :], ALU.mult).then_inc(s_embx, 1)
                    dve.wait_ge(s_nrm, 1)
                    ch.step(dve.tensor_scalar(nrm[:, :], nrm[:, :], 1e-12, None, ALU.add))
                    ch.step(dve.reciprocal(nrm[:, :], nrm[:, :]))
                    dve.tensor_tensor(rhat[:, :, :], ea3[:, :, :], nrm[:, :].unsqueeze(2).to_broadcast([R, ET, 3]),
                                      ALU.mult)
                    dve.wait_ge(s_embe, 1)
                    dve.tensor_tensor(emb[:, :, :], emb[:, :, :], mask[:, :].unsqueeze(2).to_broadcast([R, ET, NB]),
                                      ALU.mult)
                    dve.wait_ge(s_epsmm, 1)
                    dve.tensor_scalar(eps1[:, :], p_eps[:, 0:1], 1.0, None, ALU.add)
                    dve.wait_ge(s_wload, 16 * n_wload)
                    dve.wait_ge(s_blank, 8)
                    for h in range(2):
                        rows = slice(HM * h, HM * h + HM)
                        dve.tensor_copy(w_mlp2[rows, h, :, 0:MUL],
                                        mlp2_in[rows, 0:2 * MUL].rearrange("p (q k) -> p q k", q=2))
                        for c in range(3):
                            dve.tensor_copy(w_mlp2[rows, h, :, MUL * (c + 1):MUL * (c + 2)],
                                            mlp2_in[rows, 2 * MUL:4 * MUL].rearrange("p (q k) -> p q k", q=2))
                    dve.tensor_scalar(w_up[:, :], w_up[:, :], float(MUL) ** -0.5, None, ALU.mult)
                    c_out = float(2 * MUL) ** -0.5 / 16.0
                    for w, t, head in ((w_outA, tmpA, c_out), (w_outB, tmpB, c_out * 3.0 ** 0.5)):
                        dve.tensor_scalar(w[0:MUL, 0:MUL], w[0:MUL, 0:MUL], head, None, ALU.mult)
                        for c in range(3):
                            rows = slice(MUL * (c + 1), MUL * (c + 2))
                            dve.tensor_scalar(w[rows, MUL + c:P:3], t[rows, :], c_out, None, ALU.mult)

        with ExitStack() as ctx:
            sb, pb, sem = phase(ctx)
            xg = [sb(f"xg{b}", [R, TC, D]) for b in range(ES)]
            ea = [sb(f"attr{h}", [R, 2, TC, D]) for h in range(EP)]
            mo = [sb(f"mo{h}", [R, 2, TC, MW]) for h in range(EP)]
            idx = [sb(f"idx{b}", [R, TC], I32) for b in range(ES)]
            G = 2 * TC
            low = [sb(f"low{h}", [R, G, COARSE + 1]) for h in range(EP)]
            inside = [sb(f"inside{h}", [R, G, COARSE]) for h in range(EP)]
            over = [sb(f"over{h}", [R, G]) for h in range(EP)]
            rest = [sb(f"rest{h}", [R, G]) for h in range(EP)]
            fine = [sb(f"fine{h}", [R, G, FINE]) for h in range(EP)]
            coarse_at = sb("coarse_at", [P, COARSE + 1])
            first_cf = sb("first_cf", [COARSE, FINE])
            emb_in = [sb(f"emb_in{h}", [R, P]) for h in range(EP)]
            emb_t = [sb(f"emb_t{h}", [G * NB, R]) for h in range(EP)]
            h1 = [sb(f"h1_{h}", [P, CN]) for h in range(EP)]
            h2 = [sb(f"h2_{h}", [P, CN]) for h in range(EP)]
            p_t, p_h1, p_h2, p_cnt = pb("p_t"), pb("p_h1"), pb("p_h2"), pb("p_cnt")
            g_done = [sem(f"rows_gathered{b}") for b in range(ES)]
            i_ready, i_passed = sem("index_ready"), sem("index_wait_passed")
            e_load = [sem(f"attr_loaded{h}") for h in range(EP)]
            m_sum, m_dst, m_relu = sem("messages_summed"), sem("destination_written"), sem("messages_ready")
            m_store = [sem(f"messages_stored{h}") for h in range(EP)]
            k_ready = sem("coarse_bounds_ready")
            c_low, c_in, c_over, c_rest, c_fine = (sem("low_ready"), sem("inside_ready"), sem("over_ready"),
                                                   sem("rest_ready"), sem("fine_ready"))
            c_cnt = sem("counted")
            r_blank, r_in = sem("embedding_tile_blanked"), sem("embedding_copied")
            r_t, r_tc = sem("embedding_transposed"), sem("embedding_transpose_copied")
            r_m0, r_m1 = sem("mlp0_product"), sem("mlp1_product")
            r_h1, r_h2 = sem("hidden1_ready"), sem("hidden2_ready")
            r_store = [sem(f"hidden2_stored{h}") for h in range(EP)]
            b_blank = sem("messages_blanked")

            def tiles(n, b):
                return bass.ds((n * ES + b) * TC, TC)

            def pair_tiles(n, b):
                return bass.ds((n * ES + b) * TC, G)

            with nc.Block() as block:
                @block.gpsimd
                def _(pool):
                    for h in range(EP):
                        pool.memset(mo[h][:, :, :, :], 0.0).then_inc(b_blank, 1)

                    def gather(n, b):
                        wait_reuse(pool, m_relu, (n - 1) * ES + b + 1)
                        wait_apart(pool, i_ready, n * ES + b + 1, i_passed)
                        for j in range(TC):
                            pool.indirect_dma_start(
                                out=xg[b][:, j, :], out_offset=None, in_=x,
                                in_offset=bass.IndirectOffsetOnAxis(ap=idx[b][:, j:j + 1], axis=0),
                                bounds_check=N - 1, oob_is_err=False).then_inc(g_done[b], 16)

                    run(pool, EC, (0, gather), ring=ES)

                @block.sync
                def _(sp):
                    def load(n, b):
                        if b % 2 == 0:
                            wait_reuse(sp, m_sum, (n - 1) * ES + b + 2)
                            for lo, hi in split_rows():
                                sp.dma_start(ea[b // 2][lo:hi, :, :, :].rearrange("p a j d -> p (a j) d"),
                                             ea_rows[lo:hi, pair_tiles(n, b), :]).then_inc(e_load[b // 2], 16)

                    run(sp, EC, (0, load), ring=ES)

                @block.scalar
                def _(act):
                    def messages(n, b):
                        act.wait_ge(m_sum, n * ES + b + 1)
                        if isinstance(n, int) and n == 0:
                            act.wait_ge(b_blank, EP)
                        wait_reuse(act, m_store[b // 2], n * 32)
                        act.activation(mo[b // 2][:, b % 2, :, 0:D], xg[b][:, :, :], ACT.Relu).then_inc(m_relu, 1)
                        if b % 2:
                            act.wait_ge(m_relu, n * ES + b + 1)
                            act.wait_ge(m_dst, n * ES + b + 1)
                            for lo, hi in split_rows():
                                act.dma_start(msg_rows[lo:hi, pair_tiles(n, b - 1), :],
                                              mo[b // 2][lo:hi, :, :, :].rearrange("p a j d -> p (a j) d"))\
                                    .then_inc(m_store[b // 2], 16)

                    def embedding(n, b):
                        if b % 2 == 0:
                            act.wait_ge(r_t, n * EP + b // 2 + 1)
                            wait_reuse(act, r_m0, (n - 1) * EP + b // 2 + 1)
                            act.activation(emb_t[b // 2][:, :], p_t[0:G * NB, 0:R], ACT.Copy).then_inc(r_tc, 1)

                    def hidden1(n, b):
                        if b % 2 == 0:
                            act.wait_ge(r_m0, n * EP + b // 2 + 1)
                            wait_reuse(act, r_m1, (n - 1) * EP + b // 2 + 1)
                            act.activation(h1[b // 2][:, :], p_h1[:, 0:CN], ACT.Silu, bias=b_mlp0[:, 0:1])\
                                .then_inc(r_h1, 1)

                    def hidden2(n, b):
                        if b % 2 == 0:
                            act.wait_ge(r_m1, n * EP + b // 2 + 1)
                            wait_reuse(act, r_store[b // 2], n * 16)
                            act.activation(h2[b // 2][:, :], p_h2[:, 0:CN], ACT.Silu, bias=b_mlp1[:, 0:1])\
                                .then_inc(r_h2, 1)
                            act.wait_ge(r_h2, n * EP + b // 2 + 1)
                            act.dma_start(h2_dram[bass.ds(n * EP + b // 2, 1), :, :].rearrange("a p n -> (a p) n"),
                                          h2[b // 2][:, :]).then_inc(r_store[b // 2], 16)

                    run(act, EC, (0, embedding), (1, hidden1), (2, hidden2), (0, messages), ring=ES, peeled=2)
                    for h in range(EP):
                        pairs = uses(EC // 2, h, EP)
                        act.wait_ge(m_store[h], 32 * pairs)
                        act.wait_ge(r_store[h], 16 * pairs)

                @block.vector
                def _(dve):
                    for h in range(EP):
                        dve.memset(emb_in[h][:, :], 0.0).then_inc(r_blank, 1)
                    dve.tensor_copy(coarse_at[:, 0:COARSE], tile_base[:, 0:NT:FINE]).then_inc(k_ready, 1)
                    dve.memset(coarse_at[:, COARSE:COARSE + 1], float(N)).then_inc(k_ready, 1)
                    dve.wait_ge(r_blank, EP)
                    dve.wait_ge(k_ready, 2)

                    def index(n, b):
                        wait_reuse(dve, g_done[b], n * (16 * TC))
                        dve.tensor_copy(idx[b][:, :], src_all[:, tiles(n, b)]).then_inc(i_ready, 1)

                    def embedding(n, b):
                        if b % 2 == 0:
                            wait_reuse(dve, r_t, (n - 1) * EP + b // 2 + 1)
                            dve.tensor_copy(emb_in[b // 2][:, 0:G * NB].rearrange("p (j n) -> p j n", n=NB),
                                            emb[:, pair_tiles(n, b), :]).then_inc(r_in, 1)

                    def count(n, b):
                        if b % 2 == 0:
                            h, i = b // 2, n * EP + b // 2
                            dst_p = dst_f[:, pair_tiles(n, b)]
                            wait_reuse(dve, c_cnt, i + 1 - EP)
                            dve.tensor_tensor(low[h][:, :, :], dst_p.unsqueeze(2).to_broadcast([R, G, COARSE + 1]),
                                              coarse_at[0:R, :].unsqueeze(1).to_broadcast([R, G, COARSE + 1]),
                                              ALU.is_lt).then_inc(c_low, 1)
                            dve.wait_ge(c_low, i + 1)
                            dve.tensor_tensor(inside[h][:, :, :], low[h][:, :, 1:COARSE + 1],
                                              low[h][:, :, 0:COARSE], ALU.subtract).then_inc(c_in, 1)
                            dve.tensor_reduce(over[h][:, :], low[h][:, :, 1:COARSE + 1], AX_X, ALU.add)\
                                .then_inc(c_over, 1)
                            dve.wait_ge(c_over, i + 1)
                            dve.tensor_scalar(over[h][:, :], over[h][:, :], float(R * FINE), float(-R * NT),
                                              ALU.mult, ALU.add).then_inc(c_rest, 1)
                            dve.wait_ge(c_rest, 2 * i + 1)
                            dve.tensor_tensor(rest[h][:, :], dst_p, over[h][:, :], ALU.add).then_inc(c_rest, 1)
                            dve.wait_ge(c_rest, 2 * i + 2)
                            dve.tensor_tensor(fine[h][:, :, :], rest[h][:, :].unsqueeze(2).to_broadcast([R, G, FINE]),
                                              tile_base[0:R, 0:FINE].unsqueeze(1).to_broadcast([R, G, FINE]),
                                              ALU.is_lt).then_inc(c_fine, 1)

                    def messages(n, b):
                        dve.wait_ge(g_done[b], (n + 1) * (16 * TC))
                        dve.wait_ge(e_load[b // 2], (n + 1) * 32)
                        dve.tensor_tensor(xg[b][:, :, :], xg[b][:, :, :], ea[b // 2][:, b % 2, :, :], ALU.add)\
                            .then_inc(m_sum, 1)
                        if isinstance(n, int) and n == 0:
                            dve.wait_ge(b_blank, EP)
                        wait_reuse(dve, m_store[b // 2], n * 32)
                        dve.tensor_copy(mo[b // 2][:, b % 2, :, D:D + 1], dst_f[:, tiles(n, b)].unsqueeze(2))\
                            .then_inc(m_dst, 1)

                    run(dve, EC, (0, index), (3, embedding), (3, messages), (3, count), ring=ES, peeled=2)

                @block.tensor
                def _(pe):
                    def hidden0(n, b):
                        if b % 2 == 0:
                            h, i = b // 2, n * EP + b // 2
                            pe.wait_ge(r_in, i + 1)
                            wait_reuse(pe, r_tc, i)
                            pe.transpose(p_t[:, 0:R], emb_in[h][:, :], ident[0:R, 0:R]).then_inc(r_t, 1)
                            pe.wait_ge(r_tc, i + 1)
                            wait_reuse(pe, r_h1, i)
                            for v in range(TC):
                                mm = pe.matmul(p_h1[:, v * R:(v + 1) * R], w_mlp0[:, v, :], emb_t[h][:, :],
                                               start=True, stop=True)
                            mm.then_inc(r_m0, 1)

                    def hidden1(n, b):
                        if b % 2 == 0:
                            h, i = b // 2, n * EP + b // 2
                            pe.wait_ge(r_h1, i + 1)
                            wait_reuse(pe, r_h2, i)
                            pe.matmul(p_h2[:, 0:CN], w_mlp1[:, :], h1[h][:, :], start=True, stop=True)\
                                .then_inc(r_m1, 1)

                    def count(n, b):
                        if b % 2 == 0:
                            h, i = b // 2, n * EP + b // 2
                            pe.wait_ge(c_in, i + 1)
                            pe.wait_ge(c_fine, i + 1)
                            for j in range(G):
                                pe.matmul(p_cnt[0:COARSE, 0:FINE], low[h][:, j, 0:COARSE], ones[0:R, 0:FINE],
                                          start=False, stop=False, skip_group_check=True)
                                mm = pe.matmul(p_cnt[0:COARSE, 0:FINE], inside[h][:, j, :], fine[h][:, j, :],
                                               start=False, stop=False, skip_group_check=True)
                            mm.then_inc(c_cnt, 1)

                    pe.wait_ge(r_blank, 1)
                    pe.matmul(p_cnt[0:COARSE, 0:FINE], emb_in[0][:, P - COARSE:P], ones[0:R, 0:FINE], start=True,
                              stop=False, skip_group_check=True)
                    run(pe, EC, (0, hidden0), (1, hidden1), (1, count), ring=ES)

            s_cnt, s_cf, s_out, s_in = sem("unsorted_summed"), sem("counts_copied"), sem("counts_out"), sem("counts_in")
            s_step = sem("tables_step")
            first = sb("first", [1, NT + 1])
            size = sb("size", [1, NT])
            flags = sb("flags", [1, 2])
            with nc.Block() as block:
                @block.tensor
                def _(pe):
                    pe.matmul(p_t[0:1, 0:1], ones[0:R, 0:1], unsorted[:, :], start=True, stop=True)\
                        .then_inc(s_cnt, 1)

                @block.sync
                def _(sp):
                    sp.wait_ge(s_cf, 1)
                    sp.dma_start(first_dram[:, :], first_cf[:, :]).then_inc(s_out, 16)
                    sp.wait_ge(s_out, 16)
                    sp.dma_start(first[:, 0:NT], first_dram.rearrange("(o c) f -> o (c f)", o=1)).then_inc(s_in, 16)

                @block.vector
                def _(dve):
                    ch = Chain(dve, s_step)
                    dve.tensor_copy(first_cf[:, :], p_cnt[0:COARSE, 0:FINE]).then_inc(s_cf, 1)
                    dve.wait_ge(s_cnt, 1)
                    ch.step(dve.memset(first[:, NT:NT + 1], float(E)))
                    ch.step(dve.tensor_scalar(flags[:, 1:2], p_t[0:1, 0:1], 0.0, None, ALU.is_gt))
                    dve.wait_ge(s_in, 16)
                    ch.step(dve.tensor_tensor(size[:, :], first[:, 1:NT + 1], first[:, 0:NT], ALU.subtract))
                    ch.step(dve.tensor_reduce(flags[:, 0:1], size[:, :], AX_X, ALU.max))
                    ch.step(dve.tensor_scalar(flags[:, 0:1], flags[:, 0:1], float(WIN), None, ALU.is_gt))
                    ch.step(dve.tensor_tensor(flags[:, 0:1], flags[:, 0:1], flags[:, 1:2], ALU.max))
                    ch.step(dve.tensor_copy(slow_i[:, :], flags[:, 0:1]))
                    ch.step(dve.tensor_scalar(size[:, :], first[:, 0:NT], -1.0, float(E), ALU.mult, ALU.add))
                    ch.step(dve.scalar_tensor_tensor(out=size[:, :], in0=size[:, :], scalar=flags[:, 0:1],
                                                     in1=first[:, 0:NT], op0=ALU.mult, op1=ALU.add))
                    ch.step(dve.tensor_copy(starts[:, :], size[:, :]))

        def slow_path(layer):
            with ExitStack() as ctx:
                sb, pb, sem = phase(ctx)
                zero = sb(f"slow{layer}_zero", [R, TC, D])
                below = sb(f"slow{layer}_below", [R, R])
                rows = sb(f"slow{layer}_rows", [R, MW])
                dmat = sb(f"slow{layer}_dmat", [R, P])
                same = sb(f"slow{layer}_same", [R, R])
                earlier = sb(f"slow{layer}_earlier", [R, R])
                place = sb(f"slow{layer}_place", [R, 2])
                at = sb(f"slow{layer}_at", [R, 2], I32)
                held = sb(f"slow{layer}_held", [R, D])
                total = sb(f"slow{layer}_total", [R, D])
                p_d, p_s = pb(f"slow{layer}_p_d"), pb(f"slow{layer}_p_s")
                s_blank = sem(f"slow{layer}_blanked")
                s_zero = sem(f"slow{layer}_zeroed")
                s_below = sem(f"slow{layer}_below_ready")
                s_rows = sem(f"slow{layer}_rows_loaded")
                s_dmat, s_dt = sem(f"slow{layer}_dmat_ready"), sem(f"slow{layer}_dmat_transposed")
                s_same, s_sum = sem(f"slow{layer}_same_ready"), sem(f"slow{layer}_summed")
                s_step = sem(f"slow{layer}_dve_step")
                s_at, s_got = sem(f"slow{layer}_index_ready"), sem(f"slow{layer}_held_loaded")
                s_tot, s_put = sem(f"slow{layer}_total_ready"), sem(f"slow{layer}_total_stored")
                s_pass = sem(f"slow{layer}_wait_passed")
                steps = 6

                with nc.Block() as block:
                    @block.sync
                    def _(sp):
                        with sp.If(sp.value_load(slow_i[0:1, 0:1], min_val=0, max_val=1) > 0):
                            sp.wait_ge(s_blank, 1)

                            def blank(k):
                                for lo, hi in split_rows():
                                    sp.dma_start(agg_tiles[lo:hi, bass.ds(k * TC, TC), :], zero[lo:hi, :, :])\
                                        .then_inc(s_zero, 16)

                            with sp.Fori(0, NC) as k:
                                blank(k)

                            def load(t):
                                wait_reuse(sp, s_put, t * 16)
                                sp.dma_start(rows[:, :], msg[bass.ds(t * R, R), :]).then_inc(s_rows, 16)

                            load(0)
                            with sp.Fori(1, ET) as t:
                                load(t)

                    @block.gpsimd
                    def _(pool):
                        with pool.If(pool.value_load(slow_i[0:1, 0:1], min_val=0, max_val=1) > 0):
                            pool.memset(below[:, :], 1.0).then_inc(s_pass, 1)
                            pool.wait_ge(s_pass, 1)
                            pool.affine_select(out=below[:, :], in_=below[:, :], compare_op=ALU.is_gt, fill=0.0,
                                               base=0, pattern=[[-1, R]], channel_multiplier=1).then_inc(s_below, 1)
                            pool.wait_ge(s_zero, 32 * NC)

                            def update(t):
                                wait_apart(pool, s_at, t + 1, s_pass)
                                pool.indirect_dma_start(
                                    out=held[:, :], out_offset=None, in_=agg,
                                    in_offset=bass.IndirectOffsetOnAxis(ap=at[:, 0:1], axis=0),
                                    bounds_check=N - 1, oob_is_err=False).then_inc(s_got, 16)
                                wait_apart(pool, s_tot, t + 1, s_pass)
                                pool.indirect_dma_start(
                                    out=agg, out_offset=bass.IndirectOffsetOnAxis(ap=at[:, 1:2], axis=0),
                                    in_=held[:, :], in_offset=None,
                                    bounds_check=N - 1, oob_is_err=False).then_inc(s_put, 16)

                            update(0)
                            with pool.Fori(1, ET) as t:
                                update(t)
                            pool.wait_ge(s_put, 16 * ET)

                    @block.tensor
                    def _(pe):
                        with pe.If(pe.value_load(slow_i[0:1, 0:1], min_val=0, max_val=1) > 0):
                            def sums(t):
                                pe.wait_ge(s_dmat, t + 1)
                                pe.transpose(p_d[:, 0:R], dmat[:, :], ident[0:R, 0:R]).then_inc(s_dt, 1)
                                pe.wait_ge(s_same, t + 1)
                                pe.matmul(p_s[0:R, 0:D], same[:, :], rows[:, 0:D], start=True, stop=True)\
                                    .then_inc(s_sum, 1)

                            sums(0)
                            with pe.Fori(1, ET) as t:
                                sums(t)

                    @block.vector
                    def _(dve):
                        with dve.If(dve.value_load(slow_i[0:1, 0:1], min_val=0, max_val=1) > 0):
                            dve.memset(zero[:, :, :], 0.0).then_inc(s_blank, 1)

                            def combine(t):
                                def step(n, ins):
                                    ins.then_inc(s_step, 1)
                                    dve.wait_ge(s_step, t * steps + n)

                                dve.wait_ge(s_rows, (t + 1) * 16)
                                dve.tensor_copy(dmat[:, :], rows[:, D:D + 1].to_broadcast([R, P])).then_inc(s_dmat, 1)
                                dve.wait_ge(s_dt, t + 1)
                                dve.tensor_scalar(same[:, :], p_d[0:R, 0:R], rows[:, D:D + 1], None, ALU.is_equal)\
                                    .then_inc(s_same, 1)
                                dve.wait_ge(s_same, t + 1)
                                dve.wait_ge(s_below, 1)
                                step(1, dve.tensor_tensor(earlier[:, :], same[:, :], below[:, :], ALU.mult))
                                step(2, dve.tensor_reduce(place[:, 0:1], earlier[:, :], AX_X, ALU.add))
                                step(3, dve.tensor_scalar(place[:, 1:2], place[:, 0:1], float(NO_ROW), None, ALU.mult))
                                step(4, dve.tensor_tensor(place[:, 1:2], place[:, 1:2], rows[:, D:D + 1], ALU.add))
                                step(5, dve.tensor_copy(at[:, 1:2], place[:, 1:2]))
                                dve.tensor_copy(at[:, 0:1], rows[:, D:D + 1]).then_inc(s_at, 1)
                                dve.wait_ge(s_sum, t + 1)
                                step(6, dve.tensor_copy(total[:, :], p_s[0:R, 0:D]))
                                dve.wait_ge(s_got, (t + 1) * 16)
                                dve.tensor_tensor(held[:, :], held[:, :], total[:, :], ALU.add).then_inc(s_tot, 1)

                            combine(0)
                            with dve.Fori(1, ET) as t:
                                combine(t)

        def either(eng, program):
            with eng.If(eng.value_load(slow_i[0:1, 0:1], min_val=0, max_val=1) > 0):
                program(True)
            with eng.Else():
                program(False)

        def load_windows(eng, engine, which, win, w_load, a_done, n, b):
            if b % 2 == 0:
                wait_reuse(eng, a_done, (n - 1) * S + b + 2)
                _, rows = nc.values_load_multi_w_load_instructions(
                    starts[0:1, bass.ds((n * S + b) * TC, 2 * TC)], engines=(engine,), min_val=0, max_val=E,
                    skip_runtime_bounds_check_because="a count of the E edges, made on the chip from compares")
                for c in range(2):
                    for j in which:
                        eng.dma_start(win[b + c][:, j, :], msg[bass.ds(rows[c * TC + j], WIN), :])\
                            .then_inc(w_load[b + c], 16)

        def load_quad(eng, into, tiled, loaded, used, n, b, passed=None):
            if b % QD == 0:
                if passed is None:
                    wait_reuse(eng, used, (n - 1) * S + b + QD)
                else:
                    wait_reuse_apart(eng, used, (n - 1) * S + b + QD, passed)
                for lo, hi in split_rows():
                    eng.dma_start(into[b // QD][lo:hi, :, :, :].rearrange("p a j d -> p (a j) d"),
                                  tiled[lo:hi, bass.ds((n * S + b) * TC, QD * TC), :])\
                        .then_inc(loaded[b // QD], 16)

        def load_sums(eng, into, loaded, used, n, b):
            if b % QD == 0:
                wait_reuse(eng, used, n * S + b)
                for lo, hi in split_rows():
                    eng.dma_start(into[lo:hi, :, :, :].rearrange("p a j d -> p (a j) d"),
                                  agg_tiles[lo:hi, bass.ds((n * S + b) * TC, QD * TC), :]).then_inc(loaded, 16)

        slow_path(0)

        keep = ExitStack()
        kept = keep.enter_context(nc.sbuf_tensor("kept", [P, -(-NC // KEEP), CN], F32))

        def kept_chunk(n, b):
            return kept[:, bass.ds(n * (S // KEEP) + b // KEEP, 1), :].rearrange("p a n -> p (a n)")

        stored = [b for b in range(S) if b % KEEP]

        def stored_before(n, b):
            return n * len(stored) + stored.index(b)

        with ExitStack() as ctx:
            sb, pb, sem = phase(ctx)
            xs = [sb(f"xs{h}", [R, QD, TC, D]) for h in range(QS)]
            ax = sb("ax", [R, QD, TC, D])
            win = [sb(f"win{b}", [WIN, TC, MW]) for b in range(S)]
            local = [sb(f"local{b}", [WIN, TC]) for b in range(S)]
            hot = [sb(f"hot{b}", [WIN, TC, R]) for b in range(S)]
            z = [sb(f"z{b}", [R, TC, D + 4]) for b in range(4)]
            zt = {b: sb(f"zt{b}", [P, CN]) for b in stored}
            zero = sb("zero", [R, D + 4])
            p_agg = [pb(f"p_agg{b}") for b in range(2)]
            p_zt = [pb(f"p_zt{b}") for b in range(2)]
            p_gram = pb("p_gram")
            x_load = [sem(f"nodes_loaded{h}") for h in range(QS)]
            s_load = sem("slow_sums_loaded")
            w_load = [sem(f"windows_loaded{b}") for b in range(S)]
            l_ready, o_ready, a_done = sem("local_ready"), sem("one_hot_ready"), sem("messages_added")
            z_ready, z_used, t_copied = sem("z_ready"), sem("z_used"), sem("z_transpose_copied")
            t_store = {b: sem(f"z_stored{b}") for b in stored}
            z_blank, z_passed = sem("z_blanked"), sem("z_wait_passed")
            with nc.Block() as block:
                @block.sync
                def _(sp):
                    def program(slow):
                        def load(n, b):
                            load_quad(sp, xs, x_tiles, x_load, z_ready, n, b)
                            load_windows(sp, mybir.EngineType.SP, range(0, 2), win, w_load, a_done, n, b)
                            if slow:
                                load_sums(sp, ax, s_load, z_ready, n, b)

                        run(sp, NC, (0, load))

                    either(sp, program)

                @block.gpsimd
                def _(pool):
                    def store(n, b):
                        if b in stored:
                            pool.wait_ge(t_copied, n * S + b + 1)
                            pool.dma_start(zt_dram[bass.ds(n * S + b, 1), :, :].rearrange("a p n -> (a p) n"),
                                           zt[b][:, :]).then_inc(t_store[b], 16)

                    run(pool, NC, (0, store))
                    for b in stored:
                        pool.wait_ge(t_store[b], 16 * uses(NC, b, S))

                @block.vector
                def _(dve):
                    dve.memset(zero[:, :], 0.0).then_inc(z_blank, 1)
                    for b in range(4):
                        dve.memset(z[b][:, :, D:D + 4], 1.0).then_inc(z_blank, 1)

                    def program(slow):
                        def one_hot(n, b):
                            dve.wait_ge(w_load[b], (n + 1) * (16 * TC))
                            wait_reuse(dve, o_ready, (n - 1) * S + b + 1)
                            dve.tensor_tensor(local[b][:, :].unsqueeze(2), win[b][:, :, D:D + 1],
                                              tile_base[0:WIN, bass.ds((n * S + b) * TC, TC)].unsqueeze(2),
                                              ALU.subtract).then_inc(l_ready, 1)
                            wait_reuse(dve, a_done, (n - 1) * S + b + 1)
                            dve.wait_ge(l_ready, n * S + b + 1)
                            shape = [WIN, TC, R]
                            dve.tensor_tensor(hot[b][:, :, :], node_iota[0:WIN, :].unsqueeze(1).to_broadcast(shape),
                                              local[b][:, :].unsqueeze(2).to_broadcast(shape), ALU.is_equal)\
                                .then_inc(o_ready, 1)

                        def z_sum(n, b):
                            h = b // QD
                            dve.wait_ge(x_load[h], (n + 1) * 32)
                            dve.wait_ge(a_done, n * S + b + 1)
                            if slow:
                                dve.wait_ge(s_load, (n * QS + h + 1) * 32)
                            wait_reuse(dve, z_used, n * S + b - 3)
                            dve.scalar_tensor_tensor(
                                out=z[b % 4][:, :, 0:D], in0=xs[h][:, b % QD, :, :], scalar=eps1[0:R, 0:1],
                                in1=ax[:, b % QD, :, :] if slow
                                else p_agg[b % 2][0:R, :].rearrange("p (j d) -> p j d", d=D),
                                op0=ALU.mult, op1=ALU.add).then_inc(z_ready, 1)

                        run(dve, NC, (0, one_hot), (1, z_sum), peeled=2)

                    either(dve, program)

                @block.tensor
                def _(pe):
                    def aggregate(n, b):
                        pe.wait_ge(o_ready, n * S + b + 1)
                        wait_reuse(pe, z_ready, n * S + b - 1)
                        for j in range(TC):
                            mm = pe.matmul(p_agg[b % 2][0:R, j * D:(j + 1) * D], hot[b][:, j, :],
                                           win[b][:, j, 0:D], start=True, stop=True)
                        mm.then_inc(a_done, 1)

                    def moments(n, b):
                        pe.wait_ge(z_ready, n * S + b + 1)
                        for j in range(TC):
                            pe.matmul(p_gram[:, 0:D + 1], z[b % 4][:, j, 0:D], z[b % 4][:, j, 0:D + 1],
                                      start=False, stop=False, skip_group_check=True)
                        wait_reuse(pe, t_copied, n * S + b - 1)
                        for j in range(TC):
                            mm = pe.transpose(p_zt[b % 2][:, j * R:(j + 1) * R], z[b % 4][:, j, 0:D], ident[0:R, 0:R])
                        mm.then_inc(z_used, 1)

                    pe.wait_ge(z_blank, 1 + 4)
                    pe.matmul(p_gram[:, 0:D + 1], zero[:, 0:D], zero[:, 0:D + 1], start=True, stop=False,
                              skip_group_check=True)
                    run(pe, NC, (0, aggregate), (1, moments))

                @block.scalar
                def _(act):
                    def copy(n, b):
                        if b in stored:
                            act.wait_ge(z_used, n * S + b + 1)
                            wait_reuse(act, t_store[b], n * 16)
                            into = zt[b][:, :]
                        else:
                            wait_apart(act, z_used, n * S + b + 1, z_passed)
                            into = kept_chunk(n, b)
                        act.activation(into, p_zt[b % 2][:, 0:CN], ACT.Copy).then_inc(t_copied, 1)

                    def load(n, b):
                        load_windows(act, mybir.EngineType.Activation, range(2, TC), win, w_load, a_done, n, b)

                    run(act, NC, (0, load), (AHEAD + 2, copy), peeled=2)

            cov = sb("cov", [P, D])
            mean = sb("mean", [P, 1])
            mean_row = sb("mean_row", [1, P])
            neg_row = sb("neg_row", [1, P])
            wc = sb("wc", [P, H])
            var1, mean1 = sb("var1", [P, 2]), sb("mean1", [P, 2])
            p_s = pb("p_s")
            p_row = pb("p_row")
            s_step = sem("bn1_dve_step")
            s_mean, s_row, s_rowc = sem("mean_ready"), sem("mean_transposed"), sem("mean_row_ready")
            s_outer, s_cov, s_cw, s_wc = sem("outer_added"), sem("cov_ready"), sem("cov_w"), sem("w_cov_w")
            s_var, s_std, s_sq = sem("moments_ready"), sem("variance_ready"), sem("std_ready")
            with nc.Block() as block:
                @block.tensor
                def _(pe):
                    pe.wait_ge(s_mean, 1)
                    pe.transpose(p_row[0:1, 0:P], mean[:, :], ident[:, :]).then_inc(s_row, 1)
                    pe.wait_ge(s_rowc, 2)
                    pe.matmul(p_s[:, 0:D], neg_row[:, :], mean_row[:, :], start=True, stop=True)\
                        .then_inc(s_outer, 1)
                    pe.wait_ge(s_cov, 1)
                    pe.matmul(p_row[:, 0:H], cov[:, :], w1[:, :], start=True, stop=True).then_inc(s_cw, 1)
                    pe.wait_ge(s_wc, 1)
                    for h in range(2):
                        pe.matmul(p_s[:, h:h + 1], wc[:, h * P:(h + 1) * P], ones[:, 0:1], start=True, stop=True)
                        mm = pe.matmul(p_s[:, 2 + h:3 + h], w1[:, h * P:(h + 1) * P], mean[:, :],
                                       start=True, stop=True)
                    mm.then_inc(s_var, 1)

                @block.vector
                def _(dve):
                    ch = Chain(dve, s_step)
                    dve.tensor_scalar(mean[:, :], p_gram[:, D:D + 1], 1.0 / N, None, ALU.mult).then_inc(s_mean, 1)
                    dve.wait_ge(s_row, 1)
                    dve.tensor_copy(mean_row[:, :], p_row[0:1, 0:P]).then_inc(s_rowc, 1)
                    dve.tensor_scalar(neg_row[:, :], p_row[0:1, 0:P], -1.0, None, ALU.mult).then_inc(s_rowc, 1)
                    ch.step(dve.tensor_scalar(cov[:, :], p_gram[:, 0:D], 1.0 / N, None, ALU.mult))
                    dve.wait_ge(s_outer, 1)
                    dve.tensor_tensor(cov[:, :], cov[:, :], p_s[:, 0:D], ALU.add).then_inc(s_cov, 1)
                    dve.wait_ge(s_cw, 1)
                    dve.tensor_tensor(wc[:, :], w1[:, :], p_row[:, 0:H], ALU.mult).then_inc(s_wc, 1)
                    dve.wait_ge(s_var, 1)
                    ch.step(dve.tensor_copy(mean1[:, :], p_s[:, 2:4]))
                    dve.tensor_scalar(var1[:, :], p_s[:, 0:2], BN_EPS, None, ALU.add).then_inc(s_std, 1)
                    dve.wait_ge(s_sq, 1)
                    ch.step(dve.reciprocal(var1[:, :], var1[:, :]))
                    ch.step(dve.tensor_tensor(scale1[:, :], g1c[:, :], var1[:, :], ALU.mult))
                    ch.step(dve.tensor_tensor(mean1[:, :], mean1[:, :], scale1[:, :], ALU.mult))
                    ch.step(dve.tensor_tensor(shift1[:, :], b1c[:, :], mean1[:, :], ALU.subtract))

                @block.scalar
                def _(act):
                    act.wait_ge(s_std, 1)
                    act.activation(var1[:, :], var1[:, :], ACT.Sqrt).then_inc(s_sq, 1)

        with ExitStack() as ctx:
            sb, pb, sem = phase(ctx)
            zt = {b: sb(f"zt_in{b}", [P, CN]) for b in stored}
            z_hi = [sb(f"zt_rounded{b}", [P, CN], F32R) for b in range(4)]
            z_lo = [sb(f"zt_rest{b}", [P, CN], F32R) for b in range(4)]
            hid = [sb(f"hid{b}", [P, 2, CN]) for b in range(4)]
            hid_hi = [sb(f"hid_rounded{b}", [P, 2, CN], F32R) for b in range(4)]
            hid_lo = [sb(f"hid_rest{b}", [P, 2, CN], F32R) for b in range(4)]
            w1_hi, w1_lo = sb("w1_rounded", [P, H], F32R), sb("w1_rest", [P, H], F32R)
            w2_hi, w2_lo = sb("w2_rounded", [P, 2, D], F32R), sb("w2_rest", [P, 2, D], F32R)
            y = {b: sb(f"y{b}", [P, CN]) for b in stored}
            stats = sb("stats", [P, NC, 6])
            p_h = [[pb(f"p_h{b}{h}") for h in range(2)] for b in range(2)]
            p_y = [pb(f"p_y{b}") for b in range(4)]
            t_load = {b: sem(f"zt_loaded{b}") for b in stored}
            w_hi, w_lo = sem("weights_rounded"), sem("weight_rests_ready")
            z_hi_ready, z_lo_ready, z_passed = sem("z_rounded"), sem("z_rest_ready"), sem("z_kept_wait_passed")
            h_prod, h_ready = sem("hidden_product"), sem("hidden_ready")
            h_hi_ready, h_lo_ready = sem("hidden_rounded"), sem("hidden_rest_ready")
            y_prod, y_stats, y_copied = sem("y_product"), sem("y_moments"), sem("y_copied")
            y_store = {b: sem(f"y_stored{b}") for b in stored}

            def z_in(n, b):
                return zt[b][:, :] if b in stored else kept_chunk(n, b)

            with nc.Block() as block:
                @block.sync
                def _(sp):
                    def load(n, b):
                        if b in stored:
                            wait_reuse(sp, z_lo_ready, (n - 1) * S + b + 1)
                            sp.dma_start(zt[b][:, :],
                                         zt_dram[bass.ds(n * S + b, 1), :, :].rearrange("a p n -> (a p) n"))\
                                .then_inc(t_load[b], 16)

                    run(sp, NC, (0, load))

                @block.gpsimd
                def _(pool):
                    def rest_of_z(n, b):
                        pool.wait_ge(z_hi_ready, n * S + b + 1)
                        wait_reuse(pool, h_prod, n * S + b - 3)
                        pool.tensor_tensor(z_lo[b % 4][:, :], z_in(n, b), z_hi[b % 4][:, :], ALU.subtract)\
                            .then_inc(z_lo_ready, 1)

                    run(pool, NC, (0, rest_of_z))

                @block.tensor
                def _(pe):
                    def up(n, b):
                        pe.wait_ge(z_lo_ready, n * S + b + 1)
                        wait_reuse(pe, h_ready, n * S + b - 1)
                        c = b % 4
                        for h in range(2):
                            cols = slice(h * P, (h + 1) * P)
                            for k, (w, v) in enumerate(((w1_hi, z_hi), (w1_hi, z_lo), (w1_lo, z_hi))):
                                mm = pe.matmul(p_h[b % 2][h][:, 0:CN], w[:, cols], v[c][:, :],
                                               start=(k == 0), stop=(k == 2))
                        mm.then_inc(h_prod, 1)

                    def down(n, b):
                        pe.wait_ge(h_lo_ready, n * S + b + 1)
                        wait_reuse(pe, y_copied, n * S + b - 3)
                        c = b % 4
                        parts = [(w, v, h) for h in range(2)
                                 for w, v in ((w2_hi, hid_hi), (w2_hi, hid_lo), (w2_lo, hid_hi))]
                        for k, (w, v, h) in enumerate(parts):
                            mm = pe.matmul(p_y[c][:, 0:CN], w[:, h, :], v[c][:, h, :],
                                           start=(k == 0), stop=(k == len(parts) - 1))
                        mm.then_inc(y_prod, 1)

                    pe.wait_ge(w_lo, 2)
                    run(pe, NC, (0, up), (LAG_DOWN, down))

                @block.scalar
                def _(act):
                    def round_z(n, b):
                        if b in stored:
                            act.wait_ge(t_load[b], (n + 1) * 16)
                            wait_reuse(act, h_prod, n * S + b - 3)
                        else:
                            wait_reuse_apart(act, h_prod, n * S + b - 3, z_passed)
                        act.activation(z_hi[b % 4][:, :], z_in(n, b), ACT.Copy).then_inc(z_hi_ready, 1)

                    def relu(n, b):
                        act.wait_ge(h_prod, n * S + b + 1)
                        wait_reuse(act, h_lo_ready, n * S + b - 3)
                        for h in range(2):
                            ins = act.activation(hid[b % 4][:, h, :], p_h[b % 2][h][:, 0:CN], ACT.Relu,
                                                 bias=shift1[:, h:h + 1], scale=scale1[:, h:h + 1])
                        ins.then_inc(h_ready, 1)

                    def copy(n, b):
                        if b in stored:
                            act.wait_ge(y_stats, n * S + b + 1)
                            wait_reuse(act, y_store[b], n * 16)
                            into = y[b][:, :]
                        else:
                            wait_apart(act, y_stats, n * S + b + 1, z_passed)
                            into = kept_chunk(n, b)
                        act.activation(into, p_y[b % 4][:, 0:CN], ACT.Copy).then_inc(y_copied, 1)

                    def store(n, b):
                        if b in stored:
                            act.wait_ge(y_copied, n * S + b + 1)
                            act.dma_start(zt_dram[bass.ds(n * S + b, 1), :, :].rearrange("a p n -> (a p) n"),
                                          y[b][:, :]).then_inc(y_store[b], 16)

                    run(act, NC, (0, round_z), (2, relu), (LAG_DOWN + 3, copy), (LAG_DOWN + 4, store), peeled=2)
                    for b in stored:
                        act.wait_ge(y_store[b], 16 * uses(NC, b, S))

                @block.vector
                def _(dve):
                    dve.tensor_copy(w1_hi[:, :], w1[:, :]).then_inc(w_hi, 1)
                    dve.tensor_copy(w2_hi[:, :, :], w2[:, :, :]).then_inc(w_hi, 1)
                    dve.wait_ge(w_hi, 2)
                    dve.tensor_tensor(w1_lo[:, :], w1[:, :], w1_hi[:, :], ALU.subtract).then_inc(w_lo, 1)
                    dve.tensor_tensor(w2_lo[:, :, :], w2[:, :, :], w2_hi[:, :, :], ALU.subtract).then_inc(w_lo, 1)

                    def round_hidden(n, b):
                        dve.wait_ge(h_ready, n * S + b + 1)
                        wait_reuse(dve, y_prod, n * S + b - 3)
                        dve.tensor_copy(hid_hi[b % 4][:, :, :], hid[b % 4][:, :, :]).then_inc(h_hi_ready, 1)

                    def rest_of_hidden(n, b):
                        dve.wait_ge(h_hi_ready, n * S + b + 1)
                        dve.tensor_tensor(hid_lo[b % 4][:, :, :], hid[b % 4][:, :, :], hid_hi[b % 4][:, :, :],
                                          ALU.subtract).then_inc(h_lo_ready, 1)

                    def moments(n, b):
                        dve.wait_ge(y_prod, n * S + b + 1)
                        dve.bn_stats(stats[:, bass.ds(n * S + b, 1), :].rearrange("p a n -> p (a n)"),
                                     p_y[b % 4][:, 0:CN]).then_inc(y_stats, 1)

                    run(dve, NC, (0, round_hidden), (LAG_DOWN, moments), (0, rest_of_hidden))

            mv = sb("mv", [P, 2])
            s_agg, s_std, s_sq = sem("moments2"), sem("variance2"), sem("std2")
            s_step = sem("bn2_dve_step")
            with nc.Block() as block:
                @block.vector
                def _(dve):
                    ch = Chain(dve, s_step)
                    ch.step(dve.bn_aggr(mv[:, :], stats[:, :, :].rearrange("p a n -> p (a n)")))
                    dve.tensor_scalar(mv[:, 1:2], mv[:, 1:2], BN_EPS, None, ALU.add).then_inc(s_std, 1)
                    dve.wait_ge(s_sq, 1)
                    ch.step(dve.reciprocal(mv[:, 1:2], mv[:, 1:2]))
                    ch.step(dve.tensor_tensor(scale2[:, :], g2c[:, :], mv[:, 1:2], ALU.mult))
                    ch.step(dve.tensor_tensor(mv[:, 0:1], mv[:, 0:1], scale2[:, :], ALU.mult))
                    ch.step(dve.tensor_tensor(shift2[:, :], b2c[:, :], mv[:, 0:1], ALU.subtract))
                    dve.tensor_scalar(scale2[:, :], scale2[:, :], 0.5, None, ALU.mult)
                    dve.tensor_scalar(shift2[:, :], shift2[:, :], 0.5, None, ALU.mult)

                @block.scalar
                def _(act):
                    act.wait_ge(s_std, 1)
                    act.activation(mv[:, 1:2], mv[:, 1:2], ACT.Sqrt).then_inc(s_sq, 1)

        class Norm:

            def __init__(self, tag, sb, sem, out_tiles, eps):
                self.u = [sb(f"{tag}_u{b}", [R, TC, D]) for b in range(S)]
                self.o = [sb(f"{tag}_o{h}", [R, QD, TC, D]) for h in range(QS)]
                self.st = [sb(f"{tag}_st{b}", [R, TC, 6]) for b in range(S)]
                self.mv = [sb(f"{tag}_mv{b}", [R, TC, 2]) for b in range(S)]
                self.nb = [sb(f"{tag}_nb{b}", [R, TC]) for b in range(S)]
                self.out_tiles, self.eps = out_tiles, eps
                self.passed = sem(f"{tag}_wait_passed")
                self.u_ready, self.s_ready = sem(f"{tag}_sum_ready"), sem(f"{tag}_stats_ready")
                self.v_ready, self.q_ready = sem(f"{tag}_variance_ready"), sem(f"{tag}_sqrt_ready")
                self.r_ready, self.f_ready = sem(f"{tag}_rstd_ready"), sem(f"{tag}_factors_ready")
                self.o_ready, self.a_ready = sem(f"{tag}_norm_ready"), sem(f"{tag}_aggregated")
                self.o_store = [sem(f"{tag}_stored{h}") for h in range(QS)]

            def dve_run(self, dve, *stages):
                lag = stages[-1][0]
                run(dve, NC, *stages, (lag + 1, lambda n, b: self.aggregate(dve, n, b)),
                    (lag + 2, lambda n, b: self.invert(dve, n, b)), (lag, lambda n, b: self.moments(dve, n, b)),
                    (lag + 1, lambda n, b: self.variance(dve, n, b)), (lag + 2, lambda n, b: self.offset(dve, n, b)),
                    peeled=2 if lag else 1)

            def moments(self, dve, n, b):
                dve.wait_ge(self.u_ready, n * S + b + 1)
                for j in range(TC):
                    ins = dve.bn_stats(self.st[b][:, j, :], self.u[b][:, j, :])
                ins.then_inc(self.s_ready, 1)

            def aggregate(self, dve, n, b):
                wait_apart(dve, self.s_ready, n * S + b + 1, self.passed)
                for j in range(TC):
                    ins = dve.bn_aggr(self.mv[b][:, j, :], self.st[b][:, j, :])
                ins.then_inc(self.a_ready, 1)

            def variance(self, dve, n, b):
                dve.wait_ge(self.a_ready, n * S + b + 1)
                dve.tensor_scalar(self.mv[b][:, :, 1:2], self.mv[b][:, :, 1:2], self.eps, None, ALU.add)\
                    .then_inc(self.v_ready, 1)

            def root(self, act, n, b):
                act.wait_ge(self.v_ready, n * S + b + 1)
                act.activation(self.mv[b][:, :, 1:2], self.mv[b][:, :, 1:2], ACT.Sqrt).then_inc(self.q_ready, 1)

            def invert(self, dve, n, b):
                dve.wait_ge(self.q_ready, n * S + b + 1)
                dve.reciprocal(self.mv[b][:, :, 1:2], self.mv[b][:, :, 1:2]).then_inc(self.r_ready, 1)

            def offset(self, dve, n, b):
                dve.wait_ge(self.r_ready, n * S + b + 1)
                dve.scalar_tensor_tensor(out=self.nb[b][:, :].unsqueeze(2), in0=self.mv[b][:, :, 0:1], scalar=-1.0,
                                         in1=self.mv[b][:, :, 1:2], op0=ALU.mult, op1=ALU.mult)\
                    .then_inc(self.f_ready, 1)

            def scale(self, act, n, b):
                act.wait_ge(self.f_ready, n * S + b + 1)
                wait_reuse(act, self.o_store[b // QD], n * 32)
                for j in range(TC):
                    ins = act.activation(self.o[b // QD][:, b % QD, j, :], self.u[b][:, j, :], ACT.Identity,
                                         bias=self.nb[b][:, j:j + 1], scale=self.mv[b][:, j, 1:2])
                ins.then_inc(self.o_ready, 1)

            def store(self, eng, n, b):
                if b % QD == QD - 1:
                    eng.wait_ge(self.o_ready, n * S + b + 1)
                    for lo, hi in split_rows():
                        eng.dma_start(self.out_tiles[lo:hi, bass.ds((n * S + b - QD + 1) * TC, QD * TC), :],
                                      self.o[b // QD][lo:hi, :, :, :].rearrange("p a j d -> p (a j) d"))\
                            .then_inc(self.o_store[b // QD], 16)

            def stored(self, eng):
                for h in range(QS):
                    eng.wait_ge(self.o_store[h], 32 * uses(NC // QD, h, QS))

        with ExitStack() as ctx:
            sb, pb, sem = phase(ctx)
            yt = {b: sb(f"yt{b}", [P, CN]) for b in stored}
            xs = [sb(f"x2s{h}", [R, QD, TC, D]) for h in range(QS)]
            r = [sb(f"r{b}", [P, CN]) for b in range(6)]
            p_r = [pb(f"p_r{b}") for b in range(4)]
            y_load = {b: sem(f"y_loaded{b}") for b in stored}
            x_load = [sem(f"x_loaded{h}") for h in range(QS)]
            r_ready, k_ready = sem("bn_of_stored_ready"), sem("bn_of_kept_ready")
            t_done, y_passed, k_passed = sem("bn_transposed"), sem("y_wait_passed"), sem("kept_wait_passed")
            norm = Norm("norm0", sb, sem, x1_tiles, LN_EPS / 4)
            with nc.Block() as block:
                @block.sync
                def _(sp):
                    def load(n, b):
                        if b in stored:
                            wait_reuse(sp, r_ready, stored_before(n - 1, b) + 1)
                            sp.dma_start(yt[b][:, :],
                                         zt_dram[bass.ds(n * S + b, 1), :, :].rearrange("a p n -> (a p) n"))\
                                .then_inc(y_load[b], 16)
                        load_quad(sp, xs, x_tiles, x_load, norm.u_ready, n, b)

                    run(sp, NC, (0, load))

                @block.gpsimd
                def _(pool):
                    def batch_norm(n, b):
                        if b in stored:
                            wait_apart(pool, y_load[b], (n + 1) * 16, y_passed)
                            wait_reuse_apart(pool, t_done, n * S + b - 5, y_passed)
                            pool.tensor_scalar(r[b % 6][:, :], yt[b][:, :], scale2[:, 0:1], shift2[:, 0:1],
                                               ALU.mult, ALU.add).then_inc(r_ready, 1)

                    run(pool, NC, (0, batch_norm), (8, lambda n, b: norm.store(pool, n, b)))
                    norm.stored(pool)

                @block.scalar
                def _(act):
                    def batch_norm_kept(n, b):
                        if b not in stored:
                            wait_reuse_apart(act, t_done, n * S + b - 5, k_passed)
                            act.activation(r[b % 6][:, :], kept_chunk(n, b), ACT.Identity, bias=shift2[:, 0:1],
                                           scale=scale2[:, 0:1]).then_inc(k_ready, 1)

                    run(act, NC, (0, batch_norm_kept), (3, lambda n, b: norm.root(act, n, b)),
                        (5, lambda n, b: norm.scale(act, n, b)), peeled=2)

                @block.tensor
                def _(pe):
                    def turn(n, b):
                        if b in stored:
                            pe.wait_ge(r_ready, stored_before(n, b) + 1)
                        else:
                            pe.wait_ge(k_ready, n * (S // KEEP) + b // KEEP + 1)
                        wait_reuse(pe, norm.u_ready, n * S + b - 3)
                        for j in range(TC):
                            mm = pe.transpose(p_r[b % 4][0:R, j * D:(j + 1) * D], r[b % 6][:, j * R:(j + 1) * R],
                                              ident[:, :])
                        mm.then_inc(t_done, 1)

                    run(pe, NC, (0, turn))

                @block.vector
                def _(dve):
                    def total(n, b):
                        dve.wait_ge(x_load[b // QD], (n + 1) * 32)
                        dve.wait_ge(t_done, n * S + b + 1)
                        wait_reuse(dve, norm.o_ready, (n - 1) * S + b + 1)
                        dve.scalar_tensor_tensor(
                            out=norm.u[b][:, :, :], in0=p_r[b % 4][0:R, :].rearrange("p (j d) -> p j d", d=D),
                            scalar=0.0, in1=xs[b // QD][:, b % QD, :, :],
                            op0=ALU.max, op1=ALU.add).then_inc(norm.u_ready, 1)

                    norm.dve_run(dve, (0, total))

        keep.close()

        with ExitStack() as ctx:
            sb, pb, sem = phase(ctx)
            xg = [sb(f"x1g{b}", [R, TC, D]) for b in range(ES)]
            idx = [sb(f"idx1_{b}", [R, TC], I32) for b in range(ES)]
            h2 = [sb(f"h2_in{h}", [P, CN]) for h in range(EP)]
            h2_hi = [sb(f"h2_rounded{h}", [P, CN], F32R) for h in range(EP)]
            h2_lo = [sb(f"h2_rest{h}", [P, CN], F32R) for h in range(EP)]
            xt = [sb(f"xt{b}", [P, CN]) for b in range(2)]
            wm_hi, wm_lo = sb("w_mlp2_rounded", [P, 2, 2, P], F32R), sb("w_mlp2_rest", [P, 2, 2, P], F32R)
            wq = [[sb(f"wq{b}{q}", [P, CN]) for q in range(2)] for b in range(2)]
            m = [[sb(f"m{b}{q}", [P, CN]) for q in range(2)] for b in range(2)]
            rv = [sb(f"rv{b}", [R, TC, MUL, 3]) for b in range(2)]
            gs = [sb(f"gs{b}", [R, TC, MUL, 3]) for b in range(2)]
            gr = [sb(f"gr{b}", [R, TC, MUL]) for b in range(2)]
            mo = [sb(f"mo1_{h}", [R, 2, TC, MW]) for h in range(EP)]
            p_xt, p_up = pb("p_xt"), pb("p_up")
            p_w = [pb(f"p_w{q}") for q in range(2)]
            p_o = [[pb(f"p_o{b}{q}") for q in range(2)] for b in range(2)]
            g_done = [sem(f"x1_gathered{b}") for b in range(ES)]
            i_ready, i_passed = sem("index1_ready"), sem("index1_wait_passed")
            h_load = [sem(f"h2_loaded{h}") for h in range(EP)]
            wh_ready, wl_ready = sem("weights1_rounded"), sem("weights1_rest_ready")
            hh_ready, hl_ready = sem("h2_rounded_ready"), sem("h2_rest_ready")
            t_done, t_copied = sem("x1_transposed"), sem("x1_transpose_copied")
            u_done, w_done = sem("up_product"), sem("path_weights_product")
            w_copied, m_ready, o_done = sem("path_weights_ready"), sem("paths_ready"), sem("out_product")
            c1, c2, c3 = sem("direction_products"), sem("direction_sums"), sem("messages1_ready")
            b_blank, m_dst = sem("messages1_blanked"), sem("destination1_written")
            m_store = [sem(f"messages1_stored{h}") for h in range(EP)]
            with nc.Block() as block:
                @block.gpsimd
                def _(pool):
                    for h in range(EP):
                        pool.memset(mo[h][:, :, :, :], 0.0).then_inc(b_blank, 1)

                    def gather(n, b):
                        wait_reuse(pool, t_done, (n - 1) * ES + b + 1)
                        wait_apart(pool, i_ready, n * ES + b + 1, i_passed)
                        for j in range(TC):
                            pool.indirect_dma_start(
                                out=xg[b][:, j, :], out_offset=None, in_=x1_dram,
                                in_offset=bass.IndirectOffsetOnAxis(ap=idx[b][:, j:j + 1], axis=0),
                                bounds_check=N - 1, oob_is_err=False).then_inc(g_done[b], 16)

                    run(pool, EC, (0, gather), ring=ES)

                @block.sync
                def _(sp):
                    def load(n, b):
                        if b % 2 == 0:
                            wait_reuse(sp, hl_ready, (n - 1) * EP + b // 2 + 1)
                            sp.dma_start(h2[b // 2][:, :],
                                         h2_dram[bass.ds(n * EP + b // 2, 1), :, :].rearrange("a p n -> (a p) n"))\
                                .then_inc(h_load[b // 2], 16)

                    def store(n, b):
                        if b % 2:
                            sp.wait_ge(c3, n * ES + b + 1)
                            sp.wait_ge(m_dst, n * ES + b + 1)
                            for lo, hi in split_rows():
                                sp.dma_start(msg_rows[lo:hi, bass.ds((n * ES + b - 1) * TC, 2 * TC), :],
                                             mo[b // 2][lo:hi, :, :, :].rearrange("p a j d -> p (a j) d"))\
                                    .then_inc(m_store[b // 2], 16)

                    run(sp, EC, (0, load), (AHEAD, store), ring=ES)
                    for h in range(EP):
                        sp.wait_ge(m_store[h], 32 * uses(EC // 2, h, EP))

                @block.tensor
                def _(pe):
                    def inputs(n, b):
                        pe.wait_ge(g_done[b], (n + 1) * (16 * TC))
                        wait_reuse(pe, t_copied, n * ES + b)
                        for j in range(TC):
                            mm = pe.transpose(p_xt[:, j * R:(j + 1) * R], xg[b][:, j, :], ident[0:R, 0:R])
                        mm.then_inc(t_done, 1)
                        pe.wait_ge(hl_ready, n * EP + b // 2 + 1)
                        wait_reuse(pe, w_copied, n * ES + b)
                        for q in range(2):
                            for k, (w, v) in enumerate(((wm_hi, h2_hi), (wm_hi, h2_lo), (wm_lo, h2_hi))):
                                mm = pe.matmul(p_w[q][:, 0:CN], w[:, b % 2, q, :], v[b // 2][:, :],
                                               start=(k == 0), stop=(k == 2))
                        mm.then_inc(w_done, 1)

                    def outputs(n, b):
                        pe.wait_ge(m_ready, n * ES + b + 1)
                        wait_reuse(pe, c3, n * ES + b - 1)
                        for q, w in ((0, w_outA), (1, w_outB)):
                            for j in range(TC):
                                mm = pe.matmul(p_o[b % 2][q][0:R, j * D:(j + 1) * D],
                                               m[b % 2][q][:, j * R:(j + 1) * R], w[:, :], start=True, stop=True)
                        mm.then_inc(o_done, 1)

                    def up(n, b):
                        pe.wait_ge(t_copied, n * ES + b + 1)
                        wait_reuse(pe, m_ready, n * ES + b)
                        pe.matmul(p_up[:, 0:CN], w_up[:, :], xt[b % 2][:, :], start=True, stop=True)\
                            .then_inc(u_done, 1)

                    pe.wait_ge(wl_ready, 1)
                    run(pe, EC, (0, inputs), (1, outputs), (0, up), ring=ES)

                @block.scalar
                def _(act):
                    def round_hidden(n, b):
                        if b % 2 == 0:
                            act.wait_ge(h_load[b // 2], (n + 1) * 16)
                            wait_reuse(act, w_done, (n - 1) * ES + b + 2)
                            act.activation(h2_hi[b // 2][:, :], h2[b // 2][:, :], ACT.Copy).then_inc(hh_ready, 1)

                    def copies(n, b):
                        act.wait_ge(t_done, n * ES + b + 1)
                        wait_reuse(act, u_done, n * ES + b - 1)
                        act.activation(xt[b % 2][:, :], p_xt[:, 0:CN], ACT.Copy).then_inc(t_copied, 1)
                        act.wait_ge(w_done, n * ES + b + 1)
                        wait_reuse(act, m_ready, n * ES + b - 1)
                        for q in range(2):
                            ins = act.activation(wq[b % 2][q][:, :], p_w[q][:, 0:CN], ACT.Identity,
                                                 bias=b_mlp2[:, q:q + 1])
                        ins.then_inc(w_copied, 1)

                    run(act, EC, (0, round_hidden), (1, copies), ring=ES, peeled=2)

                @block.vector
                def _(dve):
                    def combine(n, b):
                        full = [R, TC, MUL, 3]
                        c = b % 2
                        rh = rhat[:, bass.ds((n * ES + b) * TC, TC), :].unsqueeze(2).to_broadcast(full)
                        oA = p_o[c][0][0:R, :].rearrange("p (j d) -> p j d", d=D)
                        oB = p_o[c][1][0:R, :].rearrange("p (j d) -> p j d", d=D)
                        out_m = mo[b // 2][:, c, :, :]
                        dve.wait_ge(o_done, n * ES + b + 1)
                        wait_reuse(dve, c3, n * ES + b)
                        dve.tensor_tensor(rv[c][:, :, :, :], oB[:, :, 0:MUL].unsqueeze(3).to_broadcast(full), rh,
                                          ALU.mult)
                        dve.tensor_tensor(gs[c][:, :, :, :],
                                          oB[:, :, MUL:D].rearrange("p j (k c) -> p j k c", c=3), rh,
                                          ALU.mult).then_inc(c1, 1)
                        dve.wait_ge(c1, n * ES + b + 1)
                        dve.tensor_reduce(gr[c][:, :, :], gs[c][:, :, :, :], AX_X, ALU.add).then_inc(c2, 1)
                        wait_reuse(dve, m_store[b // 2], n * 32)
                        if isinstance(n, int) and n == 0:
                            dve.wait_ge(b_blank, EP)
                        dve.tensor_tensor(out_m[:, :, MUL:D].rearrange("p j (k c) -> p j k c", c=3),
                                          oA[:, :, MUL:D].rearrange("p j (k c) -> p j k c", c=3),
                                          rv[c][:, :, :, :], ALU.add)
                        dve.tensor_copy(out_m[:, :, D:D + 1],
                                        dst_f[:, bass.ds((n * ES + b) * TC, TC)].unsqueeze(2)).then_inc(m_dst, 1)
                        dve.wait_ge(c2, n * ES + b + 1)
                        dve.tensor_tensor(out_m[:, :, 0:MUL], oA[:, :, 0:MUL], gr[c][:, :, :], ALU.add)\
                            .then_inc(c3, 1)

                    def index(n, b):
                        wait_reuse(dve, g_done[b], n * (16 * TC))
                        dve.tensor_copy(idx[b][:, :], src_all[:, bass.ds((n * ES + b) * TC, TC)]).then_inc(i_ready, 1)

                    def rest_of_hidden(n, b):
                        if b % 2 == 0:
                            dve.wait_ge(hh_ready, n * EP + b // 2 + 1)
                            dve.tensor_tensor(h2_lo[b // 2][:, :], h2[b // 2][:, :], h2_hi[b // 2][:, :],
                                              ALU.subtract).then_inc(hl_ready, 1)

                    def products(n, b):
                        c = b % 2
                        dve.wait_ge(u_done, n * ES + b + 1)
                        dve.wait_ge(w_copied, n * ES + b + 1)
                        wait_reuse(dve, o_done, n * ES + b - 1)
                        for q in range(2):
                            ins = dve.tensor_tensor(m[c][q][:, :], p_up[:, 0:CN], wq[c][q][:, :], ALU.mult)
                        ins.then_inc(m_ready, 1)

                    dve.tensor_copy(wm_hi[:, :, :, :], w_mlp2[:, :, :, :]).then_inc(wh_ready, 1)
                    dve.wait_ge(wh_ready, 1)
                    dve.tensor_tensor(wm_lo[:, :, :, :], w_mlp2[:, :, :, :], wm_hi[:, :, :, :],
                                      ALU.subtract).then_inc(wl_ready, 1)
                    run(dve, EC, (0, index), (2, rest_of_hidden), (3, products), (4, combine), ring=ES,
                        peeled=2)

        slow_path(1)

        with ExitStack() as ctx:
            sb, pb, sem = phase(ctx)
            xs = [sb(f"x3s{h}", [R, QD, TC, D]) for h in range(QS)]
            ax = [sb(f"ax1_{h}", [R, QD, TC, D]) for h in range(QS)]
            win = [sb(f"win1_{b}", [WIN, TC, MW]) for b in range(S)]
            local = [sb(f"local1_{b}", [WIN, TC]) for b in range(S)]
            hot = [sb(f"hot1_{b}", [WIN, TC, R]) for b in range(S)]
            p_agg = [pb(f"p_agg1_{b}") for b in range(4)]
            x_load = [sem(f"x1_loaded{h}") for h in range(QS)]
            s_load = [sem(f"slow_sums1_loaded{h}") for h in range(QS)]
            w_load = [sem(f"windows1_loaded{b}") for b in range(S)]
            l_ready, l_passed = sem("local1_ready"), sem("local1_wait_passed")
            o_ready, d_ready = sem("pool_one_hot_ready"), sem("dve_one_hot_ready")
            a_done, x_passed = sem("messages1_added"), sem("x1_wait_passed")
            norm = Norm("norm1", sb, sem, out_tiles, LN_EPS)
            with nc.Block() as block:
                @block.sync
                def _(sp):
                    run(sp, NC, (0, lambda n, b: load_windows(sp, mybir.EngineType.SP, range(TC), win, w_load,
                                                              a_done, n, b)))

                @block.gpsimd
                def _(pool):
                    def one_hot(n, b):
                        pool.wait_ge(w_load[b], (n + 1) * (16 * TC))
                        wait_reuse(pool, o_ready, (n - 1) * S + b + 1)
                        pool.tensor_tensor(local[b][:, :].unsqueeze(2), win[b][:, :, D:D + 1],
                                           tile_base[0:WIN, bass.ds((n * S + b) * TC, TC)].unsqueeze(2),
                                           ALU.subtract).then_inc(l_ready, 1)
                        wait_reuse(pool, a_done, (n - 1) * S + b + 1)
                        wait_apart(pool, l_ready, n * S + b + 1, l_passed)
                        for j in range(POOL_HOT):
                            ins = pool.tensor_scalar(hot[b][:, j, :], node_iota[0:WIN, :], local[b][:, j:j + 1], None,
                                                     ALU.is_equal)
                        ins.then_inc(o_ready, 1)

                    def program(slow):
                        def load(n, b):
                            load_quad(pool, xs, x1_tiles, x_load, norm.u_ready, n, b, x_passed)
                            if slow:
                                load_quad(pool, ax, agg_tiles, s_load, norm.u_ready, n, b, x_passed)

                        run(pool, NC, (0, load), (AHEAD, one_hot), peeled=2)

                    either(pool, program)

                @block.tensor
                def _(pe):
                    def aggregate(n, b):
                        pe.wait_ge(o_ready, n * S + b + 1)
                        pe.wait_ge(d_ready, n * S + b + 1)
                        wait_reuse(pe, norm.u_ready, n * S + b - 3)
                        for j in range(TC):
                            mm = pe.matmul(p_agg[b % 4][0:R, j * D:(j + 1) * D], hot[b][:, j, :],
                                           win[b][:, j, 0:D], start=True, stop=True)
                        mm.then_inc(a_done, 1)

                    run(pe, NC, (0, aggregate))

                @block.vector
                def _(dve):
                    def program(slow):
                        def one_hot(n, b):
                            dve.wait_ge(l_ready, n * S + b + 1)
                            wait_reuse(dve, a_done, (n - 1) * S + b + 1)
                            shape = [WIN, TC - POOL_HOT, R]
                            dve.tensor_tensor(hot[b][:, POOL_HOT:TC, :],
                                              node_iota[0:WIN, :].unsqueeze(1).to_broadcast(shape),
                                              local[b][:, POOL_HOT:TC].unsqueeze(2).to_broadcast(shape), ALU.is_equal)\
                                .then_inc(d_ready, 1)

                        def total(n, b):
                            h = b // QD
                            dve.wait_ge(x_load[h], (n + 1) * 32)
                            dve.wait_ge(a_done, n * S + b + 1)
                            if slow:
                                dve.wait_ge(s_load[h], (n + 1) * 32)
                            wait_reuse(dve, norm.o_ready, (n - 1) * S + b + 1)
                            dve.tensor_tensor(norm.u[b][:, :, :], xs[h][:, b % QD, :, :],
                                              ax[h][:, b % QD, :, :] if slow
                                              else p_agg[b % 4][0:R, :].rearrange("p (j d) -> p j d", d=D), ALU.add)\
                                .then_inc(norm.u_ready, 1)

                        norm.dve_run(dve, (0, one_hot), (2, total))

                    either(dve, program)

                @block.scalar
                def _(act):
                    run(act, NC, (0, lambda n, b: norm.root(act, n, b)), (2, lambda n, b: norm.scale(act, n, b)),
                        (2, lambda n, b: norm.store(act, n, b)), peeled=2)
                    norm.stored(act)


_INS = ["x", "src", "dst", "edge_attr_128", "edge_attr_3", "edge_weight", "L0_gnn_eps", "L0_gnn_W1", "L0_gnn_g1",
        "L0_gnn_b1", "L0_gnn_W2", "L0_gnn_g2", "L0_gnn_b2", "L1_gnn_W_up0", "L1_gnn_W_up1", "L1_gnn_mlp_w0",
        "L1_gnn_mlp_b0", "L1_gnn_mlp_w1", "L1_gnn_mlp_b1", "L1_gnn_mlp_w2", "L1_gnn_mlp_b2", "L1_gnn_W_out0",
        "L1_gnn_W_out1"]


def kernel(**inputs):
    import numpy as _np
    import concourse.bacc as _bacc
    from concourse import mybir as _mybir
    from concourse.bass_utils import run_bass_kernel_spmd as _run

    nc = _bacc.Bacc("TRN2", target_bir_lowering=False, num_devices=1)
    arrays, args = {}, []
    for name in _INS:
        a = _np.ascontiguousarray(inputs[name])
        if a.ndim == 0:
            a = a.reshape(1)
        arrays[f"in_{name}_dram"] = a
        args.append(nc.dram_tensor(f"in_{name}_dram", a.shape, _mybir.dt.from_np(a.dtype), kind="ExternalInput").ap())
    shape = tuple(inputs["x"].shape)
    args.append(nc.dram_tensor("out_0_dram", shape, _mybir.dt.float32, kind="ExternalOutput").ap())
    gnn_kernel(nc, *args)
    r = _run(nc, [arrays], core_ids=[0])
    return r.results[0]["out_0_dram"]
```
